# Optimizing a Trainium2 kernel written in Bass

```python
import numpy as np
import jax
import jax.numpy as jnp

def _softmax(x, axis=-1):
    return jax.nn.softmax(x, axis=axis)

def _gelu(x):
    return jax.nn.gelu(x, approximate=True)

def _silu(x):
    return jax.nn.silu(x)

def _sigmoid(x):
    return jax.nn.sigmoid(x)

def _layernorm(x, axis=-1, eps=1e-05):
    m = jnp.mean(x, axis=axis, keepdims=True)
    v = jnp.var(x, axis=axis, keepdims=True)
    return (x - m) / jnp.sqrt(v + eps)

def _scatter_add(tgt, idx, src, axis=0):
    return tgt.at[idx].add(src)

def _segment_sum(src, seg, n):
    return jax.ops.segment_sum(src, seg, n)
kernel_name = 'mk_perceiver_d2_seqx_r4_5ff850'

def setup_inputs(seed: int=0):
    np.random.seed(seed)
    _w = jnp.asarray

    def _rec_inputs():
        import jax
        import jax.numpy as jnp
        _rk = jax.random.key(seed)
        x = 7.22e-05 + 1 * jax.random.normal(jax.random.fold_in(_rk, 1), (64, 32, 256), jnp.float32)
        _lenS = 32 - jax.random.randint(jax.random.fold_in(_rk, 7), (64,), 0, max(1, 32 // 4) + 1, jnp.int32)
        _lenS2 = 257 - jax.random.randint(jax.random.fold_in(_rk, 8), (64,), 0, max(1, 257 // 4) + 1, jnp.int32)
        _ctx_1024P = jax.random.normal(jax.random.fold_in(_rk, 11), (64, 16, 256), jnp.float32)
        _ctx_1024c = jax.random.dirichlet(jax.random.fold_in(_rk, 511), 0.3 * jnp.ones((16,), jnp.float32), (64, 257))
        _ctx_1024t = jnp.einsum('bsk,bkd->bsd', _ctx_1024c, _ctx_1024P)
        _ctx_1024t = _ctx_1024t * jax.lax.rsqrt(jnp.mean(jnp.square(_ctx_1024t)) + 1e-12) * 0.953939
        ctx_1024 = 4.13588e-05 + 0.999923 * (_ctx_1024t + 0.3 * jax.random.normal(jax.random.fold_in(_rk, 611), (64, 257, 256), jnp.float32))
        _validS = jnp.arange(32)[None, :] < _lenS[:, None]
        _validS2 = jnp.arange(257)[None, :] < _lenS2[:, None]
        _causal = jnp.tril(jnp.ones((32, 32), dtype=bool))
        mask_BxSxS2_ik1 = jnp.where(jnp.broadcast_to(_validS2[:, None, :], (64, 32, 257)), 1, 0).astype(jnp.int32)
        return (x, ctx_1024, mask_BxSxS2_ik1)
    x, ctx_1024, mask_BxSxS2_ik1 = _rec_inputs()

    def _L0_xattn_setup():
        import jax, jax.numpy as jnp
        import numpy as np
        N_HEADS = 16
        D_MODEL = 256
        HEAD_D = D_MODEL // N_HEADS
        key = jax.random.key(seed)
        ks = jax.random.split(key, 8)
        B, S, D = (4, 512, D_MODEL)
        scale = 1.0 / np.sqrt(D)
        return {'query': jax.random.normal(ks[0], (B, S, D), jnp.float32), 'key': jax.random.normal(ks[1], (B, S, D), jnp.float32), 'value': jax.random.normal(ks[2], (B, S, D), jnp.float32), 'mask': jax.random.randint(ks[3], (B, S, S), 0, 2, jnp.int32), 'wq': jax.random.normal(ks[4], (D, D), jnp.float32) * scale, 'wk': jax.random.normal(ks[5], (D, D), jnp.float32) * scale, 'wv': jax.random.normal(ks[6], (D, D), jnp.float32) * scale, 'w_out': jax.random.normal(ks[7], (D, D), jnp.float32) * scale}
    _L0_xattn_all = _L0_xattn_setup()
    _L0_xattn_in = {k: v for k, v in _L0_xattn_all.items() if k in ('wq', 'wk', 'wv', 'w_out')}
    del _L0_xattn_all

    def _L0_attn_setup():
        import jax, jax.numpy as jnp
        import numpy as np

        def log_g(x):
            return jnp.where(x >= 0, jnp.log(jax.nn.relu(x) + 0.5), -jax.nn.softplus(-x))

        def _reference_tuple_inner(x, W1, b1, W2, b2, init_h):
            B, S, _ = x.shape
            Din = init_h.shape[0]
            proj = x @ W1 + b1
            hidden, forget_gate, input_gate = jnp.split(proj, 3, axis=-1)
            diff = jax.nn.softplus(-forget_gate) - jax.nn.softplus(-input_gate)
            log_coeffs = -jax.nn.softplus(diff)
            log_val_coeffs = -jax.nn.softplus(-diff)
            log_values = log_val_coeffs + log_g(hidden)
            prev_log_hidden = jnp.broadcast_to(log_g(init_h), (B, 1, Din))
            log_values = jnp.concatenate([prev_log_hidden, log_values], axis=1)
            log_coeffs = jnp.pad(log_coeffs, ((0, 0), (1, 0), (0, 0)))
            a_star = jnp.cumsum(log_coeffs, axis=1)
            log_h = a_star + jax.lax.cumlogsumexp(log_values - a_star, axis=1)
            out_h = jnp.exp(log_h[:, -S:])
            next_hidden = out_h[:, -1:]
            next_log_hidden = log_h[:, -1:]
            out = out_h @ W2 + b2
            return (out, next_hidden, next_log_hidden)
        key = jax.random.key(seed)
        ks = jax.random.split(key, 6)
        B, S, D, Din = (4, 1024, 256, 512)
        x = jax.random.normal(ks[0], (B, S, D), jnp.float32)
        s1 = 1.0 / np.sqrt(D)
        W1 = jax.random.normal(ks[1], (D, 3 * Din), jnp.float32) * s1
        b1 = jax.random.normal(ks[2], (3 * Din,), jnp.float32) * s1
        b1 = b1.at[Din:2 * Din].add(1.0)
        s2 = 1.0 / np.sqrt(Din)
        W2 = jax.random.normal(ks[3], (Din, D), jnp.float32) * s2
        b2 = jax.random.normal(ks[4], (D,), jnp.float32) * s2
        init_h = jax.random.normal(ks[5], (Din,), jnp.float32)
        return {'x': x, 'W1': W1, 'b1': b1, 'W2': W2, 'b2': b2, 'init_h': init_h}
    _L0_attn_all = _L0_attn_setup()
    _L0_attn_in = {k: v for k, v in _L0_attn_all.items() if k in ('W1', 'b1', 'W2', 'b2', 'init_h')}
    del _L0_attn_all

    def _L0_ffn_setup():
        import jax, jax.numpy as jnp
        import numpy as np
        B, S, H = (2, 512, 256)
        F = 1024
        E = 8
        TOP_K = 2
        SHARED_SCALE = 0.1
        EPS = 1e-09

        def _moe_forward(x3, Wg, W1, b1, W2, b2, Ws1, bs1, Ws2, bs2):
            b, s, h = x3.shape
            x = x3.reshape(-1, h)
            T = x.shape[0]
            logits = x @ Wg
            probs = jax.nn.softmax(logits, axis=-1)
            vals, idx = jax.lax.top_k(probs, TOP_K)
            weights = vals / (jnp.sum(vals, axis=-1, keepdims=True) + EPS)
            cw = jnp.zeros((T, E), dtype=x.dtype).at[jnp.arange(T)[:, None], idx].set(weights)
            hpre = jnp.einsum('th,ehf->tef', x, W1) + b1
            act = jax.nn.silu(hpre)
            y = jnp.einsum('tef,efh->teh', act, W2) + b2
            out = jnp.einsum('te,teh->th', cw, y)
            shared = jax.nn.silu(x @ Ws1 + bs1) @ Ws2 + bs2
            out = out + SHARED_SCALE * shared
            return out.reshape(b, s, h)
        key = jax.random.key(seed)
        ks = jax.random.split(key, 10)
        sc = 0.02
        return {'hidden_states': jax.random.normal(ks[0], (B, S, H), dtype=jnp.float32), 'Wg': jax.random.normal(ks[1], (H, E), dtype=jnp.float32) * sc, 'W1': jax.random.normal(ks[2], (E, H, F), dtype=jnp.float32) * sc, 'b1': jnp.zeros((E, F), dtype=jnp.float32), 'W2': jax.random.normal(ks[3], (E, F, H), dtype=jnp.float32) * sc, 'b2': jnp.zeros((E, H), dtype=jnp.float32), 'Ws1': jax.random.normal(ks[4], (H, F), dtype=jnp.float32) * sc, 'bs1': jnp.zeros((F,), dtype=jnp.float32), 'Ws2': jax.random.normal(ks[5], (F, H), dtype=jnp.float32) * sc, 'bs2': jnp.zeros((H,), dtype=jnp.float32)}
    _L0_ffn_all = _L0_ffn_setup()
    _L0_ffn_in = {k: v for k, v in _L0_ffn_all.items() if k in ('Wg', 'W1', 'b1', 'W2', 'b2', 'Ws1', 'bs1', 'Ws2', 'bs2')}
    del _L0_ffn_all

    def _L1_xattn_setup():
        import jax, jax.numpy as jnp
        import numpy as np
        EMBED_DIM = 256
        B, S = (4, 512)
        SCALE = float(np.sqrt(EMBED_DIM))
        key = jax.random.key(seed)
        ks = jax.random.split(key, 9)
        d = EMBED_DIM
        init = 1.0 / np.sqrt(d)
        return {'query': jax.random.normal(ks[0], (B, S, d), jnp.float32), 'key': jax.random.normal(ks[1], (B, S, d), jnp.float32), 'value': jax.random.normal(ks[2], (B, S, d), jnp.float32), 'wq': jax.random.uniform(ks[3], (d, d), jnp.float32, -init, init), 'bq': jax.random.uniform(ks[4], (d,), jnp.float32, -init, init), 'wk': jax.random.uniform(ks[5], (d, d), jnp.float32, -init, init), 'bk': jax.random.uniform(ks[6], (d,), jnp.float32, -init, init), 'wv': jax.random.uniform(ks[7], (d, d), jnp.float32, -init, init), 'bv': jax.random.uniform(ks[8], (d,), jnp.float32, -init, init)}
    _L1_xattn_all = _L1_xattn_setup()
    _L1_xattn_in = {k: v for k, v in _L1_xattn_all.items() if k in ('wq', 'bq', 'wk', 'bk', 'wv', 'bv')}
    del _L1_xattn_all

    def _L1_attn_setup():
        import jax, jax.numpy as jnp
        import numpy as np
        key = jax.random.key(seed)
        ks = jax.random.split(key, 7)
        B, P, D = (4, 512, 256)
        s = 1.0 / np.sqrt(D)
        return {'x': jax.random.normal(ks[0], (B, P, D), dtype=jnp.float32), 'Wq': jax.random.normal(ks[1], (D, D), dtype=jnp.float32) * s, 'bq': jnp.zeros((D,), dtype=jnp.float32), 'Wk': jax.random.normal(ks[2], (D, D), dtype=jnp.float32) * s, 'bk': jnp.zeros((D,), dtype=jnp.float32), 'Wv': jax.random.normal(ks[3], (D, D), dtype=jnp.float32) * s, 'bv': jnp.zeros((D,), dtype=jnp.float32)}
    _L1_attn_all = _L1_attn_setup()
    _L1_attn_in = {k: v for k, v in _L1_attn_all.items() if k in ('Wq', 'bq', 'Wk', 'bk', 'Wv', 'bv')}
    del _L1_attn_all

    def _L1_ffn_setup():
        import jax, jax.numpy as jnp
        import numpy as np
        B, S, H = (1, 512, 256)
        E = 16
        I = 192
        TOPK = 4
        G = 4
        TOPK_G = 2
        SCALE = 2.5
        N_SHARED = 1

        def _route(x, gate_w, gate_bias):
            n = x.shape[0]
            logits = jnp.einsum('nh,eh->ne', x.astype(jnp.float32), gate_w)
            scores = jax.nn.sigmoid(logits)
            sb = scores + gate_bias
            gs = sb.reshape(n, G, E // G)
            group_scores = jnp.sum(jax.lax.top_k(gs, 2)[0], axis=-1)
            _, gidx = jax.lax.top_k(group_scores, TOPK_G)
            gmask = jnp.sum(jax.nn.one_hot(gidx, G, dtype=sb.dtype), axis=1)
            emask = jnp.repeat(gmask, E // G, axis=-1)
            masked = jnp.where(emask > 0, sb, -jnp.inf)
            _, tidx = jax.lax.top_k(masked, TOPK)
            w = jnp.take_along_axis(scores, tidx, axis=1)
            w = w / (jnp.sum(w, axis=-1, keepdims=True) + 1e-20)
            return (tidx, w * SCALE)
        key = jax.random.key(seed)
        ks = jax.random.split(key, 9)

        def rn(k, shape, scale=0.02):
            return jax.random.normal(k, shape, dtype=jnp.float32) * scale
        return dict(hidden_states=jax.random.normal(ks[0], (B, S, H), dtype=jnp.float32), gate_w=rn(ks[1], (E, H)), gate_bias=jax.random.normal(ks[2], (E,), dtype=jnp.float32) * 0.1, w1=rn(ks[3], (E, I, H)), w2=rn(ks[4], (E, H, I)), w3=rn(ks[5], (E, I, H)), ws1=rn(ks[6], (I * N_SHARED, H)), ws2=rn(ks[7], (H, I * N_SHARED)), ws3=rn(ks[8], (I * N_SHARED, H)))
    _L1_ffn_all = _L1_ffn_setup()
    _L1_ffn_in = {k: v for k, v in _L1_ffn_all.items() if k in ('gate_w', 'gate_bias', 'w1', 'w2', 'w3', 'ws1', 'ws2', 'ws3')}
    del _L1_ffn_all
    return {'x': x, 'ctx_1024': ctx_1024, 'mask_BxSxS2_ik1': mask_BxSxS2_ik1, 'L0_xattn_wq': _L0_xattn_in['wq'], 'L0_xattn_wk': _L0_xattn_in['wk'], 'L0_xattn_wv': _L0_xattn_in['wv'], 'L0_xattn_w_out': _L0_xattn_in['w_out'], 'L0_attn_W1': _L0_attn_in['W1'], 'L0_attn_b1': _L0_attn_in['b1'], 'L0_attn_W2': _L0_attn_in['W2'], 'L0_attn_b2': _L0_attn_in['b2'], 'L0_attn_init_h': _L0_attn_in['init_h'], 'L0_ffn_Wg': _L0_ffn_in['Wg'], 'L0_ffn_W1': _L0_ffn_in['W1'], 'L0_ffn_b1': _L0_ffn_in['b1'], 'L0_ffn_W2': _L0_ffn_in['W2'], 'L0_ffn_b2': _L0_ffn_in['b2'], 'L0_ffn_Ws1': _L0_ffn_in['Ws1'], 'L0_ffn_bs1': _L0_ffn_in['bs1'], 'L0_ffn_Ws2': _L0_ffn_in['Ws2'], 'L0_ffn_bs2': _L0_ffn_in['bs2'], 'L1_xattn_wq': _L1_xattn_in['wq'], 'L1_xattn_bq': _L1_xattn_in['bq'], 'L1_xattn_wk': _L1_xattn_in['wk'], 'L1_xattn_bk': _L1_xattn_in['bk'], 'L1_xattn_wv': _L1_xattn_in['wv'], 'L1_xattn_bv': _L1_xattn_in['bv'], 'L1_attn_Wq': _L1_attn_in['Wq'], 'L1_attn_bq': _L1_attn_in['bq'], 'L1_attn_Wk': _L1_attn_in['Wk'], 'L1_attn_bk': _L1_attn_in['bk'], 'L1_attn_Wv': _L1_attn_in['Wv'], 'L1_attn_bv': _L1_attn_in['bv'], 'L1_ffn_gate_w': _L1_ffn_in['gate_w'], 'L1_ffn_gate_bias': _L1_ffn_in['gate_bias'], 'L1_ffn_w1': _L1_ffn_in['w1'], 'L1_ffn_w2': _L1_ffn_in['w2'], 'L1_ffn_w3': _L1_ffn_in['w3'], 'L1_ffn_ws1': _L1_ffn_in['ws1'], 'L1_ffn_ws2': _L1_ffn_in['ws2'], 'L1_ffn_ws3': _L1_ffn_in['ws3']}

def reference(x, ctx_1024, mask_BxSxS2_ik1, L0_xattn_wq, L0_xattn_wk, L0_xattn_wv, L0_xattn_w_out, L0_attn_W1, L0_attn_b1, L0_attn_W2, L0_attn_b2, L0_attn_init_h, L0_ffn_Wg, L0_ffn_W1, L0_ffn_b1, L0_ffn_W2, L0_ffn_b2, L0_ffn_Ws1, L0_ffn_bs1, L0_ffn_Ws2, L0_ffn_bs2, L1_xattn_wq, L1_xattn_bq, L1_xattn_wk, L1_xattn_bk, L1_xattn_wv, L1_xattn_bv, L1_attn_Wq, L1_attn_bq, L1_attn_Wk, L1_attn_bk, L1_attn_Wv, L1_attn_bv, L1_ffn_gate_w, L1_ffn_gate_bias, L1_ffn_w1, L1_ffn_w2, L1_ffn_w3, L1_ffn_ws1, L1_ffn_ws2, L1_ffn_ws3):
    import jax
    import jax.numpy as jnp

    def _L0_xattn_ref(query, key, value, mask, wq, wk, wv, w_out):
        import jax, jax.numpy as jnp
        import numpy as np
        N_HEADS = 16
        D_MODEL = 256
        HEAD_D = D_MODEL // N_HEADS
        B, Sq, D = query.shape
        H, hd = (N_HEADS, HEAD_D)

        def split(x):
            return x.reshape(B, -1, H, hd).transpose(0, 2, 1, 3)
        Q = split(jnp.einsum('bsd,ed->bse', query, wq))
        K = split(jnp.einsum('bsd,ed->bse', key, wk))
        V = split(jnp.einsum('bsd,ed->bse', value, wv))
        scores = jnp.einsum('bhqd,bhkd->bhqk', Q, K) / np.sqrt(hd)
        scores = jnp.where(mask[:, None, :, :] == 1, jnp.float32(-1000000000.0), scores)
        attn = jax.nn.softmax(scores, axis=-1)
        out = jnp.einsum('bhqk,bhkd->bhqd', attn, V)
        out = out.transpose(0, 2, 1, 3).reshape(B, Sq, D)
        return jnp.einsum('bsd,ed->bse', out, w_out)

    def _L0_attn_ref(x, W1, b1, W2, b2, init_h):
        import jax, jax.numpy as jnp
        import numpy as np

        def log_g(x):
            return jnp.where(x >= 0, jnp.log(jax.nn.relu(x) + 0.5), -jax.nn.softplus(-x))

        def _reference_tuple_inner(x, W1, b1, W2, b2, init_h):
            B, S, _ = x.shape
            Din = init_h.shape[0]
            proj = x @ W1 + b1
            hidden, forget_gate, input_gate = jnp.split(proj, 3, axis=-1)
            diff = jax.nn.softplus(-forget_gate) - jax.nn.softplus(-input_gate)
            log_coeffs = -jax.nn.softplus(diff)
            log_val_coeffs = -jax.nn.softplus(-diff)
            log_values = log_val_coeffs + log_g(hidden)
            prev_log_hidden = jnp.broadcast_to(log_g(init_h), (B, 1, Din))
            log_values = jnp.concatenate([prev_log_hidden, log_values], axis=1)
            log_coeffs = jnp.pad(log_coeffs, ((0, 0), (1, 0), (0, 0)))
            a_star = jnp.cumsum(log_coeffs, axis=1)
            log_h = a_star + jax.lax.cumlogsumexp(log_values - a_star, axis=1)
            out_h = jnp.exp(log_h[:, -S:])
            next_hidden = out_h[:, -1:]
            next_log_hidden = log_h[:, -1:]
            out = out_h @ W2 + b2
            return (out, next_hidden, next_log_hidden)
        return _reference_tuple_inner(x, W1, b1, W2, b2, init_h)[0]

    def _L0_ffn_ref(hidden_states, Wg, W1, b1, W2, b2, Ws1, bs1, Ws2, bs2):
        import jax, jax.numpy as jnp
        import numpy as np
        B, S, H = (2, 512, 256)
        F = 1024
        E = 8
        TOP_K = 2
        SHARED_SCALE = 0.1
        EPS = 1e-09

        def _moe_forward(x3, Wg, W1, b1, W2, b2, Ws1, bs1, Ws2, bs2):
            b, s, h = x3.shape
            x = x3.reshape(-1, h)
            T = x.shape[0]
            logits = x @ Wg
            probs = jax.nn.softmax(logits, axis=-1)
            vals, idx = jax.lax.top_k(probs, TOP_K)
            weights = vals / (jnp.sum(vals, axis=-1, keepdims=True) + EPS)
            cw = jnp.zeros((T, E), dtype=x.dtype).at[jnp.arange(T)[:, None], idx].set(weights)
            hpre = jnp.einsum('th,ehf->tef', x, W1) + b1
            act = jax.nn.silu(hpre)
            y = jnp.einsum('tef,efh->teh', act, W2) + b2
            out = jnp.einsum('te,teh->th', cw, y)
            shared = jax.nn.silu(x @ Ws1 + bs1) @ Ws2 + bs2
            out = out + SHARED_SCALE * shared
            return out.reshape(b, s, h)
        return _moe_forward(hidden_states, Wg, W1, b1, W2, b2, Ws1, bs1, Ws2, bs2)

    def _L1_xattn_ref(query, key, value, wq, bq, wk, bk, wv, bv):
        import jax, jax.numpy as jnp
        import numpy as np
        EMBED_DIM = 256
        B, S = (4, 512)
        SCALE = float(np.sqrt(EMBED_DIM))
        q = query @ wq + bq
        k = key @ wk + bk
        v = value @ wv + bv
        scores = jnp.einsum('bqd,bkd->bqk', q, k) / SCALE
        attn = jax.nn.softmax(scores, axis=-1)
        return jnp.einsum('bqk,bkd->bqd', attn, v)

    def _L1_attn_ref(x, Wq, bq, Wk, bk, Wv, bv):
        import jax, jax.numpy as jnp
        import numpy as np
        b, p, d = x.shape
        q = jnp.einsum('bpd,ed->bpe', x, Wq) + bq
        k = jnp.einsum('bpd,ed->bpe', x, Wk) + bk
        v = jnp.einsum('bpd,ed->bpe', x, Wv) + bv
        attn = jnp.einsum('bqd,bkd->bqk', q, k)
        causal = jnp.triu(jnp.ones((p, p), dtype=bool), k=1)
        attn = jnp.where(causal, -jnp.inf, attn)
        attn = attn / jnp.sqrt(jnp.asarray(d, dtype=attn.dtype))
        scores = jax.nn.softmax(attn, axis=-1)
        return jnp.einsum('bqk,bkd->bqd', scores, v)

    def _L1_ffn_ref(hidden_states, gate_w, gate_bias, w1, w2, w3, ws1, ws2, ws3):
        import jax, jax.numpy as jnp
        import numpy as np
        B, S, H = (1, 512, 256)
        E = 16
        I = 192
        TOPK = 4
        G = 4
        TOPK_G = 2
        SCALE = 2.5
        N_SHARED = 1

        def _route(x, gate_w, gate_bias):
            n = x.shape[0]
            logits = jnp.einsum('nh,eh->ne', x.astype(jnp.float32), gate_w)
            scores = jax.nn.sigmoid(logits)
            sb = scores + gate_bias
            gs = sb.reshape(n, G, E // G)
            group_scores = jnp.sum(jax.lax.top_k(gs, 2)[0], axis=-1)
            _, gidx = jax.lax.top_k(group_scores, TOPK_G)
            gmask = jnp.sum(jax.nn.one_hot(gidx, G, dtype=sb.dtype), axis=1)
            emask = jnp.repeat(gmask, E // G, axis=-1)
            masked = jnp.where(emask > 0, sb, -jnp.inf)
            _, tidx = jax.lax.top_k(masked, TOPK)
            w = jnp.take_along_axis(scores, tidx, axis=1)
            w = w / (jnp.sum(w, axis=-1, keepdims=True) + 1e-20)
            return (tidx, w * SCALE)
        b, s, h = hidden_states.shape
        x = hidden_states.reshape(-1, h)
        tidx, tw = _route(x, gate_w, gate_bias)
        n = x.shape[0]
        combine = jnp.zeros((n, E), x.dtype).at[jnp.arange(n)[:, None], tidx].add(tw)
        g = jnp.einsum('nh,eih->nei', x, w1)
        u = jnp.einsum('nh,eih->nei', x, w3)
        hact = jax.nn.silu(g) * u * combine[:, :, None]
        y = jnp.einsum('nei,ehi->nh', hact, w2)
        shared = jnp.einsum('ni,hi->nh', jax.nn.silu(x @ ws1.T) * (x @ ws3.T), ws2)
        return (y + shared).reshape(b, s, h)
    x = x + _L0_xattn_ref(_layernorm(x, axis=-1), ctx_1024, ctx_1024, mask_BxSxS2_ik1, L0_xattn_wq, L0_xattn_wk, L0_xattn_wv, L0_xattn_w_out)
    x = x + _L0_attn_ref(_layernorm(x, axis=-1), L0_attn_W1, L0_attn_b1, L0_attn_W2, L0_attn_b2, L0_attn_init_h)
    x = x + _L0_ffn_ref(_layernorm(x, axis=-1), L0_ffn_Wg, L0_ffn_W1, L0_ffn_b1, L0_ffn_W2, L0_ffn_b2, L0_ffn_Ws1, L0_ffn_bs1, L0_ffn_Ws2, L0_ffn_bs2)
    x = x + _L1_xattn_ref(_layernorm(x, axis=-1), ctx_1024, ctx_1024, L1_xattn_wq, L1_xattn_bq, L1_xattn_wk, L1_xattn_bk, L1_xattn_wv, L1_xattn_bv)
    x = x + _L1_attn_ref(_layernorm(x, axis=-1), L1_attn_Wq, L1_attn_bq, L1_attn_Wk, L1_attn_bk, L1_attn_Wv, L1_attn_bv)
    x = x + _L1_ffn_ref(_layernorm(x, axis=-1), L1_ffn_gate_w, L1_ffn_gate_bias, L1_ffn_w1, L1_ffn_w2, L1_ffn_w3, L1_ffn_ws1, L1_ffn_ws2, L1_ffn_ws3)
    return x

_drawn_inputs = setup_inputs


def setup_inputs(seed=0):
    import zlib

    import numpy as np

    out = dict(_drawn_inputs(seed))
    spreads = {'L0_ffn_b1': (0.0, 0.489),
     'L0_ffn_b2': (0.0, 0.1),
     'L0_ffn_bs1': (0.0, 0.8),
     'L0_ffn_bs2': (0.0, 0.8),
     'L1_attn_bq': (0.0, 0.732),
     'L1_attn_bk': (0.0, 0.8),
     'L1_attn_bv': (0.0, 0.1)}
    factors = {'L0_ffn_Ws1': 8.0,
     'L0_ffn_Ws2': 7.45,
     'L1_xattn_bq': 8.0,
     'L1_xattn_bk': 8.0,
     'L1_ffn_gate_w': 6.679,
     'L1_ffn_gate_bias': 5.922,
     'L1_ffn_w1': 5.035,
     'L1_ffn_w2': 4.776,
     'L1_ffn_w3': 4.851,
     'L1_ffn_ws1': 6.596,
     'L1_ffn_ws2': 6.717,
     'L1_ffn_ws3': 6.676}
    for name, (base, spread) in spreads.items():
        noise = np.random.default_rng([zlib.crc32(name.encode()), seed]).standard_normal(out[name].shape)
        drawn = base * np.exp(spread * noise) if base else spread * noise
        out[name] = jnp.asarray(drawn.astype(out[name].dtype))
    for name, factor in factors.items():
        out[name] = (out[name] * factor).astype(out[name].dtype)
    return out
```

```python
from contextlib import ExitStack

import numpy as np

import concourse.bass as bass
from concourse import mybir

F32 = mybir.dt.float32
BF16 = mybir.dt.bfloat16
I32 = mybir.dt.int32
U32 = mybir.dt.uint32
ALU = mybir.AluOpType
ACT = mybir.ActivationFunctionType
AX = mybir.AxisListType

P = 128
B, S, D = 64, 32, 256
SK = 257
T = B * S
C = D // P
G = 4
TG = T // G
NT = T // P
H, HD = 16, 16
HC = P // HD
DIN = 512
J = DIN // P
E0, F0, K0 = 8, 1024, 2
E1, I1, K1 = 16, 192, 4
IH = I1 // 2
EPS = 1e-5
MASKED = -1e30
TINY = 1e-37

STAGES = range(6)


class Count:

    def __init__(self, sem, credit=0, unit=1):
        self.sem, self.credit, self.unit, self.base = sem, credit, unit, 0

    def at(self, n):
        return (n + self.credit + self.base) * self.unit

    def next(self):
        self.base += 1
        return self.at(0)


class Core:

    def __init__(self, nc, ctx, dram):
        self.nc, self.ctx, self.dram = nc, ctx, dram
        self.counts = []

    def sb(self, name, shape, dt=F32, ctx=None):
        if ctx is not None:
            name = f"{self.stage}_{name}"
        return (ctx or self.ctx).enter_context(self.nc.sbuf_tensor(name, shape, dt))

    def count(self, name, credit=0, unit=1):
        self.counts.append(Count(self.ctx.enter_context(self.nc.semaphore(name)), credit, unit))
        return self.counts[-1]


def group(g):
    return bass.ds(g * TG, TG)


CONST = {"ident": (P, P), "head_block": (P, HC * S), "repeat": (P, P), "causal": (P, P),
         "iota": (P, E1), "earlier": (P, 16), "expert_last": (P, 1)}


def const_table():
    p = np.arange(P)[:, None]
    c = np.arange(P)[None, :]
    parts = {
        "ident": (p == c),
        "head_block": (p // HD == np.arange(HC * S)[None, :] // S),
        "repeat": (p == c % S),
        "causal": np.where((p // S == c // S) & (c <= p), 0.0, MASKED),
        "iota": np.broadcast_to(np.arange(E1)[None, :], (P, E1)),
        "earlier": np.broadcast_to((np.arange(16)[None, :] % 4) < (np.arange(16)[None, :] // 4), (P, 16)),
        "expert_last": np.ones((P, 1)),
    }
    return np.concatenate([np.asarray(parts[k], np.float32) for k in CONST], axis=1)


def load_all(k):
    nc, d = k.nc, k.dram
    with nc.Block() as block:
        @block.sync
        def _(sp):
            sp.dma_start(k.x_t[:, :, :], d["x_t"].rearrange("(c p) t -> p c t", p=P)).then_inc(k.x_loaded.sem, 16)
            sp.dma_start(k.consts[:, :], d["consts"]).then_inc(k.x_loaded.sem, 16)
            for name, rows in k.weights.items():
                sp.dma_start(k.w[name][:, :, :], d[name].rearrange("(c p) n -> p c n", p=rows)).then_inc(k.weights_loaded.sem, 16)

        @block.gpsimd
        def _(pool):
            for s in k.counts:
                if s.credit:
                    pool.sem_inc(s.sem, s.credit * s.unit)

        @block.vector
        def _(dve):
            dve.memset(k.ones_mean[:, :], 1.0 / D)
            dve.memset(k.ones_row[:, :], 1.0)
            dve.memset(k.eps[:, :], EPS)
            dve.wait_ge(k.x_loaded.sem, k.x_loaded.at(2))
            dve.tensor_copy(k.ident_bf[:, :], k.c["ident"])
            dve.tensor_copy(k.repeat_bf[:, :], k.c["repeat"][0:S, :])
            dve.tensor_copy(k.causal_bf[:, :], k.c["causal"])
            dve.wait_ge(k.weights_loaded.sem, k.weights_loaded.at(len(k.weights)))


def layernorm(k):
    nc = k.nc
    ps = k.ps
    with nc.Block() as block:
        @block.tensor
        def _(pe):
            for g in range(G):
                for c in range(C):
                    last = pe.matmul(ps[:, g, :], k.ones_mean[:, :], k.x_t[:, c, group(g)], start=(c == 0), stop=(c == C - 1))
                last.then_inc(k.mean_ready.sem, 1)
            for g in range(G):
                pe.wait_ge(k.squared.sem, k.squared.at(g + 1))
                for c in range(C):
                    last = pe.matmul(ps[:, G + g, :], k.ones_mean[:, :], k.big[:, c, group(g)], start=(c == 0), stop=(c == C - 1))
                last.then_inc(k.var_ready.sem, 1)

        @block.scalar
        def _(act):
            for g in range(G):
                act.wait_ge(k.centred.sem, k.centred.at(C * (g + 1)))
                act.activation(k.big[:, 0:C, group(g)], k.n_t[:, :, group(g)], ACT.Square).then_inc(k.squared.sem, 1)
            for g in range(G):
                act.wait_ge(k.var_ready.sem, k.var_ready.at(g + 1))
                act.activation(k.big[:, 2, group(g)], ps[:, G + g, :], ACT.Sqrt, bias=k.eps[:, 0:1]).then_inc(k.std_ready.sem, 1)

        @block.vector
        def _(dve):
            for g in range(G):
                dve.wait_ge(k.mean_ready.sem, k.mean_ready.at(g + 1))
                for c in range(C):
                    dve.tensor_tensor(k.n_t[:, c, group(g)], k.x_t[:, c, group(g)], ps[:, g, :], ALU.subtract).then_inc(k.centred.sem, 1)
            for g in range(G):
                dve.wait_ge(k.std_ready.sem, k.std_ready.at(g + 1))
                dve.reciprocal(k.big[:, 3, group(g)], k.big[:, 2, group(g)]).then_inc(k.inv_ready.sem, 1)
                dve.wait_ge(k.inv_ready.sem, k.inv_ready.at(g + 1))
                dve.wait_ge(k.squared.sem, k.squared.at(g + 1))
                for c in range(C):
                    dve.tensor_tensor(k.n_t[:, c, group(g)], k.n_t[:, c, group(g)], k.big[:, 3, group(g)], ALU.mult)
    for s, n in ((k.mean_ready, G), (k.squared, G), (k.var_ready, G), (k.std_ready, G), (k.inv_ready, G), (k.centred, C * G)):
        s.base += n


def project(k, weight, src, finish_block, n_in=C, n_out=C, rows=P):
    nc, ps = k.nc, k.ps
    with nc.Block() as block:
        @block.tensor
        def _(pe):
            for g in range(G):
                for m in range(n_out):
                    for c in range(n_in):
                        last = pe.matmul(ps[:, g * n_out + m, :], weight[:, c, m * P:(m + 1) * P], src[:, c, group(g)],
                                         start=(c == 0), stop=(c == n_in - 1))
                    last.then_inc(k.projected.sem, 1)
        finish_block(block)
    k.projected.base += G * n_out


def stage_heads_attention(k):
    nc, ps, c_ = k.nc, k.ps, k.c
    layernorm(k)

    def take_q(block):
        @block.scalar
        def _(act):
            for g in range(G):
                for m in range(C):
                    act.wait_ge(k.projected.sem, k.projected.at(g * C + m + 1))
                    act.activation(k.q_t[:, m, group(g)], ps[:, g * C + m, :], ACT.Copy, scale=HD ** -0.5)
    project(k, k.w["L0_xattn_wq_t"], k.n_t, take_q)

    with ExitStack() as ctx:
        ctx_t = [k.sb(f"ctx_t{p}", [P, C, SK], ctx=ctx) for p in range(2)]
        mask_i = [k.sb(f"mask_i{p}", [S, SK], I32, ctx=ctx) for p in range(2)]
        mask_b = [k.sb(f"mask_b{p}", [S, SK], BF16, ctx=ctx) for p in range(2)]
        k_t = [k.sb(f"k_t{p}", [P, C, SK], ctx=ctx) for p in range(2)]
        v = [k.sb(f"v{p}", [P, 2, D], ctx=ctx) for p in range(2)]
        v_last = [k.sb(f"v_last{p}", [1, D], ctx=ctx) for p in range(2)]
        q_blk = [k.sb(f"q_blk{p}", [P, C, HC * S], ctx=ctx) for p in range(2)]
        neg_max = k.sb("neg_max", [P, 2, 4], ctx=ctx)
        sums = k.sb("sums", [P, 2, 4], ctx=ctx)
        inv = k.sb("inv", [P, 2, 4], ctx=ctx)
        probs = [k.sb(f"probs{p}", [P, 4, SK], ctx=ctx) for p in range(2)]
        pn = k.sb("pn", [P, 4, SK], ctx=ctx)
        p_t = k.sb("p_t", [P, 2, 512], ctx=ctx)
        p_last = k.sb("p_last", [1, 512], ctx=ctx)
        o_own = k.sb("o_own", [P, C, HC, S], ctx=ctx)
        KB, VB, OB, SB = 0, 2, 3, 4
        wk, wv = k.w["L0_xattn_wk_t"], k.w["L0_xattn_wv_t"]

        with nc.Block() as block:
            @block.sync
            def _(sp):
                def fetch(i, p):
                    b = 2 * i + p
                    sp.wait_ge(k.a_keys_done.sem, k.a_keys_done.at(b - 1))
                    sp.dma_start(ctx_t[p][:, :, :], k.dram["ctx_t"][bass.ds(b, 1), :, :].rearrange("o (c p) n -> p (o c) n", p=P)).then_inc(k.a_ctx[p].sem, 16)
                    sp.wait_ge(k.a_maskb.sem, k.a_maskb.at(b - 1))
                    sp.dma_start(mask_i[p][:, :], k.dram["mask"][bass.ds(b, 1), :, :].rearrange("o s n -> (o s) n")).then_inc(k.a_mask[p].sem, 16)
                with sp.Fori(0, B // 2) as i:
                    fetch(i, 0)
                    fetch(i, 1)

            @block.tensor
            def _(pe):
                def keys_values(i, p):
                    b = 2 * i + p
                    pe.wait_ge(k.a_ctx[p].sem, k.a_ctx[p].at(i + 1))
                    pe.wait_ge(k.a_kcopied.sem, k.a_kcopied.at(2 * b))
                    for m in range(C):
                        for c in range(C):
                            pe.matmul(ps[0:1, KB + m, 384:512], ctx_t[p][:, c, 256:257], wv[:, c, m * P:(m + 1) * P], start=(c == 0), stop=(c == C - 1))
                        for c in range(C):
                            last = pe.matmul(ps[:, KB + m, 0:SK], wk[:, c, m * P:(m + 1) * P], ctx_t[p][:, c, :], start=(c == 0), stop=(c == C - 1))
                        last.then_inc(k.a_kproj.sem, 1)
                    pe.wait_ge(k.a_vcopied.sem, k.a_vcopied.at(b))
                    for r in range(2):
                        for c in range(C):
                            last = pe.matmul(ps[:, VB, r * D:(r + 1) * D], ctx_t[p][:, c, r * P:(r + 1) * P], wv[:, c, :], start=(c == 0), stop=(c == C - 1))
                    last.then_inc(k.a_keys_done.sem, 1)

                def scores(i, p):
                    b = 2 * i + p
                    pe.wait_ge(k.a_kcopied.sem, k.a_kcopied.at(2 * b + 2))
                    pe.wait_ge(k.a_qblk.sem, k.a_qblk.at(b + 1))
                    pe.wait_ge(k.a_maskb.sem, k.a_maskb.at(b + 1))
                    pe.wait_ge(k.a_ptcopied.sem, k.a_ptcopied.at(3 * b))
                    for j in range(4):
                        pe.matmul(ps[:, SB + j, 0:SK], k.repeat_bf[:, :], mask_b[p][:, :], start=True, stop=False)
                        last = pe.matmul(ps[:, SB + j, 0:SK], q_blk[p][:, j // 2, (j % 2) * P:(j % 2 + 1) * P], k_t[p][:, j // 2, :], start=False, stop=True)
                    last.then_inc(k.a_scored.sem, 1)

                def weigh(i, p):
                    b = 2 * i + p
                    pe.wait_ge(k.a_normed.sem, k.a_normed.at(4 * (b + 1)))
                    for r in range(2):
                        for j in range(4):
                            last = pe.transpose(ps[:, SB + r, j * P:(j + 1) * P], pn[:, j, r * P:(r + 1) * P], c_["ident"])
                        last.then_inc(k.a_pt.sem, 1)
                    for j in range(4):
                        last = pe.transpose(ps[0:1, SB + 2, j * P:(j + 1) * P], pn[:, j, 256:257], c_["ident"])
                    last.then_inc(k.a_pt.sem, 1)
                    pe.wait_ge(k.a_own.sem, k.a_own.at(b))
                    pe.wait_ge(k.a_vcopied.sem, k.a_vcopied.at(b + 1))
                    for m in range(C):
                        for r in range(2):
                            pe.wait_ge(k.a_ptcopied.sem, k.a_ptcopied.at(3 * b + r + 1))
                            pe.matmul(ps[:, OB, m * D:(m + 1) * D], v[p][:, r, m * P:(m + 1) * P], p_t[:, r, m * D:(m + 1) * D], start=(r == 0), stop=False)
                        pe.wait_ge(k.a_ptcopied.sem, k.a_ptcopied.at(3 * b + 3))
                        last = pe.matmul(ps[:, OB, m * D:(m + 1) * D], v_last[p][0:1, m * P:(m + 1) * P], p_last[0:1, m * D:(m + 1) * D], start=False, stop=True)
                    last.then_inc(k.a_out.sem, 1)

                keys_values(0, 0)
                with pe.Fori(0, B // 2 - 1) as i:
                    scores(i, 0)
                    keys_values(i, 1)
                    weigh(i, 0)
                    scores(i, 1)
                    keys_values(i + 1, 0)
                    weigh(i, 1)
                i = B // 2 - 1
                scores(i, 0)
                keys_values(i, 1)
                weigh(i, 0)
                scores(i, 1)
                weigh(i, 1)

            @block.scalar
            def _(act):
                def take_keys(i, p):
                    b = 2 * i + p
                    for m in range(C):
                        act.wait_ge(k.a_kproj.sem, k.a_kproj.at(2 * b + m + 1))
                        act.wait_ge(k.a_scored.sem, k.a_scored.at(b - 1))
                        act.wait_ge(k.a_vcopied.sem, k.a_vcopied.at(b))
                        act.activation(v_last[p][0:1, m * P:(m + 1) * P], ps[0:1, KB + m, 384:512], ACT.Copy)
                        act.activation(k_t[p][:, m, :], ps[:, KB + m, 0:SK], ACT.Copy).then_inc(k.a_kcopied.sem, 1)

                def softmax(i, p):
                    b = 2 * i + p
                    act.wait_ge(k.a_max.sem, k.a_max.at(b + 1))
                    act.wait_ge(k.a_normed.sem, k.a_normed.at(4 * (b - 1)))
                    for j in range(4):
                        act.activation(probs[p][:, j, :], ps[:, SB + j, 0:SK], ACT.Exp, bias=neg_max[:, p, j:j + 1], accum_out=sums[:, p, j:j + 1]).then_inc(k.a_exp.sem, 1)

                take_keys(0, 0)
                with act.Fori(0, B // 2 - 1) as i:
                    softmax(i, 0)
                    take_keys(i, 1)
                    softmax(i, 1)
                    take_keys(i + 1, 0)
                i = B // 2 - 1
                softmax(i, 0)
                take_keys(i, 1)
                softmax(i, 1)

            @block.vector
            def _(dve):
                def prepare(i, p):
                    b = 2 * i + p
                    dve.wait_ge(k.a_scored.sem, k.a_scored.at(b - 1))
                    dve.wait_ge(k.a_mask[p].sem, k.a_mask[p].at(i + 1))
                    dve.tensor_scalar(mask_b[p][:, :], mask_i[p][:, :], 1.0, MASKED, ALU.is_equal, ALU.mult).then_inc(k.a_maskb.sem, 1)
                    for c in range(C):
                        q = k.q_t[:, c, bass.ds(b * S, S)].unsqueeze(1).broadcast_to([P, HC, S])
                        last = dve.tensor_tensor(q_blk[p][:, c, :].rearrange("p (h q) -> p h q", h=HC), q, c_["head_block"].rearrange("p (h q) -> p h q", h=HC), ALU.mult)
                    last.then_inc(k.a_qblk.sem, 1)

                def values(i, p):
                    b = 2 * i + p
                    dve.wait_ge(k.a_keys_done.sem, k.a_keys_done.at(b + 1))
                    dve.wait_ge(k.a_out.sem, k.a_out.at(b - 1))
                    dve.tensor_copy(v[p][:, :, :].rearrange("p r n -> p (r n)"), ps[:, VB, :]).then_inc(k.a_vcopied.sem, 1)

                def softmax(i, p):
                    b = 2 * i + p
                    dve.wait_ge(k.a_scored.sem, k.a_scored.at(b + 1))
                    dve.tensor_reduce(neg_max[:, p, :], ps[:, SB:SB + 4, 0:SK], AX.X, ALU.max, negate=True).then_inc(k.a_max.sem, 1)

                def normalise(i, p):
                    b = 2 * i + p
                    dve.wait_ge(k.a_exp.sem, k.a_exp.at(4 * (b + 1)))
                    dve.reciprocal(inv[:, p, :], sums[:, p, :]).then_inc(k.a_inv.sem, 1)
                    dve.wait_ge(k.a_inv.sem, k.a_inv.at(b + 1))
                    dve.wait_ge(k.a_pt.sem, k.a_pt.at(3 * b))
                    for j in range(4):
                        dve.tensor_scalar(pn[:, j, :], probs[p][:, j, :], inv[:, p, j:j + 1], None, ALU.mult).then_inc(k.a_normed.sem, 1)

                def outputs(i, p):
                    b = 2 * i + p
                    dve.wait_ge(k.a_out.sem, k.a_out.at(b))
                    for r in range(2):
                        dve.wait_ge(k.a_pt.sem, k.a_pt.at(3 * b + r + 1))
                        dve.tensor_copy(p_t[:, r, :], ps[:, SB + r, :]).then_inc(k.a_ptcopied.sem, 1)
                    dve.wait_ge(k.a_pt.sem, k.a_pt.at(3 * b + 3))
                    dve.tensor_copy(p_last[0:1, :], ps[0:1, SB + 2, :]).then_inc(k.a_ptcopied.sem, 1)
                    dve.wait_ge(k.a_out.sem, k.a_out.at(b + 1))
                    for c in range(C):
                        last = dve.tensor_tensor(o_own[:, c, :, :], ps[:, OB, c * D:(c + 1) * D].rearrange("p (h q) -> p h q", h=HC),
                                                 c_["head_block"].rearrange("p (h q) -> p h q", h=HC), ALU.mult)
                    last.then_inc(k.a_own.sem, 1)
                    dve.wait_ge(k.a_own.sem, k.a_own.at(b + 1))
                    dve.tensor_reduce(k.n_t[:, :, bass.ds(b * S, S)], o_own[:, :, :, :].rearrange("p c h q -> p c q h"), AX.X, ALU.add)

                prepare(0, 0)
                values(0, 0)
                with dve.Fori(0, B // 2 - 1) as i:
                    for p in range(2):
                        nxt = (i, 1) if p == 0 else (i + 1, 0)
                        softmax(i, p)
                        prepare(*nxt)
                        normalise(i, p)
                        values(*nxt)
                        outputs(i, p)
                i = B // 2 - 1
                softmax(i, 0)
                prepare(i, 1)
                normalise(i, 0)
                values(i, 1)
                outputs(i, 0)
                softmax(i, 1)
                normalise(i, 1)
                outputs(i, 1)

    def add_out(block):
        @block.vector
        def _(dve):
            for g in range(G):
                for m in range(C):
                    dve.wait_ge(k.projected.sem, k.projected.at(g * C + m + 1))
                    dve.tensor_tensor(k.x_t[:, m, group(g)], k.x_t[:, m, group(g)], ps[:, g * C + m, :], ALU.add)
    project(k, k.w["L0_xattn_wout_t"], k.n_t, add_out)


def stage_recurrence(k):
    nc, ps = k.nc, k.ps
    layernorm(k)
    w1, w2 = k.w["L0_attn_W1"], k.w["L0_attn_W2"]
    bias1, bias2, init = k.w["L0_attn_b1"], k.w["L0_attn_b2"], k.w["L0_attn_init_h"]
    with ExitStack() as ctx:
        bias_half = k.sb("bias_half", [P, J], ctx=ctx)
        g_init = k.sb("g_init", [P, 2, J], ctx=ctx)
        sig = [k.sb(f"sig{p}", [P, 3, TG], ctx=ctx) for p in range(2)]
        gate = [k.sb(f"gate{p}", [P, 2, TG], ctx=ctx) for p in range(2)]
        inv = [k.sb(f"ginv{p}", [P, TG], ctx=ctx) for p in range(2)]
        val = [k.sb(f"val{p}", [P, TG], ctx=ctx) for p in range(2)]
        hid = k.sb("hid", [P, J, TG], ctx=ctx)
        with nc.Block() as block:
            @block.tensor
            def _(pe):
                with pe.Fori(0, G) as g:
                    for j in range(J):
                        u = J * g + j
                        pe.wait_ge(k.r_gated.sem, k.r_gated.at(u - 1))
                        for part in range(3):
                            for c in range(C):
                                last = pe.matmul(ps[:, 3 * (j % 2) + part, :], w1[:, c, part * DIN + j * P:part * DIN + (j + 1) * P],
                                                 k.n_t[:, c, group(g)], start=(c == 0), stop=(c == C - 1))
                        last.then_inc(k.r_proj.sem, 1)
                    pe.wait_ge(k.r_added.sem, k.r_added.at(g))
                    for m in range(C):
                        for j in range(J):
                            pe.wait_ge(k.r_scan.sem, k.r_scan.at(J * g + j + 1))
                            last = pe.matmul(ps[:, 6 + m, :], w2[:, j, m * P:(m + 1) * P], hid[:, j, :], start=(j == 0), stop=(j == J - 1))
                    last.then_inc(k.r_out.sem, 1)

            @block.scalar
            def _(act):
                act.activation(g_init[:, 0, :], init[:, 0, :], ACT.Sigmoid).then_inc(k.r_init.sem, 1)
                with act.Fori(0, G) as g:
                    for j in range(J):
                        u = J * g + j
                        act.wait_ge(k.r_proj.sem, k.r_proj.at(u + 1))
                        act.wait_ge(k.r_valued.sem, k.r_valued.at(u - 1))
                        for part in range(3):
                            last = act.activation(sig[j % 2][:, part, :], ps[:, 3 * (j % 2) + part, :], ACT.Sigmoid, bias=bias1[:, 0, part * J + j:part * J + j + 1])
                        last.then_inc(k.r_sig.sem, 1)

            @block.vector
            def _(dve):
                dve.tensor_scalar(bias_half[:, :], bias1[:, 0, 0:J], 0.5, None, ALU.add).then_inc(k.r_init.sem, 1)
                dve.wait_ge(k.r_init.sem, k.r_init.at(2))
                dve.scalar_tensor_tensor(g_init[:, 1, :], init[:, 0, :], 0.5, g_init[:, 0, :], ALU.add, ALU.max).then_inc(k.r_init.sem, 1)
                with dve.Fori(0, G) as g:
                    for j in range(J):
                        u = J * g + j
                        p = j % 2
                        sg, sf, si = (sig[p][:, n, :] for n in range(3))
                        dve.wait_ge(k.r_sig.sem, k.r_sig.at(u + 1))
                        dve.tensor_scalar(gate[p][:, 0, :], sf, TINY, None, ALU.max).then_inc(k.r_floor.sem, 1)
                        dve.scalar_tensor_tensor(val[p][:, :], ps[:, 3 * p, :], bias_half[:, j:j + 1], sg, ALU.add, ALU.max).then_inc(k.r_gated.sem, 1)
                        dve.wait_ge(k.r_floor.sem, k.r_floor.at(u + 1))
                        dve.scalar_tensor_tensor(gate[p][:, 1, :], si, TINY, gate[p][:, 0, :], ALU.max, ALU.add).then_inc(k.r_sum.sem, 1)
                        dve.wait_ge(k.r_sum.sem, k.r_sum.at(u + 1))
                        dve.reciprocal(inv[p][:, :], gate[p][:, 1, :]).then_inc(k.r_inv.sem, 1)
                        dve.wait_ge(k.r_inv.sem, k.r_inv.at(u + 1))
                        dve.scalar_tensor_tensor(gate[p][:, 1, :], si, TINY, inv[p][:, :], ALU.max, ALU.mult)
                        dve.tensor_tensor(gate[p][:, 0, :], gate[p][:, 0, :], inv[p][:, :], ALU.mult).then_inc(k.r_gates.sem, 1)
                        dve.wait_ge(k.r_gates.sem, k.r_gates.at(u + 1))
                        dve.tensor_tensor(val[p][:, :], val[p][:, :], gate[p][:, 1, :], ALU.mult).then_inc(k.r_valued.sem, 1)
                        dve.wait_ge(k.r_valued.sem, k.r_valued.at(u + 1))
                        first_val, first_coef = val[p][:, 0:TG:S], gate[p][:, 0, 0:TG:S]
                        dve.scalar_tensor_tensor(first_val, first_coef, g_init[:, 1, j:j + 1], first_val, ALU.mult, ALU.add).then_inc(k.r_first.sem, 1)
                        dve.wait_ge(k.r_first.sem, k.r_first.at(2 * u + 1))
                        dve.tensor_scalar(first_coef, first_coef, 0.0, None, ALU.mult).then_inc(k.r_first.sem, 1)
                        dve.wait_ge(k.r_first.sem, k.r_first.at(2 * u + 2))
                        dve.wait_ge(k.r_out.sem, k.r_out.at(g))
                        dve.tensor_tensor_scan(hid[:, j, :], gate[p][:, 0, :], val[p][:, :], 0.0, ALU.mult, ALU.add).then_inc(k.r_scan.sem, 1)
                    dve.wait_ge(k.r_out.sem, k.r_out.at(g + 1))
                    for m in range(C):
                        x = k.x_t[:, m, group(g)]
                        last = dve.scalar_tensor_tensor(x, ps[:, 6 + m, :], bias2[:, 0, m:m + 1], x, ALU.add, ALU.add)
                    last.then_inc(k.r_added.sem, 1)


def transpose_weights(k, cw, n):
    nc, ps, c_ = k.nc, k.ps, k.c
    with nc.Block() as block:
        @block.tensor
        def _(pe):
            for t in range(NT):
                last = pe.transpose(ps[0:n, t // 4, (t % 4) * P:(t % 4 + 1) * P], cw[:, t, 0:n], c_["ident"])
            last.then_inc(k.m_cwt.sem, 1)

        @block.vector
        def _(dve):
            dve.wait_ge(k.m_cwt.sem, k.m_cwt.at(1))
            dve.tensor_copy(k.big[0:n, 0:4, 0:512], ps[0:n, 0:4, :]).then_inc(k.m_cwt.sem, 1)

        @block.sync
        def _(sp):
            sp.wait_ge(k.m_cwt.sem, k.m_cwt.at(2))
            sp.dma_start(k.cw_rows[0:n, :].rearrange("e (a b) -> e a b", a=4), k.big[0:n, 0:4, 0:512]).then_inc(k.m_rows.sem, 16)
            sp.wait_ge(k.m_rows.sem, k.m_rows.at(1))
    k.m_cwt.base += 2
    k.m_rows.base += 1


def stage_first_mixture(k):
    nc, ps, c_ = k.nc, k.ps, k.c
    layernorm(k)
    wg = k.w["L0_ffn_Wg"]
    with ExitStack() as ctx:
        lg = k.sb("lg", [P, NT, E0], ctx=ctx)
        v8 = k.sb("v8", [P, NT, 8], ctx=ctx)
        i8 = k.sb("i8", [P, NT, 8], U32, ctx=ctx)
        i8f = k.sb("i8f", [P, NT, 8], ctx=ctx)
        ex = k.sb("ex", [P, NT, 8], ctx=ctx)
        z = k.sb("z", [P, 4, NT], ctx=ctx)
        one = k.sb("one", [P, NT, E0], ctx=ctx)
        cw = k.sb("cw", [P, NT, E0 + 1], ctx=ctx)
        with nc.Block() as block:
            @block.tensor
            def _(pe):
                for t in range(NT):
                    for c in range(C):
                        last = pe.matmul(ps[:, 0, t * E0:(t + 1) * E0], k.n_t[:, c, t * P:(t + 1) * P], wg[:, c, :], start=(c == 0), stop=(c == C - 1))
                last.then_inc(k.m_logits.sem, 1)

            @block.scalar
            def _(act):
                act.wait_ge(k.m_shift.sem, k.m_shift.at(1))
                act.activation(ex[:, :, :], ex[:, :, :], ACT.Exp).then_inc(k.m_expd.sem, 1)

            @block.vector
            def _(dve):
                dve.wait_ge(k.m_logits.sem, k.m_logits.at(1))
                dve.tensor_copy(lg[:, :, :].rearrange("p t e -> p (t e)"), ps[:, 0, 0:NT * E0]).then_inc(k.m_chain.sem, 1)
                dve.wait_ge(k.m_chain.sem, k.m_chain.next())
                top8(k, dve, lg, v8, i8, i8f)
                dve.tensor_tensor(ex[:, :, :], v8[:, :, :], v8[:, :, 0:1].broadcast_to([P, NT, 8]), ALU.subtract).then_inc(k.m_shift.sem, 1)
                dve.wait_ge(k.m_expd.sem, k.m_expd.at(1))
                dve.tensor_reduce(z[:, 0, :], ex[:, :, :], AX.X, ALU.add).then_inc(k.m_chain.sem, 1)
                dve.wait_ge(k.m_chain.sem, k.m_chain.next())
                dve.tensor_scalar(z[:, 1, :], z[:, 0, :], 1e-9, None, ALU.mult).then_inc(k.m_chain.sem, 1)
                dve.wait_ge(k.m_chain.sem, k.m_chain.next())
                dve.tensor_tensor(z[:, 2, :], ex[:, :, 0], ex[:, :, 1], ALU.add).then_inc(k.m_chain.sem, 1)
                dve.wait_ge(k.m_chain.sem, k.m_chain.next())
                dve.tensor_tensor(z[:, 1, :], z[:, 1, :], z[:, 2, :], ALU.add).then_inc(k.m_chain.sem, 1)
                dve.wait_ge(k.m_chain.sem, k.m_chain.next())
                dve.reciprocal(z[:, 3, :], z[:, 1, :]).then_inc(k.m_chain.sem, 1)
                dve.wait_ge(k.m_chain.sem, k.m_chain.next())
                dve.memset(cw[:, :, :], 0.1).then_inc(k.m_chain.sem, 1)
                dve.wait_ge(k.m_chain.sem, k.m_chain.next())
                for n in range(K0):
                    dve.tensor_tensor(z[:, n, :], ex[:, :, n], z[:, 3, :], ALU.mult).then_inc(k.m_chain.sem, 1)
                    dve.wait_ge(k.m_chain.sem, k.m_chain.next())
                    dve.tensor_tensor(one[:, :, :], c_["iota"][:, 0:E0].unsqueeze(1).broadcast_to([P, NT, E0]), i8f[:, :, n:n + 1].broadcast_to([P, NT, E0]), ALU.is_equal).then_inc(k.m_chain.sem, 1)
                    dve.wait_ge(k.m_chain.sem, k.m_chain.next())
                    w = z[:, n, :].unsqueeze(2).broadcast_to([P, NT, E0])
                    if n == 0:
                        dve.tensor_tensor(cw[:, :, 0:E0], one[:, :, :], w, ALU.mult).then_inc(k.m_chain.sem, 1)
                        dve.wait_ge(k.m_chain.sem, k.m_chain.next())
                    else:
                        dve.tensor_tensor(one[:, :, :], one[:, :, :], w, ALU.mult).then_inc(k.m_chain.sem, 1)
                        dve.wait_ge(k.m_chain.sem, k.m_chain.next())
                        dve.tensor_tensor(cw[:, :, 0:E0], cw[:, :, 0:E0], one[:, :, :], ALU.add).then_inc(k.m_chain.sem, 1)
                        dve.wait_ge(k.m_chain.sem, k.m_chain.next())
        for s in (k.m_logits, k.m_shift, k.m_expd):
            s.base += 1
        transpose_weights(k, cw, E0 + 1)

    FC = F0 // P
    with ExitStack() as ctx:
        w1 = [k.sb(f"m1w{p}", [P, C, F0], ctx=ctx) for p in range(2)]
        w2 = [k.sb(f"m2w{p}", [P, FC, D], ctx=ctx) for p in range(2)]
        b1 = [k.sb(f"m1b{p}", [P, FC], ctx=ctx) for p in range(2)]
        b2 = [k.sb(f"m2b{p}", [P, C], ctx=ctx) for p in range(2)]
        cwb = [k.sb(f"cwb{p}", [P, T], ctx=ctx) for p in range(2)]
        act_h = k.sb("act_h", [P, FC, TG], ctx=ctx)
        yw = k.sb("yw", [P, C, TG], ctx=ctx)
        NE = E0 + 1
        with nc.Block() as block:
            @block.sync
            def _(sp):
                d = k.dram

                def fetch(e, i, p):
                    sp.wait_ge(k.m_y.sem, k.m_y.at(G * (e - 1)))
                    sp.wait_ge(k.m_added.sem, k.m_added.at(G * (e - 1)))
                    row = bass.ds(e, 1)
                    sp.dma_start(w1[p][:, :, :], d["m0_w1"][row, :, :].rearrange("o (c p) n -> p (o c) n", p=P)).then_inc(k.m_w[p].sem, 16)
                    sp.dma_start(w2[p][:, :, :], d["m0_w2"][row, :, :].rearrange("o (c p) n -> p (o c) n", p=P)).then_inc(k.m_w[p].sem, 16)
                    sp.dma_start(b1[p][:, :], d["m0_b1"][row, :, :].rearrange("o p n -> p (o n)")).then_inc(k.m_w[p].sem, 16)
                    sp.dma_start(b2[p][:, :], d["m0_b2"][row, :, :].rearrange("o p n -> p (o n)")).then_inc(k.m_w[p].sem, 16)
                    sp.dma_start(cwb[p][:, :], k.cw_rows[row, :].broadcast_to([P, T])).then_inc(k.m_w[p].sem, 16)
                with sp.Fori(0, NE // 2) as i:
                    fetch(2 * i, i, 0)
                    fetch(2 * i + 1, i, 1)
                fetch(NE - 1, NE // 2, 0)

            def over_experts(eng, unit, name):
                with eng.Fori(0, NE // 2) as i:
                    for p in range(2):
                        with eng.Fori(0, G) as g:
                            unit((2 * i + p) * G + g, g, i, p)
                with eng.Fori(0, G) as g:
                    unit((NE - 1) * G + g, g, NE // 2, 0)

            @block.tensor
            def _(pe):
                def unit(u, g, i, p):
                    pe.wait_ge(k.m_w[p].sem, k.m_w[p].at(5 * (i + 1)))
                    for f in range(FC):
                        pe.wait_ge(k.m_act.sem, k.m_act.at(u * FC + f - 3))
                        for c in range(C):
                            last = pe.matmul(ps[:, f % 4, :], w1[p][:, c, f * P:(f + 1) * P], k.n_t[:, c, group(g)], start=(c == 0), stop=(c == C - 1))
                        last.then_inc(k.m_h.sem, 1)
                    pe.wait_ge(k.m_added.sem, k.m_added.at(u))
                    for m in range(C):
                        for f in range(FC):
                            if m == 0:
                                pe.wait_ge(k.m_act.sem, k.m_act.at(u * FC + f + 1))
                            last = pe.matmul(ps[:, 4 + m, :], w2[p][:, f, m * P:(m + 1) * P], act_h[:, f, :], start=(f == 0), stop=(f == FC - 1))
                    last.then_inc(k.m_y.sem, 1)
                over_experts(pe, unit, "pe")

            @block.scalar
            def _(act):
                def unit(u, g, i, p):
                    act.wait_ge(k.m_w[p].sem, k.m_w[p].at(5 * (i + 1)))
                    act.wait_ge(k.m_y.sem, k.m_y.at(u))
                    for f in range(FC):
                        act.wait_ge(k.m_h.sem, k.m_h.at(u * FC + f + 1))
                        act.activation(act_h[:, f, :], ps[:, f % 4, :], ACT.Silu, bias=b1[p][:, f:f + 1]).then_inc(k.m_act.sem, 1)
                over_experts(act, unit, "act")

            @block.vector
            def _(dve):
                def unit(u, g, i, p):
                    dve.wait_ge(k.m_w[p].sem, k.m_w[p].at(5 * (i + 1)))
                    dve.wait_ge(k.m_y.sem, k.m_y.at(u + 1))
                    for m in range(C):
                        last = dve.scalar_tensor_tensor(yw[:, m, :], ps[:, 4 + m, :], b2[p][:, m:m + 1], cwb[p][:, group(g)], ALU.add, ALU.mult)
                    last.then_inc(k.m_yw.sem, 1)
                    dve.wait_ge(k.m_yw.sem, k.m_yw.at(u + 1))
                    x = k.x_t[:, :, group(g)]
                    dve.tensor_tensor(x, x, yw[:, :, :], ALU.add).then_inc(k.m_added.sem, 1)
                over_experts(dve, unit, "dve")
        units = NE * G
        k.m_y.base += units
        k.m_h.base += units * FC
        k.m_act.base += units * FC
        k.m_yw.base += units
        k.m_added.base += units
        k.m_w[0].base += 5 * (NE // 2 + 1)
        k.m_w[1].base += 5 * (NE // 2)


def top8(k, dve, values, v8, i8, i8f):
    for t in range(NT):
        last = dve.max(v8[:, t, :], values[:, t, :])
    last.then_inc(k.m_chain.sem, 1)
    dve.wait_ge(k.m_chain.sem, k.m_chain.next())
    for t in range(NT):
        last = dve.max_index(i8[:, t, :], v8[:, t, :], values[:, t, :])
    last.then_inc(k.m_chain.sem, 1)
    dve.wait_ge(k.m_chain.sem, k.m_chain.next())
    dve.tensor_copy(i8f[:, :, :], i8[:, :, :]).then_inc(k.m_chain.sem, 1)
    dve.wait_ge(k.m_chain.sem, k.m_chain.next())


def stage_single_attention(k):
    nc, ps, c_ = k.nc, k.ps, k.c
    layernorm(k)
    scale = D ** -0.5

    def take_q(block):
        @block.scalar
        def _(act):
            for g in range(G):
                for m in range(C):
                    act.wait_ge(k.projected.sem, k.projected.at(g * C + m + 1))
                    act.activation(k.q_t[:, m, group(g)], ps[:, g * C + m, :], ACT.Identity, bias=k.w["L1_xattn_bq"][:, 0, m:m + 1])
    project(k, k.w["L1_xattn_wq"], k.n_t, take_q)

    with ExitStack() as ctx:
        QB = 4
        NQ = B // QB
        qp_t = k.big
        q_bk = k.sb("q_bk", [1, T], ctx=ctx)

        def take_qp(block):
            @block.scalar
            def _(act):
                for g in range(G):
                    for m in range(C):
                        act.wait_ge(k.projected.sem, k.projected.at(g * C + m + 1))
                        act.activation(qp_t[:, m, group(g)], ps[:, g * C + m, :], ACT.Copy, scale=scale).then_inc(k.taken.sem, 1)
        project(k, k.w["L1_xattn_wk_t"], k.q_t, take_qp)
        with nc.Block() as block:
            @block.tensor
            def _(pe):
                for g in range(G):
                    for c in range(C):
                        last = pe.matmul(ps[0:1, g, :], k.w["L1_xattn_bk"][:, 0, c:c + 1], k.q_t[:, c, group(g)], start=(c == 0), stop=(c == C - 1))
                    last.then_inc(k.projected.sem, 1)

            @block.scalar
            def _(act):
                for g in range(G):
                    act.wait_ge(k.projected.sem, k.projected.at(g + 1))
                    act.activation(q_bk[0:1, group(g)], ps[0:1, g, :], ACT.Copy, scale=scale)
        k.projected.base += G

        ctx_t = [k.sb(f"b_ctx_t{p}", [P, QB, C, SK], ctx=ctx) for p in range(2)]
        ctx_n = [k.sb(f"b_ctx{p}", [P, QB, 2, D], ctx=ctx) for p in range(2)]
        ctx_l = [k.sb(f"b_ctx_last{p}", [1, QB, D], ctx=ctx) for p in range(2)]
        q_s = [k.sb(f"b_q{p}", [P, C, P], ctx=ctx) for p in range(2)]
        qb_s = [k.sb(f"b_qbk{p}", [1, P], ctx=ctx) for p in range(2)]
        neg_max = k.sb("b_neg_max", [P, 2], ctx=ctx)
        sums = k.sb("b_sums", [P, 2], ctx=ctx)
        inv = k.sb("b_inv", [P, 2], ctx=ctx)
        probs = [k.sb(f"b_probs{p}", [P, SK], ctx=ctx) for p in range(2)]
        pn = [k.sb(f"b_pn{p}", [P, SK], ctx=ctx) for p in range(2)]
        p_t = [k.sb(f"b_p_t{p}", [P, 2, P], ctx=ctx) for p in range(2)]
        p_l = [k.sb(f"b_p_last{p}", [1, P], ctx=ctx) for p in range(2)]
        SB, TB, OB = 0, 2, 4

        with nc.Block() as block:
            @block.sync
            def _(sp):
                def fetch(i, p):
                    n = 2 * i + p
                    sp.wait_ge(k.b_scored.sem, k.b_scored.at(n - 1))
                    for j in range(QB):
                        sp.dma_start(ctx_t[p][:, j, :, :], k.dram["ctx_t"][bass.ds(n * QB + j, 1), :, :].rearrange("o (c p) n -> p (o c) n", p=P)).then_inc(k.b_ctx_t[p].sem, 16)
                with sp.Fori(0, NQ // 2) as i:
                    fetch(i, 0)
                    fetch(i, 1)

            @block.gpsimd
            def _(pool):
                def fetch(i, p):
                    n = 2 * i + p
                    pool.wait_ge(k.b_out.sem, k.b_out.at(n - 1))
                    for j in range(QB):
                        row = k.dram["ctx"][bass.ds(n * QB + j, 1), :, :]
                        pool.dma_start(ctx_n[p][:, j, :, :], row[:, 0:2 * P, :].rearrange("o (r p) d -> p (o r) d", p=P)).then_inc(k.b_ctx[p].sem, 16)
                        pool.dma_start(ctx_l[p][0:1, j, :], row[:, 2 * P, :]).then_inc(k.b_ctx[p].sem, 16)
                with pool.Fori(0, NQ // 2) as i:
                    fetch(i, 0)
                    fetch(i, 1)

            @block.tensor
            def _(pe):
                def scores(i, p):
                    n = 2 * i + p
                    pe.wait_ge(k.b_ctx_t[p].sem, k.b_ctx_t[p].at(QB * (i + 1)))
                    pe.wait_ge(k.b_qs.sem, k.b_qs.at(n + 1))
                    pe.wait_ge(k.b_exp.sem, k.b_exp.at(n - 1))
                    pe.matmul(ps[:, SB + p, 0:SK], qb_s[p][0:1, :], k.ones_row[0:1, :], start=True, stop=False, skip_group_check=True)
                    for j in range(QB):
                        for c in range(C):
                            last = pe.matmul(ps[j * S:(j + 1) * S, SB + p, 0:SK], q_s[p][:, c, j * S:(j + 1) * S], ctx_t[p][:, j, c, :],
                                             start=False, stop=(c == C - 1), skip_group_check=True)
                    last.then_inc(k.b_scored.sem, 1)

                def weigh(i, p):
                    n = 2 * i + p
                    pe.wait_ge(k.b_normed.sem, k.b_normed.at(n + 1))
                    pe.wait_ge(k.b_tcopied.sem, k.b_tcopied.at(n - 1))
                    for r in range(2):
                        pe.transpose(ps[:, TB + p, r * P:(r + 1) * P], pn[p][:, r * P:(r + 1) * P], c_["ident"])
                    pe.transpose(ps[0:1, TB + p, 2 * P:3 * P], pn[p][:, 2 * P:SK], c_["ident"]).then_inc(k.b_trans.sem, 1)
                    pe.wait_ge(k.b_ctx[p].sem, k.b_ctx[p].at(2 * QB * (i + 1)))
                    pe.wait_ge(k.b_taken.sem, k.b_taken.at(n - 1))
                    pe.wait_ge(k.b_tcopied.sem, k.b_tcopied.at(n + 1))
                    for c in range(C):
                        for j in range(QB):
                            out = ps[:, OB + p, c * P + j * S:c * P + (j + 1) * S]
                            for r in range(2):
                                pe.matmul(out, ctx_n[p][:, j, r, c * P:(c + 1) * P], p_t[p][:, r, j * S:(j + 1) * S], start=(r == 0), stop=False)
                            last = pe.matmul(out, ctx_l[p][0:1, j, c * P:(c + 1) * P], p_l[p][0:1, j * S:(j + 1) * S], start=False, stop=True)
                    last.then_inc(k.b_out.sem, 1)

                scores(0, 0)
                with pe.Fori(0, NQ // 2 - 1) as i:
                    scores(i, 1)
                    weigh(i, 0)
                    scores(i + 1, 0)
                    weigh(i, 1)
                i = NQ // 2 - 1
                scores(i, 1)
                weigh(i, 0)
                weigh(i, 1)

            @block.scalar
            def _(act):
                def softmax(i, p):
                    n = 2 * i + p
                    act.wait_ge(k.b_max.sem, k.b_max.at(n + 1))
                    act.wait_ge(k.b_normed.sem, k.b_normed.at(n - 1))
                    act.activation(probs[p][:, :], ps[:, SB + p, 0:SK], ACT.Exp, bias=neg_max[:, p:p + 1], accum_out=sums[:, p:p + 1]).then_inc(k.b_exp.sem, 1)
                with act.Fori(0, NQ // 2) as i:
                    softmax(i, 0)
                    softmax(i, 1)

            @block.vector
            def _(dve):
                def queries(i, p):
                    n = 2 * i + p
                    dve.wait_ge(k.b_scored.sem, k.b_scored.at(n - 1))
                    dve.tensor_copy(q_s[p][:, :, :], qp_t[:, 0:C, bass.ds(n * P, P)])
                    dve.tensor_copy(qb_s[p][0:1, :], q_bk[0:1, bass.ds(n * P, P)]).then_inc(k.b_qs.sem, 1)

                def softmax(i, p):
                    n = 2 * i + p
                    dve.wait_ge(k.b_scored.sem, k.b_scored.at(n + 1))
                    dve.tensor_reduce(neg_max[:, p:p + 1], ps[:, SB + p, 0:SK], AX.X, ALU.max, negate=True).then_inc(k.b_max.sem, 1)
                    dve.wait_ge(k.b_exp.sem, k.b_exp.at(n + 1))
                    dve.reciprocal(inv[:, p:p + 1], sums[:, p:p + 1]).then_inc(k.b_inv.sem, 1)
                    dve.wait_ge(k.b_inv.sem, k.b_inv.at(n + 1))
                    dve.wait_ge(k.b_trans.sem, k.b_trans.at(n - 1))
                    dve.tensor_scalar(pn[p][:, :], probs[p][:, :], inv[:, p:p + 1], None, ALU.mult).then_inc(k.b_normed.sem, 1)

                def outputs(i, p):
                    n = 2 * i + p
                    dve.wait_ge(k.b_out.sem, k.b_out.at(n - 1))
                    dve.wait_ge(k.b_trans.sem, k.b_trans.at(n + 1))
                    dve.tensor_copy(p_l[p][0:1, :], ps[0:1, TB + p, 2 * P:3 * P])
                    dve.tensor_copy(p_t[p][:, :, :].rearrange("p r q -> p (r q)"), ps[:, TB + p, 0:2 * P]).then_inc(k.b_tcopied.sem, 1)
                    dve.wait_ge(k.b_out.sem, k.b_out.at(n + 1))
                    dve.tensor_copy(k.n_t[:, :, bass.ds(n * P, P)], ps[:, OB + p, 0:2 * P].rearrange("p (c q) -> p c q", c=C)).then_inc(k.b_taken.sem, 1)

                queries(0, 0)
                with dve.Fori(0, NQ // 2 - 1) as i:
                    queries(i, 1)
                    softmax(i, 0)
                    outputs(i, 0)
                    queries(i + 1, 0)
                    softmax(i, 1)
                    outputs(i, 1)
                i = NQ // 2 - 1
                queries(i, 1)
                softmax(i, 0)
                outputs(i, 0)
                softmax(i, 1)
                outputs(i, 1)

    def add_out(block):
        @block.vector
        def _(dve):
            for g in range(G):
                for m in range(C):
                    dve.wait_ge(k.projected.sem, k.projected.at(g * C + m + 1))
                    x = k.x_t[:, m, group(g)]
                    dve.scalar_tensor_tensor(x, ps[:, g * C + m, :], k.w["L1_xattn_bv"][:, 0, m:m + 1], x, ALU.add, ALU.add)
    project(k, k.w["L1_xattn_wv"], k.n_t, add_out)


def stage_causal_attention(k):
    nc, ps, c_ = k.nc, k.ps, k.c
    layernorm(k)
    scale = D ** -0.5
    k_t = k.big

    def take_q(block):
        @block.vector
        def _(dve):
            for g in range(G):
                for m in range(C):
                    dve.wait_ge(k.projected.sem, k.projected.at(g * C + m + 1))
                    dve.tensor_scalar(k.q_t[:, m, group(g)], ps[:, g * C + m, :], k.w["L1_attn_bq"][:, 0, m:m + 1], scale, ALU.add, ALU.mult)
    project(k, k.w["L1_attn_Wq_t"], k.n_t, take_q)

    def take_k(block):
        @block.scalar
        def _(act):
            for g in range(G):
                for m in range(C):
                    act.wait_ge(k.projected.sem, k.projected.at(g * C + m + 1))
                    act.activation(k_t[:, m, group(g)], ps[:, g * C + m, :], ACT.Identity, bias=k.w["L1_attn_bk"][:, 0, m:m + 1])
    project(k, k.w["L1_attn_Wk_t"], k.n_t, take_k)

    with ExitStack() as ctx:
        n_s = [k.sb(f"c_n{p}", [P, C, P], ctx=ctx) for p in range(2)]
        q_s = [k.sb(f"c_q{p}", [P, C, P], ctx=ctx) for p in range(2)]
        v = [k.sb(f"c_v{p}", [P, D], ctx=ctx) for p in range(2)]
        neg_max = k.sb("c_neg_max", [P, 2], ctx=ctx)
        sums = k.sb("c_sums", [P, 2], ctx=ctx)
        inv = k.sb("c_inv", [P, 2], ctx=ctx)
        probs = [k.sb(f"c_probs{p}", [P, P], ctx=ctx) for p in range(2)]
        pn = [k.sb(f"c_pn{p}", [P, P], ctx=ctx) for p in range(2)]
        p_t = [k.sb(f"c_p_t{p}", [P, P], ctx=ctx) for p in range(2)]
        VB, SB, TB, OB = 0, 2, 4, 6
        wv = k.w["L1_attn_Wv_t"]

        with nc.Block() as block:
            @block.gpsimd
            def _(pool):
                with pool.Fori(0, NT // 2) as i:
                    for p in range(2):
                        t = 2 * i + p
                        pool.wait_ge(k.c_scored.sem, k.c_scored.at(t - 1))
                        pool.tensor_copy(n_s[p][:, :, :], k.n_t[:, :, bass.ds(t * P, P)])
                        pool.tensor_copy(q_s[p][:, :, :], k.q_t[:, :, bass.ds(t * P, P)]).then_inc(k.c_static.sem, 1)

            @block.tensor
            def _(pe):
                def scores(i, p):
                    t = 2 * i + p
                    pe.wait_ge(k.c_static.sem, k.c_static.at(t + 1))
                    pe.wait_ge(k.c_vcopied.sem, k.c_vcopied.at(t - 1))
                    for c in range(C):
                        pe.matmul(ps[:, VB + p, 0:D], n_s[p][:, c, :], wv[:, c, :], start=(c == 0), stop=(c == C - 1))
                    pe.wait_ge(k.c_exp.sem, k.c_exp.at(t - 1))
                    pe.matmul(ps[:, SB + p, 0:P], k.ident_bf[:, :], k.causal_bf[:, :], start=True, stop=False)
                    for c in range(C):
                        last = pe.matmul(ps[:, SB + p, 0:P], q_s[p][:, c, :], k_t[:, c, bass.ds(t * P, P)], start=False, stop=(c == C - 1))
                    last.then_inc(k.c_scored.sem, 1)

                def weigh(i, p):
                    t = 2 * i + p
                    pe.wait_ge(k.c_normed.sem, k.c_normed.at(t + 1))
                    pe.wait_ge(k.c_tcopied.sem, k.c_tcopied.at(t - 1))
                    pe.transpose(ps[:, TB + p, 0:P], pn[p][:, :], c_["ident"]).then_inc(k.c_trans.sem, 1)
                    pe.wait_ge(k.c_tcopied.sem, k.c_tcopied.at(t + 1))
                    pe.wait_ge(k.c_vcopied.sem, k.c_vcopied.at(t + 1))
                    pe.wait_ge(k.c_taken.sem, k.c_taken.at(t - 1))
                    for c in range(C):
                        last = pe.matmul(ps[:, OB + p, c * P:(c + 1) * P], v[p][:, c * P:(c + 1) * P], p_t[p][:, :], start=True, stop=True)
                    last.then_inc(k.c_out.sem, 1)

                scores(0, 0)
                with pe.Fori(0, NT // 2 - 1) as i:
                    scores(i, 1)
                    weigh(i, 0)
                    scores(i + 1, 0)
                    weigh(i, 1)
                i = NT // 2 - 1
                scores(i, 1)
                weigh(i, 0)
                weigh(i, 1)

            @block.scalar
            def _(act):
                with act.Fori(0, NT // 2) as i:
                    for p in range(2):
                        t = 2 * i + p
                        act.wait_ge(k.c_scored.sem, k.c_scored.at(t + 1))
                        act.wait_ge(k.c_out.sem, k.c_out.at(t - 1))
                        act.activation(v[p][:, :], ps[:, VB + p, 0:D], ACT.Copy).then_inc(k.c_vcopied.sem, 1)
                        act.wait_ge(k.c_max.sem, k.c_max.at(t + 1))
                        act.wait_ge(k.c_normed.sem, k.c_normed.at(t - 1))
                        act.activation(probs[p][:, :], ps[:, SB + p, 0:P], ACT.Exp, bias=neg_max[:, p:p + 1], accum_out=sums[:, p:p + 1]).then_inc(k.c_exp.sem, 1)

            @block.vector
            def _(dve):
                with dve.Fori(0, NT // 2) as i:
                    for p in range(2):
                        t = 2 * i + p
                        dve.wait_ge(k.c_scored.sem, k.c_scored.at(t + 1))
                        dve.tensor_reduce(neg_max[:, p:p + 1], ps[:, SB + p, 0:P], AX.X, ALU.max, negate=True).then_inc(k.c_max.sem, 1)
                        dve.wait_ge(k.c_exp.sem, k.c_exp.at(t + 1))
                        dve.reciprocal(inv[:, p:p + 1], sums[:, p:p + 1]).then_inc(k.c_inv.sem, 1)
                        dve.wait_ge(k.c_inv.sem, k.c_inv.at(t + 1))
                        dve.wait_ge(k.c_trans.sem, k.c_trans.at(t - 1))
                        dve.tensor_scalar(pn[p][:, :], probs[p][:, :], inv[:, p:p + 1], None, ALU.mult).then_inc(k.c_normed.sem, 1)
                        dve.wait_ge(k.c_out.sem, k.c_out.at(t - 1))
                        dve.wait_ge(k.c_trans.sem, k.c_trans.at(t + 1))
                        dve.tensor_copy(p_t[p][:, :], ps[:, TB + p, 0:P]).then_inc(k.c_tcopied.sem, 1)
                        dve.wait_ge(k.c_out.sem, k.c_out.at(t + 1))
                        for c in range(C):
                            x = k.x_t[:, c, bass.ds(t * P, P)]
                            last = dve.scalar_tensor_tensor(x, ps[:, OB + p, c * P:(c + 1) * P], k.w["L1_attn_bv"][:, 0, c:c + 1], x, ALU.add, ALU.add)
                        last.then_inc(k.c_taken.sem, 1)


def stage_second_mixture(k):
    nc, ps, c_ = k.nc, k.ps, k.c
    layernorm(k)
    NG, EG = 4, E1 // 4
    wg, gate_bias = k.w["L1_ffn_gate_w_t"], k.w["L1_ffn_gate_bias"]
    with ExitStack() as ctx:
        sc = k.sb("sc", [P, NT, E1], ctx=ctx)
        sb = k.sb("sbias", [P, NT, NG, EG], ctx=ctx)
        pair = k.sb("pair", [P, 6, NT, NG], ctx=ctx)
        rank = k.sb("rank", [P, 3, NT, NG * NG], ctx=ctx)
        allowed = k.sb("allowed", [P, NT, NG], ctx=ctx)
        masked = k.sb("masked", [P, NT, E1], ctx=ctx)
        v8 = k.sb("v8", [P, NT, 8], ctx=ctx)
        i8 = k.sb("i8", [P, NT, 8], U32, ctx=ctx)
        i8f = k.sb("i8f", [P, NT, 8], ctx=ctx)
        one = k.sb("one", [P, NT, E1], ctx=ctx)
        z = k.sb("z", [P, 2, NT], ctx=ctx)
        cw = k.sb("cw", [P, NT, E1 + 1], ctx=ctx)
        with nc.Block() as block:
            @block.tensor
            def _(pe):
                for t in range(NT):
                    for c in range(C):
                        last = pe.matmul(ps[:, 0, t * E1:(t + 1) * E1], k.n_t[:, c, t * P:(t + 1) * P], wg[:, c, :], start=(c == 0), stop=(c == C - 1))
                last.then_inc(k.m_logits.sem, 1)

            @block.scalar
            def _(act):
                act.wait_ge(k.m_logits.sem, k.m_logits.at(1))
                act.activation(sc[:, :, :].rearrange("p t e -> p (t e)"), ps[:, 0, 0:NT * E1], ACT.Sigmoid).then_inc(k.m_expd.sem, 1)

            @block.vector
            def _(dve):
                dve.wait_ge(k.m_expd.sem, k.m_expd.at(1))
                flat = sb[:, :, :, :].rearrange("p t g e -> p t (g e)")
                dve.tensor_tensor(flat, sc[:, :, :], gate_bias[:, 0:1, :].broadcast_to([P, NT, E1]), ALU.add).then_inc(k.m_chain.sem, 1)
                dve.wait_ge(k.m_chain.sem, k.m_chain.next())
                pairs = [(a, b) for a in range(EG) for b in range(a + 1, EG)]
                for n, (a, b) in enumerate(pairs):
                    last = dve.tensor_tensor(pair[:, n, :, :], sb[:, :, :, a], sb[:, :, :, b], ALU.add)
                last.then_inc(k.m_chain.sem, 1)
                dve.wait_ge(k.m_chain.sem, k.m_chain.next())
                for n in range(1, len(pairs)):
                    dve.tensor_tensor(pair[:, 0, :, :], pair[:, 0, :, :], pair[:, n, :, :], ALU.max).then_inc(k.m_chain.sem, 1)
                    dve.wait_ge(k.m_chain.sem, k.m_chain.next())
                score = pair[:, 0, :, :]
                own = score.unsqueeze(3).broadcast_to([P, NT, NG, NG])
                other = score.unsqueeze(2).broadcast_to([P, NT, NG, NG])
                r = [rank[:, n, :, :].rearrange("p t (a b) -> p t a b", a=NG) for n in range(3)]
                dve.tensor_tensor(r[0], other, own, ALU.is_gt)
                dve.tensor_tensor(r[1], other, own, ALU.is_equal).then_inc(k.m_chain.sem, 1)
                dve.wait_ge(k.m_chain.sem, k.m_chain.next())
                earlier = c_["earlier"].unsqueeze(1).broadcast_to([P, NT, NG * NG])
                dve.tensor_tensor(rank[:, 1, :, :], rank[:, 1, :, :], earlier, ALU.mult).then_inc(k.m_chain.sem, 1)
                dve.wait_ge(k.m_chain.sem, k.m_chain.next())
                dve.tensor_tensor(rank[:, 2, :, :], rank[:, 0, :, :], rank[:, 1, :, :], ALU.add).then_inc(k.m_chain.sem, 1)
                dve.wait_ge(k.m_chain.sem, k.m_chain.next())
                dve.tensor_reduce(allowed[:, :, :], r[2], AX.X, ALU.add).then_inc(k.m_chain.sem, 1)
                dve.wait_ge(k.m_chain.sem, k.m_chain.next())
                dve.tensor_scalar(allowed[:, :, :], allowed[:, :, :], 2.0, MASKED, ALU.is_ge, ALU.mult).then_inc(k.m_chain.sem, 1)
                dve.wait_ge(k.m_chain.sem, k.m_chain.next())
                dve.tensor_tensor(masked[:, :, :].rearrange("p t (g e) -> p t g e", g=NG), sb[:, :, :, :], allowed[:, :, :].unsqueeze(3).broadcast_to([P, NT, NG, EG]), ALU.add).then_inc(k.m_chain.sem, 1)
                dve.wait_ge(k.m_chain.sem, k.m_chain.next())
                top8(k, dve, masked, v8, i8, i8f)
                for n in range(K1):
                    dve.tensor_tensor(one[:, :, :], c_["iota"].unsqueeze(1).broadcast_to([P, NT, E1]), i8f[:, :, n:n + 1].broadcast_to([P, NT, E1]), ALU.is_equal).then_inc(k.m_chain.sem, 1)
                    dve.wait_ge(k.m_chain.sem, k.m_chain.next())
                    if n == 0:
                        dve.tensor_tensor(cw[:, :, 0:E1], one[:, :, :], sc[:, :, :], ALU.mult).then_inc(k.m_chain.sem, 1)
                        dve.wait_ge(k.m_chain.sem, k.m_chain.next())
                    else:
                        dve.tensor_tensor(one[:, :, :], one[:, :, :], sc[:, :, :], ALU.mult).then_inc(k.m_chain.sem, 1)
                        dve.wait_ge(k.m_chain.sem, k.m_chain.next())
                        dve.tensor_tensor(cw[:, :, 0:E1], cw[:, :, 0:E1], one[:, :, :], ALU.add).then_inc(k.m_chain.sem, 1)
                        dve.wait_ge(k.m_chain.sem, k.m_chain.next())
                dve.tensor_reduce(z[:, 0, :], cw[:, :, 0:E1], AX.X, ALU.add).then_inc(k.m_chain.sem, 1)
                dve.wait_ge(k.m_chain.sem, k.m_chain.next())
                dve.tensor_scalar(z[:, 0, :], z[:, 0, :], 1e-20, None, ALU.add).then_inc(k.m_chain.sem, 1)
                dve.wait_ge(k.m_chain.sem, k.m_chain.next())
                dve.reciprocal(z[:, 1, :], z[:, 0, :]).then_inc(k.m_chain.sem, 1)
                dve.wait_ge(k.m_chain.sem, k.m_chain.next())
                dve.tensor_scalar(z[:, 1, :], z[:, 1, :], 2.5, None, ALU.mult).then_inc(k.m_chain.sem, 1)
                dve.wait_ge(k.m_chain.sem, k.m_chain.next())
                dve.tensor_tensor(cw[:, :, 0:E1], cw[:, :, 0:E1], z[:, 1, :].unsqueeze(2).broadcast_to([P, NT, E1]), ALU.mult).then_inc(k.m_chain.sem, 1)
                dve.wait_ge(k.m_chain.sem, k.m_chain.next())
                dve.memset(cw[:, :, E1:E1 + 1], 1.0).then_inc(k.m_chain.sem, 1)
                dve.wait_ge(k.m_chain.sem, k.m_chain.next())
        for s in (k.m_logits, k.m_expd):
            s.base += 1
        transpose_weights(k, cw, E1 + 1)

    with ExitStack() as ctx:
        w1 = [k.sb(f"n1w{p}", [P, C, I1], ctx=ctx) for p in range(2)]
        w3 = [k.sb(f"n3w{p}", [P, C, I1], ctx=ctx) for p in range(2)]
        w2 = [k.sb(f"n2w{p}", [IH, 2, D], ctx=ctx) for p in range(2)]
        cwb = [k.sb(f"ncwb{p}", [P, T], ctx=ctx) for p in range(2)]
        sg = k.sb("sg", [IH, 2, TG], ctx=ctx)
        hid = k.sb("nhid", [IH, 2, TG], ctx=ctx)
        yw = k.sb("nyw", [P, C, TG], ctx=ctx)
        NE = E1 + 1
        with nc.Block() as block:
            @block.sync
            def _(sp):
                d = k.dram

                def fetch(e, i, p):
                    sp.wait_ge(k.m_y.sem, k.m_y.at(G * (e - 1)))
                    sp.wait_ge(k.m_added.sem, k.m_added.at(G * (e - 1)))
                    row = bass.ds(e, 1)
                    sp.dma_start(w1[p][:, :, :], d["m1_w1"][row, :, :].rearrange("o (c p) n -> p (o c) n", p=P)).then_inc(k.m_w[p].sem, 16)
                    sp.dma_start(w3[p][:, :, :], d["m1_w3"][row, :, :].rearrange("o (c p) n -> p (o c) n", p=P)).then_inc(k.m_w[p].sem, 16)
                    sp.dma_start(w2[p][:, :, :], d["m1_w2"][row, :, :].rearrange("o (c p) n -> p (o c) n", p=IH)).then_inc(k.m_w[p].sem, 16)
                    sp.dma_start(cwb[p][:, :], k.cw_rows[row, :].broadcast_to([P, T])).then_inc(k.m_w[p].sem, 16)
                with sp.Fori(0, NE // 2) as i:
                    fetch(2 * i, i, 0)
                    fetch(2 * i + 1, i, 1)
                fetch(NE - 1, NE // 2, 0)

            def over_experts(eng, unit):
                with eng.Fori(0, NE // 2) as i:
                    for p in range(2):
                        with eng.Fori(0, G) as g:
                            unit((2 * i + p) * G + g, g, i, p)
                with eng.Fori(0, G) as g:
                    unit((NE - 1) * G + g, g, NE // 2, 0)

            @block.tensor
            def _(pe):
                def unit(u, g, i, p):
                    pe.wait_ge(k.m_w[p].sem, k.m_w[p].at(4 * (i + 1)))
                    for h in range(2):
                        pe.wait_ge(k.m_act.sem, k.m_act.at(2 * u + h - 1))
                        for n, w in enumerate((w1, w3)):
                            for c in range(C):
                                last = pe.matmul(ps[0:IH, 2 * h + n, :], w[p][:, c, h * IH:(h + 1) * IH], k.n_t[:, c, group(g)], start=(c == 0), stop=(c == C - 1))
                        last.then_inc(k.m_h.sem, 1)
                    pe.wait_ge(k.m_added.sem, k.m_added.at(u))
                    for h in range(2):
                        pe.wait_ge(k.m_act.sem, k.m_act.at(2 * u + h + 1))
                        for m in range(C):
                            last = pe.matmul(ps[:, 4 + m, :], w2[p][:, h, m * P:(m + 1) * P], hid[:, h, :], start=(h == 0), stop=(h == 1))
                    last.then_inc(k.m_y.sem, 1)
                over_experts(pe, unit)

            @block.scalar
            def _(act):
                def unit(u, g, i, p):
                    for h in range(2):
                        act.wait_ge(k.m_h.sem, k.m_h.at(2 * u + h + 1))
                        act.wait_ge(k.m_act.sem, k.m_act.at(2 * u + h - 1))
                        act.activation(sg[:, h, :], ps[0:IH, 2 * h, :], ACT.Silu).then_inc(k.m_sg.sem, 1)
                over_experts(act, unit)

            @block.vector
            def _(dve):
                def unit(u, g, i, p):
                    dve.wait_ge(k.m_w[p].sem, k.m_w[p].at(4 * (i + 1)))
                    dve.wait_ge(k.m_y.sem, k.m_y.at(u))
                    for h in range(2):
                        dve.wait_ge(k.m_sg.sem, k.m_sg.at(2 * u + h + 1))
                        dve.tensor_tensor(hid[:, h, :], sg[:, h, :], ps[0:IH, 2 * h + 1, :], ALU.mult).then_inc(k.m_act.sem, 1)
                    dve.wait_ge(k.m_y.sem, k.m_y.at(u + 1))
                    for m in range(C):
                        last = dve.tensor_tensor(yw[:, m, :], ps[:, 4 + m, :], cwb[p][:, group(g)], ALU.mult)
                    last.then_inc(k.m_yw.sem, 1)
                    dve.wait_ge(k.m_yw.sem, k.m_yw.at(u + 1))
                    x = k.x_t[:, :, group(g)]
                    dve.tensor_tensor(x, x, yw[:, :, :], ALU.add).then_inc(k.m_added.sem, 1)
                over_experts(dve, unit)


def build(nc, dram):
    with ExitStack() as ctx:
        k = Core(nc, ctx, dram)
        k.ps = ctx.enter_context(nc.psum_tensor("ps", [P, 8, 512], F32))
        k.x_t = k.sb("x_t_sb", [P, C, T])
        k.n_t = k.sb("n_t", [P, C, T])
        k.q_t = k.sb("q_t", [P, C, T])
        k.big = k.sb("big", [P, 4, T])
        width = sum(n for _, n in CONST.values())
        k.consts = k.sb("consts_sb", [P, width])
        k.c, at = {}, 0
        for name, (_, n) in CONST.items():
            k.c[name] = k.consts[:, at:at + n]
            at += n
        k.ones_mean = k.sb("ones_mean", [P, P])
        k.ones_row = k.sb("ones_row", [1, SK])
        k.eps = k.sb("eps", [P, 1])
        k.ident_bf = k.sb("ident_bf", [P, P], BF16)
        k.repeat_bf = k.sb("repeat_bf", [S, P], BF16)
        k.causal_bf = k.sb("causal_bf", [P, P], BF16)
        k.weights = {n: P for n in ["L0_xattn_wq_t", "L0_xattn_wk_t", "L0_xattn_wv_t", "L0_xattn_wout_t", "L0_attn_W1", "L0_attn_W2",
                                    "L0_attn_b1", "L0_attn_b2", "L0_attn_init_h", "L0_ffn_Wg",
                                    "L1_xattn_wq", "L1_xattn_wk_t", "L1_xattn_wv", "L1_xattn_bq", "L1_xattn_bk", "L1_xattn_bv",
                                    "L1_attn_Wq_t", "L1_attn_Wk_t", "L1_attn_Wv_t", "L1_attn_bq", "L1_attn_bk", "L1_attn_bv", "L1_ffn_gate_w_t", "L1_ffn_gate_bias"]}
        k.w = {n: k.sb(f"w_{n}", [P, dram[n].shape[0] // P, dram[n].shape[1]]) for n in k.weights}
        k.cw_rows = nc.dram_tensor("cw_rows", [E1 + 1, T], F32, kind="Internal").ap()

        k.mean_ready = k.count("mean_ready")
        k.squared = k.count("squared")
        k.var_ready = k.count("var_ready")
        k.std_ready = k.count("std_ready")
        k.inv_ready = k.count("inv_ready")
        k.centred = k.count("centred")
        k.projected = k.count("projected")
        k.a_keys_done = k.count("a_keys_done", 2)
        k.a_kproj = k.count("a_kproj")
        k.a_kcopied = k.count("a_kcopied", 2)
        k.a_vcopied = k.count("a_vcopied", 2)
        k.a_qblk = k.count("a_qblk")
        k.a_maskb = k.count("a_maskb", 2)
        k.a_ptcopied = k.count("a_ptcopied", 3)
        k.a_scored = k.count("a_scored", 2)
        k.a_normed = k.count("a_normed", 8)
        k.a_pt = k.count("a_pt", 3)
        k.a_own = k.count("a_own", 1)
        k.a_out = k.count("a_out", 2)
        k.a_max = k.count("a_max")
        k.a_exp = k.count("a_exp")
        k.a_inv = k.count("a_inv")
        k.r_gated = k.count("r_gated", 2)
        k.r_proj = k.count("r_proj")
        k.r_added = k.count("r_added", 1)
        k.r_scan = k.count("r_scan")
        k.r_out = k.count("r_out", 1)
        k.r_init = k.count("r_init")
        k.r_valued = k.count("r_valued", 2)
        k.r_sig = k.count("r_sig")
        k.r_floor = k.count("r_floor")
        k.r_sum = k.count("r_sum")
        k.r_inv = k.count("r_inv")
        k.r_gates = k.count("r_gates")
        k.r_first = k.count("r_first")
        k.m_cwt = k.count("m_cwt")
        k.m_chain = k.count("m_chain")
        k.m_logits = k.count("m_logits")
        k.m_shift = k.count("m_shift")
        k.m_expd = k.count("m_expd")
        k.m_y = k.count("m_y", 8)
        k.m_added = k.count("m_added", 8)
        k.m_h = k.count("m_h")
        k.m_act = k.count("m_act", 4)
        k.m_yw = k.count("m_yw")
        k.m_sg = k.count("m_sg")
        k.taken = k.count("taken")
        k.b_scored = k.count("b_scored", 2)
        k.b_out = k.count("b_out", 2)
        k.b_qs = k.count("b_qs")
        k.b_exp = k.count("b_exp", 2)
        k.b_normed = k.count("b_normed", 2)
        k.b_tcopied = k.count("b_tcopied", 2)
        k.b_trans = k.count("b_trans", 2)
        k.b_taken = k.count("b_taken", 2)
        k.b_max = k.count("b_max")
        k.b_inv = k.count("b_inv")
        k.c_static = k.count("c_static")
        k.c_scored = k.count("c_scored", 2)
        k.c_vcopied = k.count("c_vcopied", 2)
        k.c_exp = k.count("c_exp", 2)
        k.c_normed = k.count("c_normed", 2)
        k.c_tcopied = k.count("c_tcopied", 2)
        k.c_trans = k.count("c_trans", 2)
        k.c_taken = k.count("c_taken", 2)
        k.c_out = k.count("c_out", 2)
        k.c_max = k.count("c_max")
        k.c_inv = k.count("c_inv")
        k.x_loaded = k.count("x_loaded", unit=16)
        k.weights_loaded = k.count("weights_loaded", unit=16)
        k.out_stored = k.count("out_stored", unit=16)
        k.m_rows = k.count("m_rows", unit=16)
        k.a_ctx = [k.count(f"a_ctx{p}", unit=16) for p in range(2)]
        k.a_mask = [k.count(f"a_mask{p}", unit=16) for p in range(2)]
        k.m_w = [k.count(f"m_w{p}", unit=16) for p in range(2)]
        k.b_ctx_t = [k.count(f"b_ctx_t{p}", unit=16) for p in range(2)]
        k.b_ctx = [k.count(f"b_ctx{p}", unit=16) for p in range(2)]

        load_all(k)
        stages = [stage_heads_attention, stage_recurrence, stage_first_mixture, stage_single_attention,
                  stage_causal_attention, stage_second_mixture]
        for s in STAGES:
            k.stage = stages[s].__name__
            stages[s](k)

        with nc.Block() as block:
            @block.sync
            def _(sp):
                sp.dma_start(dram["out"].rearrange("(c p) t -> p c t", p=P), k.x_t[:, :, :]).then_inc(k.out_stored.sem, 16)
                sp.wait_ge(k.out_stored.sem, k.out_stored.at(1))


def columns(a):
    return np.ascontiguousarray(a.reshape(-1, P).T)


def lay_out(i):
    T_ = np.transpose
    a = {
        "x_t": i["x"].reshape(T, D).T, "consts": const_table(),
        "ctx_t": T_(i["ctx_1024"], (0, 2, 1)), "ctx": i["ctx_1024"], "mask": i["mask_BxSxS2_ik1"],
        "L0_xattn_wq_t": i["L0_xattn_wq"].T, "L0_xattn_wk_t": i["L0_xattn_wk"].T, "L0_xattn_wv_t": i["L0_xattn_wv"].T,
        "L0_xattn_wout_t": i["L0_xattn_w_out"].T,
        "L0_attn_W1": i["L0_attn_W1"], "L0_attn_W2": i["L0_attn_W2"], "L0_ffn_Wg": i["L0_ffn_Wg"],
        "L1_xattn_wq": i["L1_xattn_wq"], "L1_xattn_wk_t": i["L1_xattn_wk"].T, "L1_xattn_wv": i["L1_xattn_wv"],
        "L1_attn_Wq_t": i["L1_attn_Wq"].T, "L1_attn_Wk_t": i["L1_attn_Wk"].T, "L1_attn_Wv_t": i["L1_attn_Wv"].T,
        "L1_ffn_gate_w_t": i["L1_ffn_gate_w"].T,
        "L1_ffn_gate_bias": np.broadcast_to(i["L1_ffn_gate_bias"][None, :], (P, E1)),
    }
    for n in ["L0_attn_b1", "L0_attn_b2", "L0_attn_init_h", "L1_xattn_bq", "L1_xattn_bk", "L1_xattn_bv", "L1_attn_bq", "L1_attn_bk", "L1_attn_bv"]:
        a[n] = columns(i[n])
    a["m0_w1"] = np.concatenate([i["L0_ffn_W1"], i["L0_ffn_Ws1"][None]])
    a["m0_w2"] = np.concatenate([i["L0_ffn_W2"], i["L0_ffn_Ws2"][None]])
    a["m0_b1"] = T_(np.concatenate([i["L0_ffn_b1"], i["L0_ffn_bs1"][None]]).reshape(E0 + 1, -1, P), (0, 2, 1))
    a["m0_b2"] = T_(np.concatenate([i["L0_ffn_b2"], i["L0_ffn_bs2"][None]]).reshape(E0 + 1, -1, P), (0, 2, 1))
    shared = {"m1_w1": "ws1", "m1_w3": "ws3", "m1_w2": "ws2"}
    for n, name in (("m1_w1", "w1"), ("m1_w3", "w3"), ("m1_w2", "w2")):
        both = np.concatenate([i[f"L1_ffn_{name}"], i[f"L1_ffn_{shared[n]}"][None]])
        a[n] = T_(both, (0, 2, 1))
    return {n: np.ascontiguousarray(v) for n, v in a.items()}


def kernel(**inputs):
    import concourse.bacc as bacc
    from concourse.bass_utils import run_bass_kernel_spmd

    arrays = lay_out({n: np.asarray(v) for n, v in inputs.items()})
    nc = bacc.Bacc("TRN2", target_bir_lowering=False, num_devices=1)
    dram = {n: nc.dram_tensor(f"in_{n}", a.shape, mybir.dt.from_np(a.dtype), kind="ExternalInput").ap() for n, a in arrays.items()}
    dram["out"] = nc.dram_tensor("out_0_dram", [D, T], F32, kind="ExternalOutput").ap()
    build(nc, dram)
    r = run_bass_kernel_spmd(nc, [{f"in_{n}": a for n, a in arrays.items()}], core_ids=[0])
    return np.ascontiguousarray(r.results[0]["out_0_dram"].T).reshape(B, S, D)
```

```python
from contextlib import ExitStack

import numpy as np

import concourse.bass as bass
from concourse import mybir

F32 = mybir.dt.float32
BF16 = mybir.dt.bfloat16
F16 = mybir.dt.float16
I32 = mybir.dt.int32
U32 = mybir.dt.uint32
ALU = mybir.AluOpType
ACT = mybir.ActivationFunctionType
AX = mybir.AxisListType

P = 128
B, S, D = 64, 32, 256
SK = 257
T = B * S
C = D // P
G = 4
TG = T // G
NT = T // P
H, HD = 16, 16
HC = P // HD
DIN = 512
J = DIN // P
E0, F0, K0 = 8, 1024, 2
E1, I1, K1 = 16, 192, 4
IH = I1 // 2
EPS = 1e-5
WS = 256.0
NS = 64.0
HS = 16.0
MASKED = -1e30
TINY = 1e-37

STAGES = range(6)


class Count:

    def __init__(self, sem, credit=0, unit=1):
        self.sem, self.credit, self.unit, self.base = sem, credit, unit, 0

    def at(self, n):
        return (n + self.credit + self.base) * self.unit

    def next(self):
        self.base += 1
        return self.at(0)


class Core:

    def __init__(self, nc, ctx, dram):
        self.nc, self.ctx, self.dram = nc, ctx, dram
        self.counts = []

    def sb(self, name, shape, dt=F32, ctx=None):
        if ctx is not None:
            name = f"{self.stage}_{name}"
        return (ctx or self.ctx).enter_context(self.nc.sbuf_tensor(name, shape, dt))

    def count(self, name, credit=0, unit=1):
        self.counts.append(Count(self.ctx.enter_context(self.nc.semaphore(name)), credit, unit))
        return self.counts[-1]


def group(g):
    return bass.ds(g * TG, TG)


CONST = {"ident": P, "head_block": HC * S, "repeat": P, "causal": P, "iota": P, "earlier": 16, "before": P, "token": NT}


def const_table():
    p = np.arange(P)[:, None]
    c = np.arange(P)[None, :]
    g = np.arange(16)[None, :]
    parts = {
        "ident": p == c,
        "head_block": p // HD == np.arange(HC * S)[None, :] // S,
        "repeat": p == c % S,
        "causal": np.where((p // S == c // S) & (c <= p), 0.0, MASKED),
        "iota": np.broadcast_to(c, (P, P)),
        "earlier": np.broadcast_to(g % 4 < g // 4, (P, 16)),
        "before": p < c,
        "token": p + P * np.arange(NT)[None, :],
    }
    return np.concatenate([np.asarray(parts[n], np.float32) for n in CONST], axis=1)


def start(k):
    nc, d = k.nc, k.dram
    with nc.Block() as block:
        @block.sync
        def _(sp):
            for g in range(G):
                sp.dma_start(k.x_t[:, :, group(g)], d["x_t"].rearrange("(c p) t -> p c t", p=P)[:, :, group(g)]).then_inc(k.x_loaded[g].sem, 16)
            sp.dma_start(k.consts[:, :], d["consts"]).then_inc(k.consts_loaded.sem, 16)

        @block.gpsimd
        def _(pool):
            for s in k.counts:
                if s.credit:
                    pool.sem_inc(s.sem, s.credit * s.unit)

        @block.vector
        def _(dve):
            dve.memset(k.ones_mean[:, :], 1.0 / D)
            dve.memset(k.ones_row[:, :], 1.0)
            dve.memset(k.ones_h[:, :], 1.0)
            dve.memset(k.eps[:, :], EPS)


def stage_weights(k, ctx, plain, split):
    k.plain, k.split = plain, split
    for n in plain:
        k.w[n] = k.sb(f"w_{n}", [P, k.dram[n].shape[0] // P, k.dram[n].shape[1]], ctx=ctx)
    for n in split:
        shape = [P, k.dram[n].shape[0] // P, k.dram[n].shape[1]]
        k.w[n] = (k.sb(f"wh_{n}", shape, F16, ctx=ctx), k.sb(f"wl_{n}", shape, F16, ctx=ctx))


def layernorm(k):
    nc = k.nc
    ps = k.ps
    with ExitStack() as ctx, nc.Block() as block:
        xc = k.sb("ln_xc", [P, C, T], ctx=ctx)
        sq = k.sb("ln_sq", [P, C, T], ctx=ctx)
        sd = k.sb("ln_sd", [P, T], ctx=ctx)
        raw = [k.sb(f"raw_{n}", [P, k.dram[n].shape[0] // P, k.dram[n].shape[1]], ctx=ctx) for n in k.split]

        @block.sync
        def _(sp):
            for n, t in zip(k.split, raw):
                sp.dma_start(t[:, :, :], k.dram[n].rearrange("(c p) n -> p c n", p=P)).then_inc(k.split_loaded.sem, 16)
            for n in k.plain:
                sp.dma_start(k.w[n][:, :, :], k.dram[n].rearrange("(c p) n -> p c n", p=P)).then_inc(k.plain_loaded.sem, 16)
            sp.wait_ge(k.plain_loaded.sem, k.plain_loaded.at(len(k.plain)))

        @block.tensor
        def _(pe):
            for g in range(G):
                if k.first:
                    pe.wait_ge(k.x_loaded[g].sem, 16)
                for c in range(C):
                    last = pe.matmul(ps[:, g, :], k.ones_mean[:, :], k.x_t[:, c, group(g)], start=(c == 0), stop=(c == C - 1))
                last.then_inc(k.mean_ready.sem, 1)
            for g in range(G):
                pe.wait_ge(k.squared.sem, k.squared.at(g + 1))
                for c in range(C):
                    last = pe.matmul(ps[:, G + g, :], k.ones_mean[:, :], sq[:, c, group(g)], start=(c == 0), stop=(c == C - 1))
                last.then_inc(k.var_ready.sem, 1)

        @block.scalar
        def _(act):
            for g in range(G):
                act.wait_ge(k.centred.sem, k.centred.at(C * (g + 1)))
                act.activation(sq[:, :, group(g)], xc[:, :, group(g)], ACT.Square).then_inc(k.squared.sem, 1)
            for g in range(G):
                act.wait_ge(k.var_ready.sem, k.var_ready.at(g + 1))
                act.activation(sd[:, group(g)], ps[:, G + g, :], ACT.Sqrt, bias=k.eps[:, 0:1]).then_inc(k.std_ready.sem, 1)
            for g in range(G):
                act.wait_ge(k.normed.sem, k.normed.at(g + 1))
                act.activation(k.n_h[:, :, group(g)], xc[:, :, group(g)], ACT.Copy).then_inc(k.high_ready.sem, 1)

        @block.vector
        def _(dve):
            for g in range(G):
                dve.wait_ge(k.mean_ready.sem, k.mean_ready.at(g + 1))
                for c in range(C):
                    dve.tensor_tensor(xc[:, c, group(g)], k.x_t[:, c, group(g)], ps[:, g, :], ALU.subtract).then_inc(k.centred.sem, 1)
            for g in range(G):
                dve.wait_ge(k.std_ready.sem, k.std_ready.at(g + 1))
                dve.reciprocal(sd[:, group(g)], sd[:, group(g)]).then_inc(k.inv_ready.sem, 1)
                dve.wait_ge(k.inv_ready.sem, k.inv_ready.at(g + 1))
                dve.wait_ge(k.squared.sem, k.squared.at(g + 1))
                for c in range(C):
                    last = dve.scalar_tensor_tensor(xc[:, c, group(g)], xc[:, c, group(g)], NS, sd[:, group(g)], ALU.mult, ALU.mult)
                last.then_inc(k.normed.sem, 1)
            if k.first:
                dve.wait_ge(k.consts_loaded.sem, 16)
                dve.tensor_copy(k.ident_h[:, :], k.c["ident"])
                dve.tensor_copy(k.before_h[:, :], k.c["before"])
                dve.tensor_copy(k.ident_bf[:, :], k.c["ident"])
                dve.tensor_copy(k.repeat_bf[:, :], k.c["repeat"][0:S, :])
                dve.tensor_copy(k.causal_bf[:, :], k.c["causal"])

        @block.gpsimd
        def _(pool):
            pool.wait_ge(k.split_loaded.sem, k.split_loaded.at(len(k.split)))
            for n, t in zip(k.split, raw):
                h, l = k.w[n]
                pool.tensor_scalar(h[:, :, :], t[:, :, :], WS, 1.0, ALU.mult, ALU.mult)
                pool.tensor_scalar(t[:, :, :], t[:, :, :], WS, 1.0, ALU.mult, ALU.mult).then_inc(k.split_high.sem, 1)
                pool.wait_ge(k.split_high.sem, k.split_high.next())
                pool.tensor_tensor(l[:, :, :], t[:, :, :], h[:, :, :], ALU.subtract)
            for g in range(G):
                pool.wait_ge(k.high_ready.sem, k.high_ready.at(g + 1))
                pool.tensor_tensor(k.n_l[:, :, group(g)], xc[:, :, group(g)], k.n_h[:, :, group(g)], ALU.subtract)
    for s, n in ((k.mean_ready, G), (k.squared, G), (k.var_ready, G), (k.std_ready, G), (k.inv_ready, G), (k.centred, C * G),
                 (k.normed, G), (k.high_ready, G), (k.split_loaded, len(k.split)), (k.plain_loaded, len(k.plain))):
        s.base += n


def three(w, x):
    return ((w[0], x[0]), (w[0], x[1]), (w[1], x[0]))


def project(k, weight, src, finish_block, n_in=C, n_out=C, rows=P):
    nc, ps = k.nc, k.ps
    pairs = three(weight, src) if isinstance(weight, tuple) else ((weight, src),)
    with nc.Block() as block:
        @block.tensor
        def _(pe):
            for g in range(G):
                for m in range(n_out):
                    products = [(w, x, c) for w, x in pairs for c in range(n_in)]
                    for n, (w, x, c) in enumerate(products):
                        last = pe.matmul(ps[:, g * n_out + m, :], w[:, c, m * P:(m + 1) * P], x[:, c, group(g)],
                                         start=(n == 0), stop=(n == len(products) - 1))
                    last.then_inc(k.projected.sem, 1)
        finish_block(block)
    k.projected.base += G * n_out


def stage_heads_attention(k):
    nc, ps, c_ = k.nc, k.ps, k.c
    with ExitStack() as stage:
        stage_weights(k, stage, ["L0_xattn_wout_t"], ["L0_xattn_wq_t", "L0_xattn_wk_t", "L0_xattn_wv_t"])
        layernorm(k)
        heads_attention(k, stage)


def heads_attention(k, stage):
    nc, ps, c_ = k.nc, k.ps, k.c
    KR = SK - 1
    n = (k.n_h, k.n_l)
    q_t = k.sb("q_t", [P, C, T], ctx=stage)
    o_t = k.sb("o_t", [P, C, T], ctx=stage)
    last_t = k.sb("last_t", [P, C, B], ctx=stage)
    last_s = [k.sb(f"last_s{x}", [P, C, B], F16, ctx=stage) for x in range(2)]
    v_last = k.sb("v_last", [P, C, B], ctx=stage)

    def take_q(block):
        @block.sync
        def _(sp):
            sp.dma_start(last_t[:, :, :], k.dram["ctx_last_t"].rearrange("(c p) b -> p c b", p=P)).then_inc(k.a_last.sem, 16)

        @block.scalar
        def _(act):
            for g in range(G):
                for m in range(C):
                    act.wait_ge(k.projected.sem, k.projected.at(g * C + m + 1))
                    act.activation(q_t[:, m, group(g)], ps[:, g * C + m, :], ACT.Copy, scale=HD ** -0.5 / (WS * NS))

        @block.vector
        def _(dve):
            dve.wait_ge(k.a_last.sem, 16)
            dve.tensor_scalar(last_t[:, :, :], last_t[:, :, :], NS, None, ALU.mult).then_inc(k.a_split.sem, 1)
            dve.wait_ge(k.a_split.sem, 1)
            dve.tensor_copy(last_s[0][:, :, :], last_t[:, :, :]).then_inc(k.a_split.sem, 1)
            dve.wait_ge(k.a_split.sem, 2)
            dve.tensor_tensor(last_s[1][:, :, :], last_t[:, :, :], last_s[0][:, :, :], ALU.subtract)
    project(k, k.w["L0_xattn_wq_t"], n, take_q)

    with ExitStack() as ctx:
        ctx_t = [k.sb(f"ctx_t{p}", [P, C, SK], ctx=ctx) for p in range(2)]
        ctx_c = [k.sb(f"ctx_c{p}", [P, C, KR], ctx=ctx) for p in range(2)]
        ctx_s = [[k.sb(f"ctx_s{p}{x}", [P, C, KR], F16, ctx=ctx) for x in range(2)] for p in range(2)]
        mask_i = [k.sb(f"mask_i{p}", [S, SK], I32, ctx=ctx) for p in range(2)]
        mask_b = [k.sb(f"mask_b{p}", [S, SK], BF16, ctx=ctx) for p in range(2)]
        k_t = [k.sb(f"k_t{p}", [P, C, SK], ctx=ctx) for p in range(2)]
        v = [k.sb(f"v{p}", [P, 2, D], ctx=ctx) for p in range(2)]
        q_blk = [k.sb(f"q_blk{p}", [P, C, HC * S], ctx=ctx) for p in range(2)]
        neg_max = k.sb("neg_max", [P, 2, 4], ctx=ctx)
        sums = k.sb("sums", [P, 2, 4], ctx=ctx)
        inv = k.sb("inv", [P, 2, 4], ctx=ctx)
        probs = [k.sb(f"probs{p}", [P, 4, SK], ctx=ctx) for p in range(2)]
        pn = k.sb("pn", [P, 4, KR], ctx=ctx)
        p_t = k.sb("p_t", [P, 2, 512], ctx=ctx)
        o_own = k.sb("o_own", [P, C, HC, S], ctx=ctx)
        o_sum = k.sb("o_sum", [P, C, S], ctx=ctx)
        KB, VB, TB, OB, SB = 0, 1, 2, 3, 4
        wk, wv = k.w["L0_xattn_wk_t"], k.w["L0_xattn_wv_t"]

        with nc.Block() as block:
            @block.sync
            def _(sp):
                def fetch(i, p):
                    b = 2 * i + p
                    sp.wait_ge(k.a_centred.sem, k.a_centred.at(b - 1))
                    sp.dma_start(ctx_t[p][:, :, :], k.dram["ctx_t"][bass.ds(b, 1), :, :].rearrange("o (c p) n -> p (o c) n", p=P)).then_inc(k.a_ctx[p].sem, 16)
                    sp.wait_ge(k.a_maskb.sem, k.a_maskb.at(b - 1))
                    sp.dma_start(mask_i[p][:, :], k.dram["mask"][bass.ds(b, 1), :, :].rearrange("o s n -> (o s) n")).then_inc(k.a_mask[p].sem, 16)
                with sp.Fori(0, B // 2) as i:
                    fetch(i, 0)
                    fetch(i, 1)

            @block.tensor
            def _(pe):
                for m in range(C):
                    products = [(w, x, c) for w, x in three(wv, last_s) for c in range(C)]
                    for n_, (w, x, c) in enumerate(products):
                        last = pe.matmul(ps[:, SB, m * B:(m + 1) * B], w[:, c, m * P:(m + 1) * P], x[:, c, :], start=(n_ == 0), stop=(n_ == len(products) - 1))
                last.then_inc(k.a_vlast.sem, 1)

                def keys_values(i, p):
                    b = 2 * i + p
                    pe.wait_ge(k.a_low.sem, k.a_low.at(b + 1))
                    pe.wait_ge(k.a_kcopied.sem, k.a_kcopied.at(b))
                    for m in range(C):
                        products = [(w, x, c) for w, x in three(wk, ctx_s[p]) for c in range(C)]
                        for n_, (w, x, c) in enumerate(products):
                            last = pe.matmul(ps[:, KB, m * KR:(m + 1) * KR], w[:, c, m * P:(m + 1) * P], x[:, c, :], start=(n_ == 0), stop=(n_ == len(products) - 1))
                    last.then_inc(k.a_kproj.sem, 1)
                    pe.wait_ge(k.a_vcopied.sem, k.a_vcopied.at(b))
                    for r in range(2):
                        products = [(w, x, c) for w, x in three(wv, ctx_s[p]) for c in range(C)]
                        for n_, (w, x, c) in enumerate(products):
                            last = pe.matmul(ps[:, VB, r * D:(r + 1) * D], x[:, c, r * P:(r + 1) * P], w[:, c, :], start=(n_ == 0), stop=(n_ == len(products) - 1))
                    last.then_inc(k.a_keys_done.sem, 1)

                def scores(i, p):
                    b = 2 * i + p
                    pe.wait_ge(k.a_kcopied.sem, k.a_kcopied.at(b + 1))
                    pe.wait_ge(k.a_qblk.sem, k.a_qblk.at(b + 1))
                    pe.wait_ge(k.a_maskb.sem, k.a_maskb.at(b + 1))
                    pe.wait_ge(k.a_exp.sem, k.a_exp.at(4 * b))
                    pe.wait_ge(k.a_ptcopied.sem, k.a_ptcopied.at(2 * b))
                    for j in range(4):
                        pe.matmul(ps[:, SB + j, 0:SK], k.repeat_bf[:, :], mask_b[p][:, :], start=True, stop=False)
                        last = pe.matmul(ps[:, SB + j, 0:SK], q_blk[p][:, j // 2, (j % 2) * P:(j % 2 + 1) * P], k_t[p][:, j // 2, :], start=False, stop=True)
                    last.then_inc(k.a_scored.sem, 1)

                def weigh(i, p):
                    b = 2 * i + p
                    pe.wait_ge(k.a_normed.sem, k.a_normed.at(4 * (b + 1)))
                    for r in range(2):
                        for j in range(4):
                            last = pe.transpose(ps[:, (SB, TB)[r], j * P:(j + 1) * P], pn[:, j, r * P:(r + 1) * P], c_["ident"])
                        last.then_inc(k.a_pt.sem, 1)
                    pe.wait_ge(k.a_own.sem, k.a_own.at(b))
                    pe.wait_ge(k.a_vcopied.sem, k.a_vcopied.at(b + 1))
                    for m in range(C):
                        for r in range(2):
                            pe.wait_ge(k.a_ptcopied.sem, k.a_ptcopied.at(2 * b + r + 1))
                            last = pe.matmul(ps[:, OB, m * D:(m + 1) * D], v[p][:, r, m * P:(m + 1) * P], p_t[:, r, m * D:(m + 1) * D], start=(r == 0), stop=(r == 1))
                    last.then_inc(k.a_out.sem, 1)

                pe.wait_ge(k.a_vtaken.sem, 1)
                keys_values(0, 0)
                with pe.Fori(0, B // 2 - 1) as i:
                    scores(i, 0)
                    keys_values(i, 1)
                    weigh(i, 0)
                    scores(i, 1)
                    keys_values(i + 1, 0)
                    weigh(i, 1)
                i = B // 2 - 1
                scores(i, 0)
                keys_values(i, 1)
                weigh(i, 0)
                scores(i, 1)
                weigh(i, 1)

            @block.scalar
            def _(act):
                act.preload_act_table(ACT.Exp)

                def high(i, p):
                    b = 2 * i + p
                    act.wait_ge(k.a_centred.sem, k.a_centred.at(b + 1))
                    act.wait_ge(k.a_keys_done.sem, k.a_keys_done.at(b - 1))
                    act.activation(ctx_s[p][0][:, :, :], ctx_c[p][:, :, :], ACT.Copy).then_inc(k.a_high.sem, 1)

                def take(i, p):
                    b = 2 * i + p
                    act.wait_ge(k.a_kproj.sem, k.a_kproj.at(b + 1))
                    act.wait_ge(k.a_scored.sem, k.a_scored.at(b - 1))
                    act.activation(k_t[p][:, :, 0:KR], ps[:, KB, :].rearrange("p (c n) -> p c n", c=C), ACT.Copy, scale=1 / (WS * NS)).then_inc(k.a_kcopied.sem, 1)
                    act.wait_ge(k.a_keys_done.sem, k.a_keys_done.at(b + 1))
                    act.wait_ge(k.a_out.sem, k.a_out.at(b - 1))
                    act.activation(v[p][:, :, :].rearrange("p r n -> p (r n)"), ps[:, VB, :], ACT.Copy, scale=1 / (WS * NS)).then_inc(k.a_vcopied.sem, 1)

                def softmax(i, p):
                    b = 2 * i + p
                    act.wait_ge(k.a_max.sem, k.a_max.at(b + 1))
                    act.wait_ge(k.a_normed.sem, k.a_normed.at(4 * (b - 1)))
                    for j in range(4):
                        act.activation(probs[p][:, j, :], ps[:, SB + j, 0:SK], ACT.Exp, bias=neg_max[:, p, j:j + 1], accum_out=sums[:, p, j:j + 1]).then_inc(k.a_exp.sem, 1)

                high(0, 0)
                high(0, 1)
                take(0, 0)
                with act.Fori(0, B // 2 - 1) as i:
                    softmax(i, 0)
                    high(i + 1, 0)
                    take(i, 1)
                    softmax(i, 1)
                    high(i + 1, 1)
                    take(i + 1, 0)
                i = B // 2 - 1
                softmax(i, 0)
                take(i, 1)
                softmax(i, 1)

            @block.gpsimd
            def _(pool):
                def queries(i, p):
                    b = 2 * i + p
                    pool.wait_ge(k.a_scored.sem, k.a_scored.at(b - 1))
                    for c in range(C):
                        q = q_t[:, c, bass.ds(b * S, S)].unsqueeze(1).broadcast_to([P, HC, S])
                        last = pool.tensor_tensor(q_blk[p][:, c, :].rearrange("p (h q) -> p h q", h=HC), q, c_["head_block"].rearrange("p (h q) -> p h q", h=HC), ALU.mult)
                    last.then_inc(k.a_qblk.sem, 1)

                def low(i, p):
                    b = 2 * i + p
                    pool.wait_ge(k.a_high.sem, k.a_high.at(b + 1))
                    pool.tensor_tensor(ctx_s[p][1][:, :, :], ctx_c[p][:, :, :], ctx_s[p][0][:, :, :], ALU.subtract).then_inc(k.a_low.sem, 1)

                low(0, 0)
                queries(0, 0)
                with pool.Fori(0, B // 2 - 1) as i:
                    low(i, 1)
                    queries(i, 1)
                    low(i + 1, 0)
                    queries(i + 1, 0)
                low(B // 2 - 1, 1)
                queries(B // 2 - 1, 1)

            @block.vector
            def _(dve):
                for p in range(2):
                    dve.memset(k_t[p][:, :, KR:SK], 0.0)
                dve.wait_ge(k.a_vlast.sem, 1)
                dve.tensor_scalar(v_last[:, :, :].rearrange("p c b -> p (c b)"), ps[:, SB, 0:C * B], 1 / (WS * NS), None, ALU.mult).then_inc(k.a_vtaken.sem, 1)

                def prepare(i, p):
                    b = 2 * i + p
                    dve.wait_ge(k.a_ctx[p].sem, k.a_ctx[p].at(i + 1))
                    dve.wait_ge(k.a_low.sem, k.a_low.at(b - 1))
                    for c in range(C):
                        last = dve.tensor_scalar(ctx_c[p][:, c, :], ctx_t[p][:, c, 0:KR], ctx_t[p][:, c, KR:SK], NS, ALU.subtract, ALU.mult)
                    last.then_inc(k.a_centred.sem, 1)
                    dve.wait_ge(k.a_scored.sem, k.a_scored.at(b - 1))
                    dve.wait_ge(k.a_mask[p].sem, k.a_mask[p].at(i + 1))
                    dve.tensor_scalar(mask_b[p][:, :], mask_i[p][:, :], 1.0, MASKED, ALU.is_equal, ALU.mult).then_inc(k.a_maskb.sem, 1)

                def softmax(i, p):
                    b = 2 * i + p
                    dve.wait_ge(k.a_scored.sem, k.a_scored.at(b + 1))
                    dve.tensor_reduce(neg_max[:, p, :], ps[:, SB:SB + 4, 0:SK], AX.X, ALU.max, negate=True).then_inc(k.a_max.sem, 1)

                def normalise(i, p):
                    b = 2 * i + p
                    dve.wait_ge(k.a_exp.sem, k.a_exp.at(4 * (b + 1)))
                    dve.reciprocal(inv[:, p, :], sums[:, p, :]).then_inc(k.a_inv.sem, 1)
                    dve.wait_ge(k.a_inv.sem, k.a_inv.at(b + 1))
                    dve.wait_ge(k.a_pt.sem, k.a_pt.at(2 * b))
                    for j in range(4):
                        dve.tensor_scalar(pn[:, j, :], probs[p][:, j, 0:KR], inv[:, p, j:j + 1], None, ALU.mult).then_inc(k.a_normed.sem, 1)

                def outputs(i, p):
                    b = 2 * i + p
                    dve.wait_ge(k.a_out.sem, k.a_out.at(b))
                    for r in range(2):
                        dve.wait_ge(k.a_pt.sem, k.a_pt.at(2 * b + r + 1))
                        dve.tensor_copy(p_t[:, r, :], ps[:, (SB, TB)[r], :]).then_inc(k.a_ptcopied.sem, 1)

                def own(i, p):
                    b = 2 * i + p
                    dve.wait_ge(k.a_out.sem, k.a_out.at(b + 1))
                    for c in range(C):
                        last = dve.tensor_tensor(o_own[:, c, :, :], ps[:, OB, c * D:(c + 1) * D].rearrange("p (h q) -> p h q", h=HC),
                                                 c_["head_block"].rearrange("p (h q) -> p h q", h=HC), ALU.mult)
                    last.then_inc(k.a_own.sem, 1)
                    dve.wait_ge(k.a_own.sem, k.a_own.at(b + 1))
                    dve.tensor_reduce(o_sum[:, :, :], o_own[:, :, :, :].rearrange("p c h q -> p c q h"), AX.X, ALU.add).then_inc(k.a_osum.sem, 1)
                    dve.wait_ge(k.a_osum.sem, k.a_osum.at(b + 1))
                    dve.tensor_tensor(o_t[:, :, bass.ds(b * S, S)], o_sum[:, :, :], v_last[:, :, bass.ds(b, 1)].broadcast_to([P, C, S]), ALU.add)

                prepare(0, 0)
                prepare(0, 1)
                with dve.Fori(0, B // 2 - 1) as i:
                    for p in range(2):
                        softmax(i, p)
                        prepare(i + 1, p)
                        normalise(i, p)
                        outputs(i, p)
                        own(i, p)
                i = B // 2 - 1
                for p in range(2):
                    softmax(i, p)
                    normalise(i, p)
                    outputs(i, p)
                    own(i, p)

    def add_out(block):
        @block.vector
        def _(dve):
            for g in range(G):
                for m in range(C):
                    dve.wait_ge(k.projected.sem, k.projected.at(g * C + m + 1))
                    dve.tensor_tensor(k.x_t[:, m, group(g)], k.x_t[:, m, group(g)], ps[:, g * C + m, :], ALU.add)
    project(k, k.w["L0_xattn_wout_t"], o_t, add_out)


def stage_recurrence(k):
    nc, ps = k.nc, k.ps
    with ExitStack() as ctx:
        stage_weights(k, ctx, ["L0_attn_W2", "L0_attn_b1", "L0_attn_b2", "L0_attn_init_h"], ["L0_attn_W1"])
        layernorm(k)
        w1, w2 = k.w["L0_attn_W1"], k.w["L0_attn_W2"]
        bias1, bias2, init = k.w["L0_attn_b1"], k.w["L0_attn_b2"], k.w["L0_attn_init_h"]
        bias_half = k.sb("bias_half", [P, J], ctx=ctx)
        g_init = k.sb("g_init", [P, 2, J], ctx=ctx)
        sig = [k.sb(f"sig{p}", [P, 3, TG], ctx=ctx) for p in range(2)]
        gate = [k.sb(f"gate{p}", [P, 2, TG], ctx=ctx) for p in range(2)]
        inv = [k.sb(f"ginv{p}", [P, TG], ctx=ctx) for p in range(2)]
        val = [k.sb(f"val{p}", [P, TG], ctx=ctx) for p in range(2)]
        hid = k.sb("hid", [P, J, TG], ctx=ctx)
        with nc.Block() as block:
            @block.tensor
            def _(pe):
                with pe.Fori(0, G) as g:
                    for j in range(J):
                        u = J * g + j
                        pe.wait_ge(k.r_sig.sem, k.r_sig.at(u - 1))
                        for part in range(3):
                            products = [(w, x, c) for w, x in three(w1, (k.n_h, k.n_l)) for c in range(C)]
                            for n, (w, x, c) in enumerate(products):
                                last = pe.matmul(ps[:, 3 * (j % 2) + part, :], w[:, c, part * DIN + j * P:part * DIN + (j + 1) * P],
                                                 x[:, c, group(g)], start=(n == 0), stop=(n == len(products) - 1))
                        last.then_inc(k.r_proj.sem, 1)
                    pe.wait_ge(k.r_added.sem, k.r_added.at(g))
                    for m in range(C):
                        for j in range(J):
                            pe.wait_ge(k.r_scan.sem, k.r_scan.at(J * g + j + 1))
                            last = pe.matmul(ps[:, 6 + m, :], w2[:, j, m * P:(m + 1) * P], hid[:, j, :], start=(j == 0), stop=(j == J - 1))
                    last.then_inc(k.r_out.sem, 1)

            @block.scalar
            def _(act):
                act.activation(g_init[:, 0, :], init[:, 0, :], ACT.Sigmoid).then_inc(k.r_init.sem, 1)
                act.wait_ge(k.r_init.sem, 2)
                with act.Fori(0, G) as g:
                    for j in range(J):
                        u = J * g + j
                        act.wait_ge(k.r_proj.sem, k.r_proj.at(u + 1))
                        act.wait_ge(k.r_scan.sem, k.r_scan.at(u - 1))
                        for part in range(3):
                            act.activation(sig[j % 2][:, part, :], ps[:, 3 * (j % 2) + part, :], ACT.Sigmoid, scale=1 / (WS * NS), bias=bias1[:, 0, part * J + j:part * J + j + 1])
                        act.activation(val[j % 2][:, :], ps[:, 3 * (j % 2), :], ACT.Identity, scale=1 / (WS * NS), bias=bias_half[:, j:j + 1]).then_inc(k.r_sig.sem, 1)

            @block.vector
            def _(dve):
                dve.tensor_scalar(bias_half[:, :], bias1[:, 0, 0:J], 0.5, None, ALU.add).then_inc(k.r_init.sem, 1)
                dve.wait_ge(k.r_init.sem, k.r_init.at(2))
                dve.scalar_tensor_tensor(g_init[:, 1, :], init[:, 0, :], 0.5, g_init[:, 0, :], ALU.add, ALU.max).then_inc(k.r_init.sem, 1)
                with dve.Fori(0, G) as g:
                    for j in range(J):
                        u = J * g + j
                        p = j % 2
                        sg, sf, si = (sig[p][:, n, :] for n in range(3))
                        dve.wait_ge(k.r_sig.sem, k.r_sig.at(u + 1))
                        dve.tensor_scalar(gate[p][:, 0, :], sf, TINY, None, ALU.max).then_inc(k.r_floor.sem, 1)
                        dve.tensor_tensor(val[p][:, :], val[p][:, :], sg, ALU.max)
                        dve.wait_ge(k.r_floor.sem, k.r_floor.at(u + 1))
                        dve.scalar_tensor_tensor(gate[p][:, 1, :], si, TINY, gate[p][:, 0, :], ALU.max, ALU.add).then_inc(k.r_sum.sem, 1)
                        dve.wait_ge(k.r_sum.sem, k.r_sum.at(u + 1))
                        dve.reciprocal(inv[p][:, :], gate[p][:, 1, :]).then_inc(k.r_inv.sem, 1)
                        dve.wait_ge(k.r_inv.sem, k.r_inv.at(u + 1))
                        dve.scalar_tensor_tensor(gate[p][:, 1, :], si, TINY, inv[p][:, :], ALU.max, ALU.mult)
                        dve.tensor_tensor(gate[p][:, 0, :], gate[p][:, 0, :], inv[p][:, :], ALU.mult).then_inc(k.r_gates.sem, 1)
                        dve.wait_ge(k.r_gates.sem, k.r_gates.at(u + 1))
                        dve.tensor_tensor(val[p][:, :], val[p][:, :], gate[p][:, 1, :], ALU.mult).then_inc(k.r_valued.sem, 1)
                        dve.wait_ge(k.r_valued.sem, k.r_valued.at(u + 1))
                        first_val, first_coef = val[p][:, 0:TG:S], gate[p][:, 0, 0:TG:S]
                        dve.scalar_tensor_tensor(first_val, first_coef, g_init[:, 1, j:j + 1], first_val, ALU.mult, ALU.add).then_inc(k.r_first.sem, 1)
                        dve.wait_ge(k.r_first.sem, k.r_first.at(2 * u + 1))
                        dve.tensor_scalar(first_coef, first_coef, 0.0, None, ALU.mult).then_inc(k.r_first.sem, 1)
                        dve.wait_ge(k.r_first.sem, k.r_first.at(2 * u + 2))
                        dve.wait_ge(k.r_out.sem, k.r_out.at(g))
                        dve.tensor_tensor_scan(hid[:, j, :], gate[p][:, 0, :], val[p][:, :], 0.0, ALU.mult, ALU.add).then_inc(k.r_scan.sem, 1)
                    dve.wait_ge(k.r_out.sem, k.r_out.at(g + 1))
                    for m in range(C):
                        x = k.x_t[:, m, group(g)]
                        last = dve.scalar_tensor_tensor(x, ps[:, 6 + m, :], bias2[:, 0, m:m + 1], x, ALU.add, ALU.add)
                    last.then_inc(k.r_added.sem, 1)


def top8(k, dve, values, v8, i8, i8f):
    for t in range(NT):
        last = dve.max(v8[:, t, :], values[:, t, :])
    last.then_inc(k.m_chain.sem, 1)
    dve.wait_ge(k.m_chain.sem, k.m_chain.next())
    for t in range(NT):
        last = dve.max_index(i8[:, t, :], v8[:, t, :], values[:, t, :])
    last.then_inc(k.m_chain.sem, 1)
    dve.wait_ge(k.m_chain.sem, k.m_chain.next())
    dve.tensor_copy(i8f[:, :, :], i8[:, :, :]).then_inc(k.m_chain.sem, 1)
    dve.wait_ge(k.m_chain.sem, k.m_chain.next())


class Mixture:

    def __init__(self, n, experts, chosen, blocks, width, rows, hidden, gated, shared_weight):
        self.n, self.E, self.K, self.blocks, self.width = n, experts, chosen, blocks, width
        self.rows, self.hidden, self.gated, self.shared_weight = rows, hidden, gated, shared_weight
        self.tiles = T * chosen // P + experts - 1
        self.feeds = blocks * experts // NT


MIX0 = Mixture(0, E0, K0, 4, F0, P, F0, False, 0.1)
MIX1 = Mixture(1, E1, K1, 1, 2 * C * I1 + 2 * D, IH, 2 * P, True, 1.0)
MAX_TILES = max(MIX0.tiles, MIX1.tiles)
FC = F0 // P


class Routing:

    def __init__(self, k, mix, ctx):
        self.w = k.sb("r_w", [P, mix.K, NT], ctx=ctx)
        self.choice = k.sb("r_choice", [P, NT, 8], ctx=ctx)
        self.slot = k.sb("r_slot", [P, NT, mix.K], I32, ctx=ctx)
        self.table = k.sb("r_table", [P, mix.tiles], ctx=ctx)
        self.expert = k.sb("r_expert", [P, mix.tiles], I32, ctx=ctx)


def route(k, mix, wg, wh, wl, scores, choose, r):
    nc, ps, c_ = k.nc, k.ps, k.c
    E, K, NTL = mix.E, mix.K, mix.tiles
    LB, PB, SB = 7, 6, 5
    with ExitStack() as ctx, nc.Block() as block:
        hot = k.sb("hot", [P, K, E, NT], ctx=ctx)
        any_h = k.sb("any_h", [P, E, NT], F16, ctx=ctx)
        total = k.sb("total", [P, E, NT], ctx=ctx)
        later = k.sb("later", [P, E, NT], ctx=ctx)
        upto = k.sb("upto", [P, E, NT], ctx=ctx)
        place = k.sb("place", [P, E, NT], ctx=ctx)
        tmp = k.sb("tmp", [P, E, NT], ctx=ctx)
        need_i = k.sb("need_i", [P, E], I32, ctx=ctx)
        need = k.sb("need", [P, E], ctx=ctx)
        ones_e = k.sb("ones_e", [P, E], ctx=ctx)
        ends = k.sb("ends", [P, E], ctx=ctx)
        begins = k.sb("begins", [P, E], ctx=ctx)
        slot_f = k.sb("slot_f", [P, K, NT], ctx=ctx)
        lo_i = k.sb("lo_i", [P, K, NT], I32, ctx=ctx)
        hi_i = k.sb("hi_i", [P, K, NT], I32, ctx=ctx)
        lo_f = k.sb("lo_f", [P, K, NT], ctx=ctx)
        hi_f = k.sb("hi_f", [P, K, NT], ctx=ctx)
        ends_le = k.sb("ends_le", [P, NTL, E], ctx=ctx)
        exp_f = k.sb("exp_f", [P, NTL], ctx=ctx)
        hot_lo = [k.sb(f"hot_lo{p}", [P, P], F16, ctx=ctx) for p in range(2)]
        hot_hi = [k.sb(f"hot_hi{p}", [P, NTL], F16, ctx=ctx) for p in range(2)]
        iota_h = k.sb("iota_h", [P, P], F16, ctx=ctx)
        raw = [k.sb(f"shared_raw{p}", [P, mix.width], ctx=ctx) for p in range(2)]
        row_sb = [k.sb(f"row_sb{p}", [P, 2 * D], F16, ctx=ctx) for p in range(2)]

        @block.tensor
        def _(pe):
            for t in range(NT):
                products = [(w, x, c) for w, x in three(wg, (k.n_h, k.n_l)) for c in range(C)]
                for n, (w, x, c) in enumerate(products):
                    last = pe.matmul(ps[:, LB, t * E:(t + 1) * E], x[:, c, t * P:(t + 1) * P], w[:, c, :], start=(n == 0), stop=(n == len(products) - 1))
            last.then_inc(k.m_logits.sem, 1)
            for t in range(NT):
                pe.wait_ge(k.m_rowcopied.sem, k.m_rowcopied.at(max(t - 1, 0)))
                row = ps[:, t % 2, 0:D].bitcast(F16)
                for x, n in enumerate((k.n_h, k.n_l)):
                    for c in range(C):
                        last = pe.transpose(row[:, (x * C + c) * P:(x * C + c + 1) * P], n[:, c, t * P:(t + 1) * P], k.ident_h[:, :])
                last.then_inc(k.m_rowt.sem, 1)
            pe.wait_ge(k.m_counted.sem, k.m_counted.at(1))
            pe.matmul(ps[:, PB, 0:E * NT], k.before_h[:, :], any_h[:, :, :].rearrange("p e t -> p (e t)"), start=True, stop=True)
            pe.matmul(ps[:, PB, E * NT:2 * E * NT], k.ones_h[:, :], any_h[:, :, :].rearrange("p e t -> p (e t)"), start=True, stop=True).then_inc(k.m_prefixed.sem, 1)

            def add_to_table(u, p, first, final):
                pe.wait_ge(k.m_onehot.sem, k.m_onehot.at(u + 1))
                pe.matmul(ps[:, SB, 0:NTL], hot_lo[p][:, :], hot_hi[p][:, :], start=first, stop=final).then_inc(k.m_placed.sem, 1)
            for kk in range(K):
                add_to_table(kk, kk % 2, kk == 0, False)
            with pe.Fori(1, NT - 1) as t:
                for kk in range(K):
                    add_to_table(t * K + kk, kk % 2, False, False)
            for kk in range(K):
                add_to_table((NT - 1) * K + kk, kk % 2, False, kk == K - 1)

        @block.scalar
        def _(act):
            scores(act)
            for t in range(NT):
                act.wait_ge(k.m_rowt.sem, k.m_rowt.at(t + 1))
                if t >= 2:
                    act.wait_ge(k.m_rows[t % 2].sem, k.m_rows[t % 2].at(t // 2))
                act.activation(row_sb[t % 2][:, :], ps[:, t % 2, 0:D].bitcast(F16), ACT.Copy).then_inc(k.m_rowcopied.sem, 1)

        @block.sync
        def _(sp):
            first = mix.E * mix.blocks
            for q in range(mix.blocks):
                sp.wait_ge(k.t_wlow.sem, k.t_wlow.at(max(q - 1, 0)))
                sp.dma_start(raw[q % 2][:, :], k.dram[f"m{mix.n}_w"][first + q, :, :]).then_inc(k.t_raw[q % 2].sem, 16)
            for t in range(NT):
                sp.wait_ge(k.m_rowcopied.sem, k.m_rowcopied.at(t + 1))
                sp.dma_start(k.n_rows[t * P:(t + 1) * P, :], row_sb[t % 2][:, :]).then_inc(k.m_rows[t % 2].sem, 16)
            for p in range(2):
                sp.wait_ge(k.m_rows[p].sem, k.m_rows[p].at(NT // 2))

        @block.gpsimd
        def _(pool):
            first = mix.E * mix.blocks
            for q in range(mix.blocks):
                pool.wait_ge(k.t_raw[q % 2].sem, k.t_raw[q % 2].at(q // 2 + 1))
                pool.tensor_scalar(wh[:, first + q, :], raw[q % 2][:, :], WS, 1.0, ALU.mult, ALU.mult)
                pool.tensor_scalar(raw[q % 2][:, :], raw[q % 2][:, :], WS, 1.0, ALU.mult, ALU.mult).then_inc(k.t_cast.sem, 1)
                pool.wait_ge(k.t_cast.sem, k.t_cast.at(q + 1))
                pool.tensor_tensor(wl[:, first + q, :], raw[q % 2][:, :], wh[:, first + q, :], ALU.subtract).then_inc(k.t_wlow.sem, 1)

        @block.vector
        def _(dve):
            dve.memset(ones_e[:, :], 1.0)
            dve.memset(later[:, :, 1:NT], 1.0)
            dve.memset(later[:, :, 0:1], 0.0)
            dve.tensor_copy(iota_h[:, :], c_["iota"])
            choose(dve)
            iota = c_["iota"][:, 0:E].unsqueeze(2).broadcast_to([P, E, NT])
            for kk in range(K):
                last = dve.tensor_tensor(hot[:, kk, :, :], iota, r.choice[:, :, kk].unsqueeze(1).broadcast_to([P, E, NT]), ALU.is_equal)
            last.then_inc(k.m_chain.sem, 1)
            dve.wait_ge(k.m_chain.sem, k.m_chain.next())
            dve.tensor_tensor(tmp[:, :, :], hot[:, 0, :, :], hot[:, 1, :, :], ALU.add).then_inc(k.m_chain.sem, 1)
            dve.wait_ge(k.m_chain.sem, k.m_chain.next())
            for kk in range(2, K):
                dve.tensor_tensor(tmp[:, :, :], tmp[:, :, :], hot[:, kk, :, :], ALU.add).then_inc(k.m_chain.sem, 1)
                dve.wait_ge(k.m_chain.sem, k.m_chain.next())
            dve.tensor_copy(any_h[:, :, :], tmp[:, :, :]).then_inc(k.m_counted.sem, 1)
            dve.wait_ge(k.m_prefixed.sem, k.m_prefixed.at(1))
            dve.tensor_copy(total[:, :, :].rearrange("p e t -> p (e t)"), ps[:, PB, E * NT:2 * E * NT]).then_inc(k.m_chain.sem, 1)
            dve.wait_ge(k.m_chain.sem, k.m_chain.next())
            dve.tensor_tensor_scan(upto[:, :, :].rearrange("p e t -> p (e t)"), later[:, :, :].rearrange("p e t -> p (e t)"),
                                   total[:, :, :].rearrange("p e t -> p (e t)"), 0.0, ALU.mult, ALU.add).then_inc(k.m_chain.sem, 1)
            dve.wait_ge(k.m_chain.sem, k.m_chain.next())
            dve.tensor_scalar(need_i[:, :], upto[:, :, NT - 1], float(P - 1), None, ALU.add).then_inc(k.m_chain.sem, 1)
            dve.tensor_tensor(tmp[:, :, :], upto[:, :, :], total[:, :, :], ALU.subtract)
            dve.wait_ge(k.m_chain.sem, k.m_chain.next())
            dve.tensor_scalar(need_i[:, :], need_i[:, :], 7, None, ALU.arith_shift_right).then_inc(k.m_chain.sem, 1)
            dve.wait_ge(k.m_chain.sem, k.m_chain.next())
            dve.tensor_copy(need[:, :], need_i[:, :]).then_inc(k.m_chain.sem, 1)
            dve.wait_ge(k.m_chain.sem, k.m_chain.next())
            dve.tensor_tensor_scan(ends[:, :], ones_e[:, :], need[:, :], 0.0, ALU.mult, ALU.add).then_inc(k.m_chain.sem, 1)
            dve.wait_ge(k.m_chain.sem, k.m_chain.next())
            dve.tensor_tensor(begins[:, :], ends[:, :], need[:, :], ALU.subtract)
            tile = c_["iota"][:, 0:NTL].unsqueeze(2).broadcast_to([P, NTL, E])
            dve.tensor_tensor(ends_le[:, :, :], ends[:, :].unsqueeze(1).broadcast_to([P, NTL, E]), tile, ALU.is_le)
            dve.tensor_tensor(place[:, :, :].rearrange("p e t -> p (e t)"), tmp[:, :, :].rearrange("p e t -> p (e t)"), ps[:, PB, 0:E * NT], ALU.add).then_inc(k.m_chain.sem, 1)
            dve.wait_ge(k.m_chain.sem, k.m_chain.next())
            dve.tensor_reduce(exp_f[:, :], ends_le[:, :, :], AX.X, ALU.add)
            dve.scalar_tensor_tensor(place[:, :, :], begins[:, :].unsqueeze(2).broadcast_to([P, E, NT]), float(P), place[:, :, :], ALU.mult, ALU.add).then_inc(k.m_chain.sem, 1)
            dve.wait_ge(k.m_chain.sem, k.m_chain.next())
            dve.tensor_scalar(r.expert[:, :], exp_f[:, :], float(E - 1), None, ALU.min)
            for kk in range(K):
                dve.tensor_tensor(hot[:, kk, :, :], hot[:, kk, :, :], place[:, :, :], ALU.mult).then_inc(k.m_chain.sem, 1)
                dve.wait_ge(k.m_chain.sem, k.m_chain.next())
                last = dve.tensor_reduce(slot_f[:, kk, :], hot[:, kk, :, :].rearrange("p e t -> p t e"), AX.X, ALU.add)
            last.then_inc(k.m_chain.sem, 1)
            dve.wait_ge(k.m_chain.sem, k.m_chain.next())
            dve.tensor_copy(r.slot[:, :, :].rearrange("p t k -> p k t"), slot_f[:, :, :]).then_inc(k.m_chain.sem, 1)
            dve.wait_ge(k.m_chain.sem, k.m_chain.next())
            dve.tensor_scalar(lo_i[:, :, :], r.slot[:, :, :].rearrange("p t k -> p k t"), P - 1, None, ALU.bitwise_and)
            dve.tensor_scalar(hi_i[:, :, :], r.slot[:, :, :].rearrange("p t k -> p k t"), 7, None, ALU.arith_shift_right).then_inc(k.m_chain.sem, 1)
            dve.wait_ge(k.m_chain.sem, k.m_chain.next())
            dve.tensor_copy(lo_f[:, :, :], lo_i[:, :, :])
            dve.tensor_copy(hi_f[:, :, :], hi_i[:, :, :]).then_inc(k.m_chain.sem, 1)
            dve.wait_ge(k.m_chain.sem, k.m_chain.next())
            with dve.Fori(0, NT) as t:
                for kk in range(K):
                    u, p = t * K + kk, kk % 2
                    dve.wait_ge(k.m_placed.sem, k.m_placed.at(u - 1))
                    dve.tensor_scalar(hot_lo[p][:, :], iota_h[:, :], lo_f[:, kk, bass.ds(t, 1)], c_["token"][:, bass.ds(t, 1)], ALU.is_equal, ALU.mult)
                    dve.tensor_scalar(hot_hi[p][:, :], iota_h[:, 0:NTL], hi_f[:, kk, bass.ds(t, 1)], None, ALU.is_equal).then_inc(k.m_onehot.sem, 1)
            dve.wait_ge(k.m_placed.sem, k.m_placed.at(NT * K))
            dve.tensor_copy(r.table[:, :], ps[:, SB, 0:NTL])
    for s, n in ((k.m_logits, 1), (k.m_rowt, NT), (k.m_rowcopied, NT), (k.m_rows[0], NT // 2), (k.m_rows[1], NT // 2), (k.m_counted, 1),
                 (k.m_prefixed, 1), (k.m_onehot, NT * K), (k.m_placed, NT * K), (k.m_shift, 1), (k.m_expd, 1), (k.t_cast, mix.blocks),
                 (k.t_wlow, mix.blocks), (k.t_raw[0], (mix.blocks + 1) // 2), (k.t_raw[1], mix.blocks // 2)):
        s.base += n


def tiles(k, mix, wh, wl, up, activate, down, r=None):
    nc, ps = k.nc, k.ps
    shared = r is None
    N = NT if shared else mix.tiles
    first_row = mix.tiles * P if shared else 0
    R, F = mix.rows, mix.feeds
    UB, YB, XB = 0, 4, 6
    with ExitStack() as ctx, nc.Block() as block:
        name = "shared" if shared else "routed"
        h32 = [k.sb(f"{name}_h{p}", [P, mix.hidden], ctx=ctx) for p in range(2)]
        hs = tuple(k.sb(f"{name}_hs{x}", [P, mix.hidden], F16, ctx=ctx) for x in range(2))
        y = [k.sb(f"{name}_y{p}", [P, D], ctx=ctx) for p in range(2)]
        if shared:
            raw = [k.sb(f"raw{p}", [P, mix.width], ctx=ctx) for p in range(2)]
        else:
            rows = [k.sb(f"rows{p}", [P, 2 * D], F16, ctx=ctx) for p in range(2)]
            x_s = [k.sb(f"x_s{p}", [P, 2, C, P], F16, ctx=ctx) for p in range(2)]
            idx = [k.sb(f"row_i{p}", [P, 1], I32, ctx=ctx) for p in range(2)]

        def source(s, p):
            if shared:
                return tuple(n[:, :, bass.ds(s * P, P)] for n in (k.n_h, k.n_l))
            return tuple(x_s[p][:, x, :, :] for x in range(2))

        def expert(eng, s):
            return mix.E if shared else eng.value_load(r.expert[0:1, bass.ds(s, 1)], min_val=0, max_val=mix.E - 1)

        def all_tiles(eng, body):
            turns = (N - 2) // 2
            with eng.Fori(0, turns) as i:
                for p in range(2):
                    body(i, 2 * i + p, p, 2)
            for s in range(2 * turns, N):
                body(s // 2, s, s % 2, min(N - 1 - s, 2))

        def fed(i, s, p):
            return [(s * F + f, f if F > 1 else p, s if F > 1 else i) for f in range(F)]

        @block.tensor
        def _(pe):
            def turn(i, s, p):
                pe.wait_ge(k.t_rows[p].sem, k.t_rows[p].at(i + 1))
                pe.wait_ge(k.t_xcopied.sem, k.t_xcopied.at(s - 1))
                out = ps[:, XB + p, 0:D].bitcast(F16)
                for x in range(2 * C):
                    last = pe.transpose(out[:, x * P:(x + 1) * P], rows[p][:, x * P:(x + 1) * P], k.ident_h[:, :])
                last.then_inc(k.t_trans.sem, 1)

            def ascend(s, p):
                e = expert(pe, s)
                if not shared:
                    pe.wait_ge(k.t_xcopied.sem, k.t_xcopied.at(s + 1))
                pe.wait_ge(k.t_low.sem, k.t_low.at(s - 1))
                up(pe, e, source(s, p), UB + 2 * p).then_inc(k.t_up.sem, 1)

            def descend(s, p):
                e = expert(pe, s)
                pe.wait_ge(k.t_low.sem, k.t_low.at(s + 1))
                pe.wait_ge(k.t_ycopied.sem, k.t_ycopied.at(s - 1))
                down(pe, e, hs, ps[:, YB + p, 0:D]).then_inc(k.t_down.sem, 1)

            if not shared:
                turn(0, 0, 0)
                turn(0, 1, 1)
            ascend(0, 0)

            def body(i, s, p, ahead):
                if not shared and ahead > 1:
                    turn(i + 1, s + 2, p)
                if ahead > 0:
                    ascend(s + 1, 1 - p)
                descend(s, p)
            all_tiles(pe, body)

        @block.scalar
        def _(act):
            def silu(s, p):
                e = None if mix.gated else expert(act, s)
                act.wait_ge(k.t_up.sem, k.t_up.at(s + 1))
                act.wait_ge(k.t_low.sem, k.t_low.at(s - 1))
                activate(act, e, h32[p], UB + 2 * p).then_inc(k.t_act.sem, 1)

            silu(0, 0)

            def body(i, s, p, ahead):
                if ahead > 0:
                    silu(s + 1, 1 - p)
                if shared:
                    for q, b, n in fed(i, s, p):
                        act.wait_ge(k.t_raw[b].sem, k.t_raw[b].at(n + 1))
                        high = wh[:, bass.ds(q, 1), :].rearrange("p o n -> p (o n)")
                        act.activation(high, raw[b][:, :], ACT.Copy, scale=WS).then_inc(k.t_cast.sem, 1)
                act.wait_ge(k.t_down.sem, k.t_down.at(s + 1))
                act.wait_ge(k.t_stored[p].sem, k.t_stored[p].at(i))
                act.activation(y[p][:, :], ps[:, YB + p, 0:D], ACT.Copy, scale=1 / (WS * HS)).then_inc(k.t_ycopied.sem, 1)
                if shared:
                    act.wait_ge(k.t_ycopied.sem, k.t_ycopied.at(s + 1))
                    act.dma_start(k.y_rows[bass.ds(first_row + s * P, P), :], y[p][:, :]).then_inc(k.t_stored[p].sem, 16)
            all_tiles(act, body)
            if shared:
                for p in range(2):
                    act.wait_ge(k.t_stored[p].sem, k.t_stored[p].at(N // 2))

        @block.vector
        def _(dve):
            def take(s, p):
                dve.wait_ge(k.t_trans.sem, k.t_trans.at(s + 1))
                dve.wait_ge(k.t_up.sem, k.t_up.at(s - 1))
                dve.tensor_copy(x_s[p][:, :, :, :].rearrange("p x c n -> p (x c n)"), ps[:, XB + p, 0:D].bitcast(F16)).then_inc(k.t_xcopied.sem, 1)

            def split(s, p):
                dve.wait_ge(k.t_act.sem, k.t_act.at(s + 1))
                h = h32[p][0:R, :]
                if mix.gated:
                    dve.scalar_tensor_tensor(h, ps[0:R, UB + 2 * p, mix.hidden:2 * mix.hidden], HS / (WS * NS), h, ALU.mult, ALU.mult).then_inc(k.t_gated.sem, 1)
                    dve.wait_ge(k.t_gated.sem, k.t_gated.at(s + 1))
                dve.wait_ge(k.t_down.sem, k.t_down.at(s))
                if mix.gated:
                    dve.tensor_copy(hs[0][0:R, :], h).then_inc(k.t_high.sem, 1)
                    dve.wait_ge(k.t_high.sem, k.t_high.at(s + 1))
                    dve.tensor_tensor(hs[1][0:R, :], h, hs[0][0:R, :], ALU.subtract).then_inc(k.t_low.sem, 1)
                else:
                    dve.tensor_scalar(hs[0][:, :], h, HS, None, ALU.mult).then_inc(k.t_high.sem, 1)
                    dve.wait_ge(k.t_high.sem, k.t_high.at(s + 1))
                    dve.scalar_tensor_tensor(hs[1][:, :], h, HS, hs[0][:, :], ALU.mult, ALU.subtract).then_inc(k.t_low.sem, 1)

            if not shared:
                take(0, 0)
                take(1, 1)
            split(0, 0)

            def body(i, s, p, ahead):
                if not shared and ahead > 1:
                    take(s + 2, p)
                if ahead > 0:
                    split(s + 1, 1 - p)
                if shared:
                    for q, b, n in fed(i, s, p):
                        dve.wait_ge(k.t_cast.sem, k.t_cast.at(q + 1))
                        low = wl[:, bass.ds(q, 1), :].rearrange("p o n -> p (o n)")
                        high = wh[:, bass.ds(q, 1), :].rearrange("p o n -> p (o n)")
                        dve.scalar_tensor_tensor(low, raw[b][:, :], WS, high, ALU.mult, ALU.subtract).then_inc(k.t_wlow.sem, 1)
            all_tiles(dve, body)

        @block.sync
        def _(sp):
            def body(i, s, p, ahead):
                if shared:
                    for q, b, n in fed(i, s, p):
                        sp.wait_ge(k.t_wlow.sem, k.t_wlow.at(q - 1))
                        sp.dma_start(raw[b][:, :], k.dram[f"m{mix.n}_w"][bass.ds(q, 1), :, :].rearrange("o p n -> p (o n)")).then_inc(k.t_raw[b].sem, 16)
                else:
                    store(i, s, p)

            def store(i, s, p):
                sp.wait_ge(k.t_ycopied.sem, k.t_ycopied.at(s + 1))
                sp.dma_start(k.y_rows[bass.ds(first_row + s * P, P), :], y[p][:, :]).then_inc(k.t_stored[p].sem, 16)
            all_tiles(sp, body)
            if not shared:
                for p in range(2):
                    sp.wait_ge(k.t_stored[p].sem, k.t_stored[p].at((N + 1 - p) // 2))

        @block.gpsimd
        def _(pool):
            def body(i, s, p, ahead):
                pool.wait_ge(k.t_trans.sem, k.t_trans.at(s - 1))
                pool.tensor_copy(idx[p][:, :], r.table[:, bass.ds(s, 1)]).then_inc(k.t_idx.sem, 1)
                pool.wait_ge(k.t_idx.sem, k.t_idx.at(2 * s + 1))
                pool.sem_inc(k.t_idx.sem, 1)
                pool.indirect_dma_start(rows[p][:, :], None, k.n_rows, bass.IndirectOffsetOnAxis(ap=idx[p][:, 0:1], axis=0)).then_inc(k.t_rows[p].sem, 16)
            if not shared:
                all_tiles(pool, body)
    for s in (k.t_up, k.t_act, k.t_high, k.t_low, k.t_down, k.t_ycopied):
        s.base += N
    if mix.gated:
        k.t_gated.base += N
    for p in range(2):
        k.t_stored[p].base += (N + 1 - p) // 2
    if shared:
        for s in (k.t_cast, k.t_wlow):
            s.base += N * F
        for p in range(2):
            k.t_raw[p].base += N * F // 2
    else:
        for s in (k.t_trans, k.t_xcopied):
            s.base += N
        k.t_idx.base += 2 * N
        for p in range(2):
            k.t_rows[p].base += (N + 1 - p) // 2


def combine(k, mix, r, biases=None):
    nc, ps, c_ = k.nc, k.ps, k.c
    E, K = mix.E, mix.K
    with ExitStack() as ctx:
        own_share = k.sb("own_share", [P, P], ctx=ctx)
        y = [k.sb(f"c_y{p}", [P, K + 1, D], ctx=ctx) for p in range(2)]
        diag = [k.sb(f"c_diag{p}", [P, K, P], ctx=ctx) for p in range(2)]
        idx = [k.sb(f"c_i{p}", [P, K], I32, ctx=ctx) for p in range(2)]
        if biases is not None:
            b2, cw_t = biases, k.sb("cw_t", [E + 1, T], ctx=ctx)
            combine_weights(k, mix, r, cw_t)
        OB = 4
        with nc.Block() as block:
            def all_tiles(eng, body):
                with eng.Fori(0, NT // 2) as i:
                    for p in range(2):
                        body(i, 2 * i + p, p)

            @block.sync
            def _(sp):
                def body(i, t, p):
                    sp.wait_ge(k.g_summed.sem, k.g_summed.at(t - 1))
                    sp.dma_start(y[p][:, K, :], k.y_rows[bass.ds((mix.tiles + t) * P, P), :]).then_inc(k.g_shared[p].sem, 16)
                all_tiles(sp, body)

            @block.gpsimd
            def _(pool):
                def body(i, t, p):
                    pool.wait_ge(k.g_summed.sem, k.g_summed.at(t - 1))
                    pool.tensor_copy(idx[p][:, :], r.slot[:, bass.ds(t, 1), :].rearrange("p o k -> p (o k)")).then_inc(k.g_idx.sem, 1)
                    pool.wait_ge(k.g_idx.sem, k.g_idx.at(2 * t + 1))
                    pool.sem_inc(k.g_idx.sem, 1)
                    for n in range(K):
                        pool.indirect_dma_start(y[p][:, n, :], None, k.y_rows[0:mix.tiles * P, :], bass.IndirectOffsetOnAxis(ap=idx[p][:, n:n + 1], axis=0)).then_inc(k.g_load[p].sem, 16)
                all_tiles(pool, body)

            @block.tensor
            def _(pe):
                def body(i, t, p):
                    pe.wait_ge(k.g_load[p].sem, k.g_load[p].at(K * (i + 1)))
                    pe.wait_ge(k.g_shared[p].sem, k.g_shared[p].at(i + 1))
                    pe.wait_ge(k.g_diag.sem, k.g_diag.at(t + 1))
                    pe.wait_ge(k.g_added.sem, k.g_added.at(t - 1))
                    for m in range(C):
                        out = ps[:, OB + p, m * P:(m + 1) * P]
                        if biases is not None:
                            pe.matmul(out, b2[:, m * P:(m + 1) * P], cw_t[:, bass.ds(t * P, P)], start=True, stop=False)
                        for n in range(K + 1):
                            share = diag[p][:, n, :] if n < K else own_share[:, :]
                            last = pe.matmul(out, y[p][:, n, m * P:(m + 1) * P], share, start=(n == 0 and biases is None), stop=(n == K))
                    last.then_inc(k.g_summed.sem, 1)
                all_tiles(pe, body)

            @block.vector
            def _(dve):
                dve.tensor_scalar(own_share[:, :], c_["ident"], mix.shared_weight, None, ALU.mult)

                def body(i, t, p):
                    dve.wait_ge(k.g_summed.sem, k.g_summed.at(t - 1))
                    for n in range(K):
                        last = dve.tensor_scalar(diag[p][:, n, :], c_["ident"], r.w[:, n, bass.ds(t, 1)], None, ALU.mult)
                    last.then_inc(k.g_diag.sem, 1)

                def add(t, p):
                    dve.wait_ge(k.g_summed.sem, k.g_summed.at(t + 1))
                    x = k.x_t[:, :, bass.ds(t * P, P)]
                    dve.tensor_tensor(x, x, ps[:, OB + p, 0:D].rearrange("p (c n) -> p c n", c=C), ALU.add).then_inc(k.g_added.sem, 1)
                with dve.Fori(0, NT // 2) as i:
                    body(i, 2 * i, 0)
                    body(i, 2 * i + 1, 1)
                    add(2 * i, 0)
                    add(2 * i + 1, 1)
    for s in (k.g_summed, k.g_diag, k.g_added):
        s.base += NT
    k.g_idx.base += 2 * NT
    for p in range(2):
        k.g_load[p].base += K * NT // 2
        k.g_shared[p].base += NT // 2


def combine_weights(k, mix, r, cw_t):
    nc, ps, c_ = k.nc, k.ps, k.c
    E, K = mix.E, mix.K
    with ExitStack() as ctx, nc.Block() as block:
        hot = k.sb("cw_hot", [P, K, NT, E], ctx=ctx)
        cw = k.sb("cw", [P, NT, E + 1], ctx=ctx)

        @block.vector
        def _(dve):
            dve.memset(cw[:, :, E:E + 1], mix.shared_weight)
            for n in range(K):
                last = dve.tensor_tensor(hot[:, n, :, :], c_["iota"][:, 0:E].unsqueeze(1).broadcast_to([P, NT, E]), r.choice[:, :, n:n + 1].broadcast_to([P, NT, E]), ALU.is_equal)
            last.then_inc(k.m_chain.sem, 1)
            dve.wait_ge(k.m_chain.sem, k.m_chain.next())
            for n in range(K):
                last = dve.tensor_tensor(hot[:, n, :, :], hot[:, n, :, :], r.w[:, n, :].unsqueeze(2).broadcast_to([P, NT, E]), ALU.mult)
            last.then_inc(k.m_chain.sem, 1)
            dve.wait_ge(k.m_chain.sem, k.m_chain.next())
            assert K == 2
            dve.tensor_tensor(cw[:, :, 0:E], hot[:, 0, :, :], hot[:, 1, :, :], ALU.add).then_inc(k.m_cw.sem, 1)
            dve.wait_ge(k.m_cwt.sem, k.m_cwt.at(1))
            dve.tensor_copy(cw_t[:, :].rearrange("e (g n) -> e g n", g=G), ps[0:E + 1, 0:G, :])

        @block.tensor
        def _(pe):
            pe.wait_ge(k.m_cw.sem, k.m_cw.at(1))
            for t in range(NT):
                last = pe.transpose(ps[0:E + 1, t // 4, (t % 4) * P:(t % 4 + 1) * P], cw[:, t, :], c_["ident"])
            last.then_inc(k.m_cwt.sem, 1)
    k.m_cw.base += 1
    k.m_cwt.base += 1


def at_block(w, q, lo, n):
    return w[:, bass.ds(q, 1), lo:lo + n].rearrange("p o n -> p (o n)")


def stage_first_mixture(k):
    nc, ps = k.nc, k.ps
    mix = MIX0
    with ExitStack() as stage:
        r = Routing(k, mix, stage)
        b1 = k.sb("b1", [P, (E0 + 1) * FC], ctx=stage)
        b2 = k.sb("b2", [E0 + 1, D], ctx=stage)
        stage_weights(k, stage, [], ["L0_ffn_Wg"])
        layernorm(k)
        with ExitStack() as ctx:
            wh, wl = (k.sb(f"m_w{x}", [P, (E0 + 1) * mix.blocks, mix.width], F16, ctx=ctx) for x in "hl")
            route_first(k, mix, wh, wl, r, b1, b2)

            def up(pe, e, x, bank):
                for f in range(FC):
                    products = [(w, a, c) for w, a in three((wh, wl), x) for c in range(C)]
                    for n, (w, a, c) in enumerate(products):
                        last = pe.matmul(ps[:, bank + f // 4, (f % 4) * P:(f % 4 + 1) * P], at_block(w, e * mix.blocks + c, f * P, P), a[:, c, :],
                                         start=(n == 0), stop=(n == len(products) - 1))
                return last

            def activate(act, e, h, bank):
                for f in range(FC):
                    last = act.activation(h[:, f * P:(f + 1) * P], ps[:, bank + f // 4, (f % 4) * P:(f % 4 + 1) * P], ACT.Silu, scale=1 / (WS * NS),
                                          bias=b1[:, bass.ds(e * FC + f, 1)])
                return last

            def down(pe, e, hs, out):
                products = [(w, a, f) for w, a in three((wh, wl), hs) for f in range(FC)]
                for n, (w, a, f) in enumerate(products):
                    last = pe.matmul(out, a[:, f * P:(f + 1) * P], at_block(w, e * mix.blocks + 2 + f // 4, (f % 4) * D, D),
                                     start=(n == 0), stop=(n == len(products) - 1))
                return last

            tiles(k, mix, wh, wl, up, activate, down)
            tiles(k, mix, wh, wl, up, activate, down, r)
        combine(k, mix, r, b2)


def route_first(k, mix, wh, wl, r, b1, b2):
    nc, ps = k.nc, k.ps
    with ExitStack() as ctx:
        lg = k.sb("lg", [P, NT, E0], ctx=ctx)
        v8 = k.sb("v8", [P, NT, 8], ctx=ctx)
        i8 = k.sb("i8", [P, NT, 8], U32, ctx=ctx)
        ex = k.sb("ex", [P, NT, 8], ctx=ctx)
        z = k.sb("z", [P, 4, NT], ctx=ctx)

        def scores(act):
            act.wait_ge(k.m_shift.sem, k.m_shift.at(1))
            act.activation(ex[:, :, :], ex[:, :, :], ACT.Exp).then_inc(k.m_expd.sem, 1)

        def choose(dve):
            dve.wait_ge(k.m_logits.sem, k.m_logits.at(1))
            dve.tensor_scalar(lg[:, :, :].rearrange("p t e -> p (t e)"), ps[:, 7, 0:NT * E0], 1 / (WS * NS), None, ALU.mult).then_inc(k.m_chain.sem, 1)
            dve.wait_ge(k.m_chain.sem, k.m_chain.next())
            top8(k, dve, lg, v8, i8, r.choice)
            dve.tensor_tensor(ex[:, :, :], v8[:, :, :], v8[:, :, 0:1].broadcast_to([P, NT, 8]), ALU.subtract).then_inc(k.m_shift.sem, 1)
            dve.wait_ge(k.m_expd.sem, k.m_expd.at(1))
            dve.tensor_reduce(z[:, 0, :], ex[:, :, :], AX.X, ALU.add)
            dve.tensor_tensor(z[:, 2, :], ex[:, :, 0], ex[:, :, 1], ALU.add).then_inc(k.m_chain.sem, 1)
            dve.wait_ge(k.m_chain.sem, k.m_chain.next())
            dve.scalar_tensor_tensor(z[:, 1, :], z[:, 0, :], 1e-9, z[:, 2, :], ALU.mult, ALU.add).then_inc(k.m_chain.sem, 1)
            dve.wait_ge(k.m_chain.sem, k.m_chain.next())
            dve.reciprocal(z[:, 3, :], z[:, 1, :]).then_inc(k.m_chain.sem, 1)
            dve.wait_ge(k.m_chain.sem, k.m_chain.next())
            for n in range(K0):
                dve.tensor_tensor(r.w[:, n, :], ex[:, :, n], z[:, 3, :], ALU.mult)

        with nc.Block() as block:
            @block.sync
            def _(sp):
                sp.dma_start(b1[:, :], k.dram["m0_b1"]).then_inc(k.m_bias.sem, 16)
                sp.dma_start(b2[:, :], k.dram["m0_b2"]).then_inc(k.m_bias.sem, 16)
                sp.wait_ge(k.m_bias.sem, 32)
        route(k, mix, k.w["L0_ffn_Wg"], wh, wl, scores, choose, r)


def stage_single_attention(k):
    with ExitStack() as stage:
        stage_weights(k, stage, ["L1_xattn_wk_t", "L1_xattn_wv", "L1_xattn_bq", "L1_xattn_bk", "L1_xattn_bv"], ["L1_xattn_wq"])
        layernorm(k)
        single_attention(k, stage)


def single_attention(k, stage):
    nc, ps, c_ = k.nc, k.ps, k.c
    scale = D ** -0.5
    q_t = k.sb("q_t", [P, C, T], ctx=stage)
    o_t = q_t
    qp_t = k.sb("qp_t", [P, C, T], ctx=stage)

    def take_q(block):
        @block.scalar
        def _(act):
            for g in range(G):
                for m in range(C):
                    act.wait_ge(k.projected.sem, k.projected.at(g * C + m + 1))
                    act.activation(q_t[:, m, group(g)], ps[:, g * C + m, :], ACT.Identity, scale=1 / (WS * NS), bias=k.w["L1_xattn_bq"][:, 0, m:m + 1])
    project(k, k.w["L1_xattn_wq"], (k.n_h, k.n_l), take_q)

    with ExitStack() as ctx:
        QB = 4
        NQ = B // QB
        q_bk = k.sb("q_bk", [1, T], ctx=ctx)

        def take_qp(block):
            @block.scalar
            def _(act):
                for g in range(G):
                    for m in range(C):
                        act.wait_ge(k.projected.sem, k.projected.at(g * C + m + 1))
                        act.activation(qp_t[:, m, group(g)], ps[:, g * C + m, :], ACT.Copy, scale=scale)
        project(k, k.w["L1_xattn_wk_t"], q_t, take_qp)
        with nc.Block() as block:
            @block.tensor
            def _(pe):
                for g in range(G):
                    for c in range(C):
                        last = pe.matmul(ps[0:1, g, :], k.w["L1_xattn_bk"][:, 0, c:c + 1], q_t[:, c, group(g)], start=(c == 0), stop=(c == C - 1))
                    last.then_inc(k.projected.sem, 1)

            @block.scalar
            def _(act):
                for g in range(G):
                    act.wait_ge(k.projected.sem, k.projected.at(g + 1))
                    act.activation(q_bk[0:1, group(g)], ps[0:1, g, :], ACT.Copy, scale=scale)
        k.projected.base += G

        ctx_t = [k.sb(f"b_ctx_t{p}", [P, QB, C, SK], ctx=ctx) for p in range(2)]
        ctx_n = [k.sb(f"b_ctx{p}", [P, QB, 2, D], ctx=ctx) for p in range(2)]
        ctx_l = [k.sb(f"b_ctx_last{p}", [1, QB, D], ctx=ctx) for p in range(2)]
        q_s = [k.sb(f"b_q{p}", [P, C, P], ctx=ctx) for p in range(2)]
        qb_s = [k.sb(f"b_qbk{p}", [1, P], ctx=ctx) for p in range(2)]
        neg_max = k.sb("b_neg_max", [P, 2], ctx=ctx)
        sums = k.sb("b_sums", [P, 2], ctx=ctx)
        inv = k.sb("b_inv", [P, 2], ctx=ctx)
        probs = [k.sb(f"b_probs{p}", [P, SK], ctx=ctx) for p in range(2)]
        pn = [k.sb(f"b_pn{p}", [P, SK], ctx=ctx) for p in range(2)]
        p_t = [k.sb(f"b_p_t{p}", [P, 2, P], ctx=ctx) for p in range(2)]
        p_l = [k.sb(f"b_p_last{p}", [1, P], ctx=ctx) for p in range(2)]
        SB, TB, OB = 0, 2, 4

        with nc.Block() as block:
            @block.sync
            def _(sp):
                def fetch(i, p):
                    n = 2 * i + p
                    sp.wait_ge(k.b_scored.sem, k.b_scored.at(n - 1))
                    for j in range(QB):
                        sp.dma_start(ctx_t[p][:, j, :, :], k.dram["ctx_t"][bass.ds(n * QB + j, 1), :, :].rearrange("o (c p) n -> p (o c) n", p=P)).then_inc(k.b_ctx_t[p].sem, 16)
                with sp.Fori(0, NQ // 2) as i:
                    fetch(i, 0)
                    fetch(i, 1)

            @block.gpsimd
            def _(pool):
                def fetch(i, p):
                    n = 2 * i + p
                    pool.wait_ge(k.b_out.sem, k.b_out.at(n - 1))
                    for j in range(QB):
                        row = k.dram["ctx"][bass.ds(n * QB + j, 1), :, :]
                        pool.dma_start(ctx_n[p][:, j, :, :], row[:, 0:2 * P, :].rearrange("o (r p) d -> p (o r) d", p=P)).then_inc(k.b_ctx[p].sem, 16)
                        pool.dma_start(ctx_l[p][0:1, j, :], row[:, 2 * P, :]).then_inc(k.b_ctx[p].sem, 16)
                with pool.Fori(0, NQ // 2) as i:
                    fetch(i, 0)
                    fetch(i, 1)

            @block.tensor
            def _(pe):
                def scores(i, p):
                    n = 2 * i + p
                    pe.wait_ge(k.b_ctx_t[p].sem, k.b_ctx_t[p].at(QB * (i + 1)))
                    pe.wait_ge(k.b_qs.sem, k.b_qs.at(n + 1))
                    pe.wait_ge(k.b_exp.sem, k.b_exp.at(n - 1))
                    pe.matmul(ps[:, SB + p, 0:SK], qb_s[p][0:1, :], k.ones_row[0:1, :], start=True, stop=False, skip_group_check=True)
                    for j in range(QB):
                        for c in range(C):
                            last = pe.matmul(ps[j * S:(j + 1) * S, SB + p, 0:SK], q_s[p][:, c, j * S:(j + 1) * S], ctx_t[p][:, j, c, :],
                                             start=False, stop=(c == C - 1), skip_group_check=True)
                    last.then_inc(k.b_scored.sem, 1)

                def weigh(i, p):
                    n = 2 * i + p
                    pe.wait_ge(k.b_normed.sem, k.b_normed.at(n + 1))
                    pe.wait_ge(k.b_tcopied.sem, k.b_tcopied.at(n - 1))
                    for r in range(2):
                        pe.transpose(ps[:, TB + p, r * P:(r + 1) * P], pn[p][:, r * P:(r + 1) * P], c_["ident"])
                    pe.transpose(ps[0:1, TB + p, 2 * P:3 * P], pn[p][:, 2 * P:SK], c_["ident"]).then_inc(k.b_trans.sem, 1)
                    pe.wait_ge(k.b_ctx[p].sem, k.b_ctx[p].at(2 * QB * (i + 1)))
                    pe.wait_ge(k.b_taken.sem, k.b_taken.at(n - 1))
                    pe.wait_ge(k.b_tcopied.sem, k.b_tcopied.at(n + 1))
                    for c in range(C):
                        for j in range(QB):
                            out = ps[:, OB + p, c * P + j * S:c * P + (j + 1) * S]
                            for r in range(2):
                                pe.matmul(out, ctx_n[p][:, j, r, c * P:(c + 1) * P], p_t[p][:, r, j * S:(j + 1) * S], start=(r == 0), stop=False)
                            last = pe.matmul(out, ctx_l[p][0:1, j, c * P:(c + 1) * P], p_l[p][0:1, j * S:(j + 1) * S], start=False, stop=True)
                    last.then_inc(k.b_out.sem, 1)

                scores(0, 0)
                with pe.Fori(0, NQ // 2 - 1) as i:
                    scores(i, 1)
                    weigh(i, 0)
                    scores(i + 1, 0)
                    weigh(i, 1)
                i = NQ // 2 - 1
                scores(i, 1)
                weigh(i, 0)
                weigh(i, 1)

            @block.scalar
            def _(act):
                def softmax(i, p):
                    n = 2 * i + p
                    act.wait_ge(k.b_max.sem, k.b_max.at(n + 1))
                    act.wait_ge(k.b_normed.sem, k.b_normed.at(n - 1))
                    act.activation(probs[p][:, :], ps[:, SB + p, 0:SK], ACT.Exp, bias=neg_max[:, p:p + 1], accum_out=sums[:, p:p + 1]).then_inc(k.b_exp.sem, 1)
                with act.Fori(0, NQ // 2) as i:
                    softmax(i, 0)
                    softmax(i, 1)

            @block.vector
            def _(dve):
                def queries(i, p):
                    n = 2 * i + p
                    dve.wait_ge(k.b_scored.sem, k.b_scored.at(n - 1))
                    dve.tensor_copy(q_s[p][:, :, :], qp_t[:, :, bass.ds(n * P, P)])
                    dve.tensor_copy(qb_s[p][0:1, :], q_bk[0:1, bass.ds(n * P, P)]).then_inc(k.b_qs.sem, 1)

                def softmax(i, p):
                    n = 2 * i + p
                    dve.wait_ge(k.b_scored.sem, k.b_scored.at(n + 1))
                    dve.tensor_reduce(neg_max[:, p:p + 1], ps[:, SB + p, 0:SK], AX.X, ALU.max, negate=True).then_inc(k.b_max.sem, 1)
                    dve.wait_ge(k.b_exp.sem, k.b_exp.at(n + 1))
                    dve.reciprocal(inv[:, p:p + 1], sums[:, p:p + 1]).then_inc(k.b_inv.sem, 1)
                    dve.wait_ge(k.b_inv.sem, k.b_inv.at(n + 1))
                    dve.wait_ge(k.b_trans.sem, k.b_trans.at(n - 1))
                    dve.tensor_scalar(pn[p][:, :], probs[p][:, :], inv[:, p:p + 1], None, ALU.mult).then_inc(k.b_normed.sem, 1)

                def outputs(i, p):
                    n = 2 * i + p
                    dve.wait_ge(k.b_out.sem, k.b_out.at(n - 1))
                    dve.wait_ge(k.b_trans.sem, k.b_trans.at(n + 1))
                    dve.tensor_copy(p_l[p][0:1, :], ps[0:1, TB + p, 2 * P:3 * P])
                    dve.tensor_copy(p_t[p][:, :, :].rearrange("p r q -> p (r q)"), ps[:, TB + p, 0:2 * P]).then_inc(k.b_tcopied.sem, 1)
                    dve.wait_ge(k.b_out.sem, k.b_out.at(n + 1))
                    dve.tensor_copy(o_t[:, :, bass.ds(n * P, P)], ps[:, OB + p, 0:2 * P].rearrange("p (c q) -> p c q", c=C)).then_inc(k.b_taken.sem, 1)

                queries(0, 0)
                with dve.Fori(0, NQ // 2 - 1) as i:
                    queries(i, 1)
                    softmax(i, 0)
                    outputs(i, 0)
                    queries(i + 1, 0)
                    softmax(i, 1)
                    outputs(i, 1)
                i = NQ // 2 - 1
                queries(i, 1)
                softmax(i, 0)
                outputs(i, 0)
                softmax(i, 1)
                outputs(i, 1)

    def add_out(block):
        @block.vector
        def _(dve):
            for g in range(G):
                for m in range(C):
                    dve.wait_ge(k.projected.sem, k.projected.at(g * C + m + 1))
                    x = k.x_t[:, m, group(g)]
                    dve.scalar_tensor_tensor(x, ps[:, g * C + m, :], k.w["L1_xattn_bv"][:, 0, m:m + 1], x, ALU.add, ALU.add)
    project(k, k.w["L1_xattn_wv"], o_t, add_out)


def stage_causal_attention(k):
    with ExitStack() as stage:
        stage_weights(k, stage, ["L1_attn_bq", "L1_attn_bk", "L1_attn_bv"], ["L1_attn_Wq_t", "L1_attn_Wk_t", "L1_attn_Wv_t"])
        layernorm(k)
        causal_attention(k, stage)


def causal_attention(k, stage):
    nc, ps, c_ = k.nc, k.ps, k.c
    scale = D ** -0.5
    q_t = k.sb("q_t", [P, C, T], ctx=stage)            
    k_t = k.sb("k_t", [P, C, T], ctx=stage)
    n = (k.n_h, k.n_l)

    def take_q(block):
        @block.scalar
        def _(act):
            for g in range(G):
                for m in range(C):
                    act.wait_ge(k.projected.sem, k.projected.at(g * C + m + 1))
                    act.activation(q_t[:, m, group(g)], ps[:, g * C + m, :], ACT.Identity, scale=1 / (WS * NS), bias=k.w["L1_attn_bq"][:, 0, m:m + 1])
    project(k, k.w["L1_attn_Wq_t"], n, take_q)

    def take_k(block):
        @block.scalar
        def _(act):
            for g in range(G):
                for m in range(C):
                    act.wait_ge(k.projected.sem, k.projected.at(g * C + m + 1))
                    act.activation(k_t[:, m, group(g)], ps[:, g * C + m, :], ACT.Identity, scale=1 / (WS * NS), bias=k.w["L1_attn_bk"][:, 0, m:m + 1])
    project(k, k.w["L1_attn_Wk_t"], n, take_k)

    with ExitStack() as ctx:
        n_s = [[k.sb(f"c_n{p}{x}", [P, C, P], F16, ctx=ctx) for x in range(2)] for p in range(2)]
        q_s = [k.sb(f"c_q{p}", [P, C, P], ctx=ctx) for p in range(2)]
        v = [k.sb(f"c_v{p}", [P, D], ctx=ctx) for p in range(2)]
        neg_max = k.sb("c_neg_max", [P, 2], ctx=ctx)
        sums = k.sb("c_sums", [P, 2], ctx=ctx)
        inv = k.sb("c_inv", [P, 2], ctx=ctx)
        probs = [k.sb(f"c_probs{p}", [P, P], ctx=ctx) for p in range(2)]
        pn = [k.sb(f"c_pn{p}", [P, P], ctx=ctx) for p in range(2)]
        p_t = [k.sb(f"c_p_t{p}", [P, P], ctx=ctx) for p in range(2)]
        VB, SB, TB, OB = 0, 2, 4, 6
        wv = k.w["L1_attn_Wv_t"]

        with nc.Block() as block:
            @block.gpsimd
            def _(pool):
                with pool.Fori(0, NT // 2) as i:
                    for p in range(2):
                        t = 2 * i + p
                        pool.wait_ge(k.c_scored.sem, k.c_scored.at(t - 1))
                        for x in range(2):
                            pool.tensor_copy(n_s[p][x][:, :, :], n[x][:, :, bass.ds(t * P, P)])
                        pool.tensor_copy(q_s[p][:, :, :], q_t[:, :, bass.ds(t * P, P)]).then_inc(k.c_static.sem, 1)

            @block.tensor
            def _(pe):
                def scores(i, p):
                    t = 2 * i + p
                    pe.wait_ge(k.c_static.sem, k.c_static.at(t + 1))
                    pe.wait_ge(k.c_vcopied.sem, k.c_vcopied.at(t - 1))
                    products = [(w, x, c) for w, x in three(wv, n_s[p]) for c in range(C)]
                    for m, (w, x, c) in enumerate(products):
                        pe.matmul(ps[:, VB + p, 0:D], x[:, c, :], w[:, c, :], start=(m == 0), stop=(m == len(products) - 1))
                    pe.wait_ge(k.c_exp.sem, k.c_exp.at(t - 1))
                    pe.matmul(ps[:, SB + p, 0:P], k.ident_bf[:, :], k.causal_bf[:, :], start=True, stop=False)
                    for c in range(C):
                        last = pe.matmul(ps[:, SB + p, 0:P], q_s[p][:, c, :], k_t[:, c, bass.ds(t * P, P)], start=False, stop=(c == C - 1))
                    last.then_inc(k.c_scored.sem, 1)

                def weigh(i, p):
                    t = 2 * i + p
                    pe.wait_ge(k.c_normed.sem, k.c_normed.at(t + 1))
                    pe.wait_ge(k.c_tcopied.sem, k.c_tcopied.at(t - 1))
                    pe.transpose(ps[:, TB + p, 0:P], pn[p][:, :], c_["ident"]).then_inc(k.c_trans.sem, 1)
                    pe.wait_ge(k.c_tcopied.sem, k.c_tcopied.at(t + 1))
                    pe.wait_ge(k.c_vcopied.sem, k.c_vcopied.at(t + 1))
                    pe.wait_ge(k.c_taken.sem, k.c_taken.at(t - 1))
                    for c in range(C):
                        last = pe.matmul(ps[:, OB + p, c * P:(c + 1) * P], v[p][:, c * P:(c + 1) * P], p_t[p][:, :], start=True, stop=True)
                    last.then_inc(k.c_out.sem, 1)

                scores(0, 0)
                with pe.Fori(0, NT // 2 - 1) as i:
                    scores(i, 1)
                    weigh(i, 0)
                    scores(i + 1, 0)
                    weigh(i, 1)
                i = NT // 2 - 1
                scores(i, 1)
                weigh(i, 0)
                weigh(i, 1)

            @block.scalar
            def _(act):
                with act.Fori(0, NT // 2) as i:
                    for p in range(2):
                        t = 2 * i + p
                        act.wait_ge(k.c_scored.sem, k.c_scored.at(t + 1))
                        act.wait_ge(k.c_out.sem, k.c_out.at(t - 1))
                        act.activation(v[p][:, :], ps[:, VB + p, 0:D], ACT.Copy, scale=1 / (WS * NS)).then_inc(k.c_vcopied.sem, 1)
                        act.wait_ge(k.c_max.sem, k.c_max.at(2 * (t + 1)))
                        act.wait_ge(k.c_normed.sem, k.c_normed.at(t - 1))
                        act.activation(probs[p][:, :], ps[:, SB + p, 0:P], ACT.Exp, scale=scale, bias=neg_max[:, p:p + 1], accum_out=sums[:, p:p + 1]).then_inc(k.c_exp.sem, 1)

            @block.vector
            def _(dve):
                with dve.Fori(0, NT // 2) as i:
                    for p in range(2):
                        t = 2 * i + p
                        dve.wait_ge(k.c_scored.sem, k.c_scored.at(t + 1))
                        dve.tensor_reduce(neg_max[:, p:p + 1], ps[:, SB + p, 0:P], AX.X, ALU.max, negate=True).then_inc(k.c_max.sem, 1)
                        dve.wait_ge(k.c_max.sem, k.c_max.at(2 * t + 1))
                        dve.tensor_scalar(neg_max[:, p:p + 1], neg_max[:, p:p + 1], scale, None, ALU.mult).then_inc(k.c_max.sem, 1)
                        dve.wait_ge(k.c_exp.sem, k.c_exp.at(t + 1))
                        dve.reciprocal(inv[:, p:p + 1], sums[:, p:p + 1]).then_inc(k.c_inv.sem, 1)
                        dve.wait_ge(k.c_inv.sem, k.c_inv.at(t + 1))
                        dve.wait_ge(k.c_trans.sem, k.c_trans.at(t - 1))
                        dve.tensor_scalar(pn[p][:, :], probs[p][:, :], inv[:, p:p + 1], None, ALU.mult).then_inc(k.c_normed.sem, 1)
                        dve.wait_ge(k.c_out.sem, k.c_out.at(t - 1))
                        dve.wait_ge(k.c_trans.sem, k.c_trans.at(t + 1))
                        dve.tensor_copy(p_t[p][:, :], ps[:, TB + p, 0:P]).then_inc(k.c_tcopied.sem, 1)
                        dve.wait_ge(k.c_out.sem, k.c_out.at(t + 1))
                        for c in range(C):
                            x = k.x_t[:, c, bass.ds(t * P, P)]
                            last = dve.scalar_tensor_tensor(x, ps[:, OB + p, c * P:(c + 1) * P], k.w["L1_attn_bv"][:, 0, c:c + 1], x, ALU.add, ALU.add)
                        last.then_inc(k.c_taken.sem, 1)


def stage_second_mixture(k):
    nc, ps = k.nc, k.ps
    mix = MIX1
    gate_at, up_at, down_at = 0, C * I1, 2 * C * I1
    with ExitStack() as stage:
        r = Routing(k, mix, stage)
        stage_weights(k, stage, ["L1_ffn_gate_bias"], ["L1_ffn_gate_w_t"])
        layernorm(k)
        with ExitStack() as ctx:
            wh, wl = (k.sb(f"m_w{x}", [P, E1 + 1, mix.width], F16, ctx=ctx) for x in "hl")
            route_second(k, mix, wh, wl, r)

            def up(pe, e, x, bank):
                for part, at in enumerate((gate_at, up_at)):
                    for h in range(2):
                        products = [(w, a, c) for w, a in three((wh, wl), x) for c in range(C)]
                        for n, (w, a, c) in enumerate(products):
                            last = pe.matmul(ps[0:IH, bank, (2 * part + h) * P:(2 * part + h + 1) * P], at_block(w, e, at + c * I1 + h * IH, IH), a[:, c, :],
                                             start=(n == 0), stop=(n == len(products) - 1))
                return last

            def activate(act, e, h, bank):
                return act.activation(h[0:IH, :], ps[0:IH, bank, 0:2 * P], ACT.Silu, scale=1 / (WS * NS))

            def down(pe, e, hs, out):
                products = [(w, a, h) for w, a in three((wh, wl), hs) for h in range(2)]
                for n, (w, a, h) in enumerate(products):
                    last = pe.matmul(out, a[0:IH, h * P:(h + 1) * P], at_block(w[0:IH, :, :], e, down_at + h * D, D),
                                     start=(n == 0), stop=(n == len(products) - 1))
                return last

            tiles(k, mix, wh, wl, up, activate, down)
            tiles(k, mix, wh, wl, up, activate, down, r)
        combine(k, mix, r)


def route_second(k, mix, wh, wl, r):
    nc, ps, c_ = k.nc, k.ps, k.c
    NG, EG = 4, E1 // 4
    gate_bias = k.w["L1_ffn_gate_bias"]
    with ExitStack() as ctx:
        sc = k.sb("sc", [P, NT, E1], ctx=ctx)
        sb = k.sb("sbias", [P, NT, NG, EG], ctx=ctx)
        pair = k.sb("pair", [P, 6, NT, NG], ctx=ctx)
        rank = k.sb("rank", [P, 3, NT, NG * NG], ctx=ctx)
        allowed = k.sb("allowed", [P, NT, NG], ctx=ctx)
        masked = k.sb("masked", [P, NT, E1], ctx=ctx)
        v8 = k.sb("v8", [P, NT, 8], ctx=ctx)
        i8 = k.sb("i8", [P, NT, 8], U32, ctx=ctx)
        one = k.sb("one", [P, K1, NT, E1], ctx=ctx)
        z = k.sb("z", [P, 2, NT], ctx=ctx)

        def scores(act):
            act.wait_ge(k.m_logits.sem, k.m_logits.at(1))
            act.activation(sc[:, :, :].rearrange("p t e -> p (t e)"), ps[:, 7, 0:NT * E1], ACT.Sigmoid, scale=1 / (WS * NS)).then_inc(k.m_expd.sem, 1)

        def choose(dve):
            dve.wait_ge(k.m_expd.sem, k.m_expd.at(1))
            flat = sb[:, :, :, :].rearrange("p t g e -> p t (g e)")
            dve.tensor_tensor(flat, sc[:, :, :], gate_bias[:, 0:1, :].broadcast_to([P, NT, E1]), ALU.add).then_inc(k.m_chain.sem, 1)
            dve.wait_ge(k.m_chain.sem, k.m_chain.next())
            pairs = [(a, b) for a in range(EG) for b in range(a + 1, EG)]
            for n, (a, b) in enumerate(pairs):
                last = dve.tensor_tensor(pair[:, n, :, :], sb[:, :, :, a], sb[:, :, :, b], ALU.add)
            last.then_inc(k.m_chain.sem, 1)
            dve.wait_ge(k.m_chain.sem, k.m_chain.next())
            for n in range(1, len(pairs)):
                dve.tensor_tensor(pair[:, 0, :, :], pair[:, 0, :, :], pair[:, n, :, :], ALU.max).then_inc(k.m_chain.sem, 1)
                dve.wait_ge(k.m_chain.sem, k.m_chain.next())
            score = pair[:, 0, :, :]
            own = score.unsqueeze(3).broadcast_to([P, NT, NG, NG])
            other = score.unsqueeze(2).broadcast_to([P, NT, NG, NG])
            ranks = [rank[:, n, :, :].rearrange("p t (a b) -> p t a b", a=NG) for n in range(3)]
            dve.tensor_tensor(ranks[0], other, own, ALU.is_gt)
            dve.tensor_tensor(ranks[1], other, own, ALU.is_equal).then_inc(k.m_chain.sem, 1)
            dve.wait_ge(k.m_chain.sem, k.m_chain.next())
            earlier = c_["earlier"].unsqueeze(1).broadcast_to([P, NT, NG * NG])
            dve.tensor_tensor(rank[:, 1, :, :], rank[:, 1, :, :], earlier, ALU.mult).then_inc(k.m_chain.sem, 1)
            dve.wait_ge(k.m_chain.sem, k.m_chain.next())
            dve.tensor_tensor(rank[:, 2, :, :], rank[:, 0, :, :], rank[:, 1, :, :], ALU.add).then_inc(k.m_chain.sem, 1)
            dve.wait_ge(k.m_chain.sem, k.m_chain.next())
            dve.tensor_reduce(allowed[:, :, :], ranks[2], AX.X, ALU.add).then_inc(k.m_chain.sem, 1)
            dve.wait_ge(k.m_chain.sem, k.m_chain.next())
            dve.tensor_scalar(allowed[:, :, :], allowed[:, :, :], 2.0, MASKED, ALU.is_ge, ALU.mult).then_inc(k.m_chain.sem, 1)
            dve.wait_ge(k.m_chain.sem, k.m_chain.next())
            dve.tensor_tensor(masked[:, :, :].rearrange("p t (g e) -> p t g e", g=NG), sb[:, :, :, :], allowed[:, :, :].unsqueeze(3).broadcast_to([P, NT, NG, EG]), ALU.add).then_inc(k.m_chain.sem, 1)
            dve.wait_ge(k.m_chain.sem, k.m_chain.next())
            top8(k, dve, masked, v8, i8, r.choice)
            for n in range(K1):
                last = dve.tensor_tensor(one[:, n, :, :], c_["iota"][:, 0:E1].unsqueeze(1).broadcast_to([P, NT, E1]), r.choice[:, :, n:n + 1].broadcast_to([P, NT, E1]), ALU.is_equal)
            last.then_inc(k.m_chain.sem, 1)
            dve.wait_ge(k.m_chain.sem, k.m_chain.next())
            for n in range(K1):
                last = dve.tensor_tensor(one[:, n, :, :], one[:, n, :, :], sc[:, :, :], ALU.mult)
            last.then_inc(k.m_chain.sem, 1)
            dve.wait_ge(k.m_chain.sem, k.m_chain.next())
            for n in range(K1):
                last = dve.tensor_reduce(r.w[:, n, :], one[:, n, :, :], AX.X, ALU.add)
            last.then_inc(k.m_chain.sem, 1)
            dve.wait_ge(k.m_chain.sem, k.m_chain.next())
            dve.tensor_reduce(z[:, 0, :], r.w[:, :, :].rearrange("p k t -> p t k"), AX.X, ALU.add).then_inc(k.m_chain.sem, 1)
            dve.wait_ge(k.m_chain.sem, k.m_chain.next())
            dve.tensor_scalar(z[:, 0, :], z[:, 0, :], 1e-20, None, ALU.add).then_inc(k.m_chain.sem, 1)
            dve.wait_ge(k.m_chain.sem, k.m_chain.next())
            dve.reciprocal(z[:, 1, :], z[:, 0, :]).then_inc(k.m_chain.sem, 1)
            dve.wait_ge(k.m_chain.sem, k.m_chain.next())
            dve.scalar_tensor_tensor(r.w[:, :, :], r.w[:, :, :], 2.5, z[:, 1, :].unsqueeze(1).broadcast_to([P, K1, NT]), ALU.mult, ALU.mult)

        route(k, mix, k.w["L1_ffn_gate_w_t"], wh, wl, scores, choose, r)


def build(nc, dram):
    with ExitStack() as ctx:
        k = Core(nc, ctx, dram)
        k.ps = ctx.enter_context(nc.psum_tensor("ps", [P, 8, 512], F32))
        k.x_t = k.sb("x_t_sb", [P, C, T])
        k.n_h = k.sb("n_h", [P, C, T], F16)
        k.n_l = k.sb("n_l", [P, C, T], F16)
        k.consts = k.sb("consts_sb", [P, sum(CONST.values())])
        k.c, at = {}, 0
        for name, n in CONST.items():
            k.c[name] = k.consts[:, at:at + n]
            at += n
        k.ones_mean = k.sb("ones_mean", [P, P])
        k.ones_row = k.sb("ones_row", [1, SK])
        k.ones_h = k.sb("ones_h", [P, P], F16)
        k.eps = k.sb("eps", [P, 1])
        k.ident_h = k.sb("ident_h", [P, P], F16)
        k.before_h = k.sb("before_h", [P, P], F16)
        k.ident_bf = k.sb("ident_bf", [P, P], BF16)
        k.repeat_bf = k.sb("repeat_bf", [S, P], BF16)
        k.causal_bf = k.sb("causal_bf", [P, P], BF16)
        k.w = {}
        k.n_rows = nc.dram_tensor("n_rows", [T, 2 * D], F16, kind="Internal").ap()
        k.y_rows = nc.dram_tensor("y_rows", [MAX_TILES * P + T, D], F32, kind="Internal").ap()

        k.mean_ready = k.count("mean_ready")
        k.squared = k.count("squared")
        k.var_ready = k.count("var_ready")
        k.std_ready = k.count("std_ready")
        k.inv_ready = k.count("inv_ready")
        k.centred = k.count("centred")
        k.normed = k.count("normed")
        k.high_ready = k.count("high_ready")
        k.split_high = k.count("split_high")
        k.projected = k.count("projected")
        k.a_keys_done = k.count("a_keys_done", 2)
        k.a_kproj = k.count("a_kproj")
        k.a_kcopied = k.count("a_kcopied", 1)
        k.a_vcopied = k.count("a_vcopied", 1)
        k.a_qblk = k.count("a_qblk")
        k.a_maskb = k.count("a_maskb", 2)
        k.a_ptcopied = k.count("a_ptcopied", 2)
        k.a_scored = k.count("a_scored", 2)
        k.a_normed = k.count("a_normed", 8)
        k.a_pt = k.count("a_pt", 2)
        k.a_own = k.count("a_own", 1)
        k.a_out = k.count("a_out", 2)
        k.a_max = k.count("a_max")
        k.a_exp = k.count("a_exp", 4)
        k.a_inv = k.count("a_inv")
        k.a_centred = k.count("a_centred", 2)
        k.a_high = k.count("a_high")
        k.a_low = k.count("a_low", 2)
        k.a_osum = k.count("a_osum")
        k.a_vlast = k.count("a_vlast")
        k.a_vtaken = k.count("a_vtaken")
        k.a_split = k.count("a_split")
        k.r_proj = k.count("r_proj")
        k.r_added = k.count("r_added", 1)
        k.r_scan = k.count("r_scan", 2)
        k.r_out = k.count("r_out", 1)
        k.r_init = k.count("r_init")
        k.r_valued = k.count("r_valued")
        k.r_sig = k.count("r_sig", 2)
        k.r_floor = k.count("r_floor")
        k.r_sum = k.count("r_sum")
        k.r_inv = k.count("r_inv")
        k.r_gates = k.count("r_gates")
        k.r_first = k.count("r_first")
        k.m_chain = k.count("m_chain")
        k.m_logits = k.count("m_logits")
        k.m_counted = k.count("m_counted")
        k.m_prefixed = k.count("m_prefixed")
        k.m_onehot = k.count("m_onehot", 2)
        k.m_placed = k.count("m_placed", 2)
        k.m_rowt = k.count("m_rowt")
        k.m_rowcopied = k.count("m_rowcopied", 1)
        k.m_shift = k.count("m_shift")
        k.m_expd = k.count("m_expd")
        k.m_cw = k.count("m_cw")
        k.m_cwt = k.count("m_cwt")
        k.t_trans = k.count("t_trans", 2)
        k.t_xcopied = k.count("t_xcopied", 2)
        k.t_up = k.count("t_up", 2)
        k.t_act = k.count("t_act", 2)
        k.t_high = k.count("t_high", 2)
        k.t_low = k.count("t_low", 2)
        k.t_down = k.count("t_down", 2)
        k.t_ycopied = k.count("t_ycopied", 2)
        k.t_idx = k.count("t_idx")
        k.t_cast = k.count("t_cast", 2)
        k.t_wlow = k.count("t_wlow", 2)
        k.t_gated = k.count("t_gated")
        k.g_idx = k.count("g_idx")
        k.g_diag = k.count("g_diag")
        k.g_added = k.count("g_added", 2)
        k.g_summed = k.count("g_summed", 2)
        k.b_scored = k.count("b_scored", 2)
        k.b_out = k.count("b_out", 2)
        k.b_qs = k.count("b_qs")
        k.b_exp = k.count("b_exp", 2)
        k.b_normed = k.count("b_normed", 2)
        k.b_tcopied = k.count("b_tcopied", 2)
        k.b_trans = k.count("b_trans", 2)
        k.b_taken = k.count("b_taken", 2)
        k.b_max = k.count("b_max")
        k.b_inv = k.count("b_inv")
        k.c_static = k.count("c_static")
        k.c_scored = k.count("c_scored", 2)
        k.c_vcopied = k.count("c_vcopied", 2)
        k.c_exp = k.count("c_exp", 2)
        k.c_normed = k.count("c_normed", 2)
        k.c_tcopied = k.count("c_tcopied", 2)
        k.c_trans = k.count("c_trans", 2)
        k.c_taken = k.count("c_taken", 2)
        k.c_out = k.count("c_out", 2)
        k.c_max = k.count("c_max")
        k.c_inv = k.count("c_inv")
        k.consts_loaded = k.count("consts_loaded", unit=16)
        k.plain_loaded = k.count("plain_loaded", unit=16)
        k.split_loaded = k.count("split_loaded", unit=16)
        k.out_stored = k.count("out_stored", unit=16)
        k.a_last = k.count("a_last", unit=16)
        k.m_bias = k.count("m_bias", unit=16)
        k.a_ctx = [k.count(f"a_ctx{p}", unit=16) for p in range(2)]
        k.a_mask = [k.count(f"a_mask{p}", unit=16) for p in range(2)]
        k.b_ctx_t = [k.count(f"b_ctx_t{p}", unit=16) for p in range(2)]
        k.b_ctx = [k.count(f"b_ctx{p}", unit=16) for p in range(2)]
        k.t_rows = [k.count(f"t_rows{p}", unit=16) for p in range(2)]
        k.t_raw = [k.count(f"t_raw{p}", unit=16) for p in range(2)]
        k.m_rows = [k.count(f"m_rows{p}", unit=16) for p in range(2)]
        k.g_shared = [k.count(f"g_shared{p}", unit=16) for p in range(2)]
        k.g_load = [k.count(f"g_load{p}", unit=16) for p in range(2)]
        k.t_stored = [k.count(f"t_stored{p}", 1, unit=16) for p in range(2)]
        k.x_loaded = [k.count(f"x_loaded{g}", unit=16) for g in range(G)]

        start(k)
        stages = [stage_heads_attention, stage_recurrence, stage_first_mixture, stage_single_attention,
                  stage_causal_attention, stage_second_mixture]
        for s in STAGES:
            k.stage = stages[s].__name__
            k.first = s == STAGES[0]
            stages[s](k)

        with nc.Block() as block:
            @block.sync
            def _(sp):
                sp.dma_start(dram["out"].rearrange("(c p) t -> p c t", p=P), k.x_t[:, :, :]).then_inc(k.out_stored.sem, 16)
                sp.wait_ge(k.out_stored.sem, k.out_stored.at(1))


def columns(a):
    return np.ascontiguousarray(a.reshape(-1, P).T)


def lay_out(i):
    T_ = np.transpose
    a = {
        "x_t": i["x"].reshape(T, D).T, "consts": const_table(),
        "ctx_t": T_(i["ctx_1024"], (0, 2, 1)), "ctx_last_t": i["ctx_1024"][:, SK - 1, :].T, "ctx": i["ctx_1024"], "mask": i["mask_BxSxS2_ik1"],
        "L0_xattn_wq_t": i["L0_xattn_wq"].T, "L0_xattn_wk_t": i["L0_xattn_wk"].T, "L0_xattn_wv_t": i["L0_xattn_wv"].T,
        "L0_xattn_wout_t": i["L0_xattn_w_out"].T,
        "L0_attn_W1": i["L0_attn_W1"], "L0_attn_W2": i["L0_attn_W2"], "L0_ffn_Wg": i["L0_ffn_Wg"],
        "L1_xattn_wq": i["L1_xattn_wq"], "L1_xattn_wk_t": i["L1_xattn_wk"].T, "L1_xattn_wv": i["L1_xattn_wv"],
        "L1_attn_Wq_t": i["L1_attn_Wq"].T, "L1_attn_Wk_t": i["L1_attn_Wk"].T, "L1_attn_Wv_t": i["L1_attn_Wv"].T,
        "L1_ffn_gate_w_t": i["L1_ffn_gate_w"].T,
        "L1_ffn_gate_bias": np.broadcast_to(i["L1_ffn_gate_bias"][None, :], (P, E1)),
    }
    for n in ["L0_attn_b1", "L0_attn_b2", "L0_attn_init_h", "L1_xattn_bq", "L1_xattn_bk", "L1_xattn_bv", "L1_attn_bq", "L1_attn_bk", "L1_attn_bv"]:
        a[n] = columns(i[n])
    w1 = np.concatenate([i["L0_ffn_W1"], i["L0_ffn_Ws1"][None]]).reshape(E0 + 1, C, P, F0)
    w2 = np.concatenate([i["L0_ffn_W2"], i["L0_ffn_Ws2"][None]]).reshape(E0 + 1, 2, F0 // P // 2, P, D)
    w2 = T_(w2, (0, 1, 3, 2, 4)).reshape(E0 + 1, 2, P, F0)
    a["m0_w"] = np.concatenate([w1, w2], axis=1).reshape(-1, P, F0)
    a["m0_b1"] = columns(np.concatenate([i["L0_ffn_b1"], i["L0_ffn_bs1"][None]]))
    a["m0_b2"] = np.concatenate([i["L0_ffn_b2"], i["L0_ffn_bs2"][None]])
    up = [np.concatenate([i[f"L1_ffn_{n}"], i[f"L1_ffn_{m}"][None]]) for n, m in (("w1", "ws1"), ("w3", "ws3"))]
    up = [T_(w, (0, 2, 1)).reshape(E1 + 1, C, P, I1) for w in up]
    down = np.concatenate([i["L1_ffn_w2"], i["L1_ffn_ws2"][None]])
    down = T_(down, (0, 2, 1)).reshape(E1 + 1, 2, IH, D)
    down = np.concatenate([down, np.zeros((E1 + 1, 2, P - IH, D), down.dtype)], axis=2)
    a["m1_w"] = np.concatenate([T_(w, (0, 2, 1, 3)).reshape(E1 + 1, P, -1) for w in (*up, down)], axis=2)
    return {n: np.ascontiguousarray(v) for n, v in a.items()}


def kernel(**inputs):
    import concourse.bacc as bacc
    from concourse.bass_utils import run_bass_kernel_spmd

    arrays = lay_out({n: np.asarray(v) for n, v in inputs.items()})
    nc = bacc.Bacc("TRN2", target_bir_lowering=False, num_devices=1)
    dram = {n: nc.dram_tensor(f"in_{n}", a.shape, mybir.dt.from_np(a.dtype), kind="ExternalInput").ap() for n, a in arrays.items()}
    dram["out"] = nc.dram_tensor("out_0_dram", [D, T], F32, kind="ExternalOutput").ap()
    build(nc, dram)
    r = run_bass_kernel_spmd(nc, [{f"in_{n}": a for n, a in arrays.items()}], core_ids=[0])
    return np.ascontiguousarray(r.results[0]["out_0_dram"].T).reshape(B, S, D)
```

```python
from contextlib import ExitStack

import numpy as np

import concourse.bass as bass
from concourse import mybir

F32 = mybir.dt.float32
BF16 = mybir.dt.bfloat16
F16 = mybir.dt.float16
I32 = mybir.dt.int32
U32 = mybir.dt.uint32
ALU = mybir.AluOpType
ACT = mybir.ActivationFunctionType
AX = mybir.AxisListType

P = 128
B, S, D = 64, 32, 256
SK = 257
T = B * S
C = D // P
G = 4
TG = T // G
NT = T // P
H, HD = 16, 16
HC = P // HD
DIN = 512
J = DIN // P
E0, F0, K0 = 8, 1024, 2
E1, I1, K1 = 16, 192, 4
IH = I1 // 2
EPS = 1e-5
WS = 256.0
NS = 64.0
HS = 16.0
MASKED = -1e30
TINY = 1e-37

STAGES = range(6)


class Count:

    def __init__(self, sem, credit=0, unit=1):
        self.sem, self.credit, self.unit, self.base = sem, credit, unit, 0

    def at(self, n):
        return (n + self.credit + self.base) * self.unit

    def next(self):
        self.base += 1
        return self.at(0)


class Core:

    def __init__(self, nc, ctx, dram):
        self.nc, self.ctx, self.dram = nc, ctx, dram
        self.counts = []

    def sb(self, name, shape, dt=F32, ctx=None):
        if ctx is not None:
            name = f"{self.stage}_{name}"
        return (ctx or self.ctx).enter_context(self.nc.sbuf_tensor(name, shape, dt))

    def count(self, name, credit=0, unit=1):
        self.counts.append(Count(self.ctx.enter_context(self.nc.semaphore(name)), credit, unit))
        return self.counts[-1]


def group(g):
    return bass.ds(g * TG, TG)


def tiles_of(g):
    return slice(g * TG // P, (g + 1) * TG // P)


CONST = {"ident": P, "head_block": HC * S, "repeat": P, "causal": P, "iota": P, "earlier": 16, "before": P, "token": NT, "sequence": P // S}


def const_table():
    p = np.arange(P)[:, None]
    c = np.arange(P)[None, :]
    g = np.arange(16)[None, :]
    parts = {
        "ident": p == c,
        "head_block": p // HD == np.arange(HC * S)[None, :] // S,
        "repeat": p == c % S,
        "causal": np.where((p // S == c // S) & (c <= p), 0.0, MASKED),
        "iota": np.broadcast_to(c, (P, P)),
        "earlier": np.broadcast_to(g % 4 < g // 4, (P, 16)),
        "before": p < c,
        "token": p + P * np.arange(NT)[None, :],
        "sequence": p // S == np.arange(P // S)[None, :],
    }
    return np.concatenate([np.asarray(parts[n], np.float32) for n in CONST], axis=1)


def start(k):
    nc, d = k.nc, k.dram
    with nc.Block() as block:
        @block.sync
        def _(sp):
            for g in range(G):
                sp.dma_start(k.x_t[:, :, group(g)], d["x_t"].rearrange("(c p) t -> p c t", p=P)[:, :, group(g)]).then_inc(k.x_loaded[g].sem, 16)
            sp.dma_start(k.consts[:, :], d["consts"]).then_inc(k.consts_loaded.sem, 16)

        @block.gpsimd
        def _(pool):
            for s in k.counts:
                if s.credit:
                    pool.sem_inc(s.sem, s.credit * s.unit)

        @block.vector
        def _(dve):
            dve.memset(k.ones_mean[:, :], 1.0 / D)
            dve.memset(k.ones_row[:, :], 1.0)
            dve.memset(k.ones_h[:, :], 1.0)
            dve.memset(k.eps[:, :], EPS)


def stage_weights(k, ctx, plain, split):
    k.plain, k.split = plain, split
    for n in plain:
        k.w[n] = k.sb(f"w_{n}", [P, k.dram[n].shape[0] // P, k.dram[n].shape[1]], ctx=ctx)
    for n in split:
        shape = [P, k.dram[n].shape[0] // P, k.dram[n].shape[1]]
        k.w[n] = (k.sb(f"wh_{n}", shape, F16, ctx=ctx), k.sb(f"wl_{n}", shape, F16, ctx=ctx))


def layernorm(k):
    nc = k.nc
    ps = k.ps
    with ExitStack() as ctx, nc.Block() as block:
        xc = k.sb("ln_xc", [P, C, T], ctx=ctx)
        sq = k.sb("ln_sq", [P, C, T], ctx=ctx)
        sd = k.sb("ln_sd", [P, NT], ctx=ctx)
        diag = k.sb("ln_diag", [P, NT, P], ctx=ctx)
        raw = [k.sb(f"raw_{n}", [P, k.dram[n].shape[0] // P, k.dram[n].shape[1]], ctx=ctx) for n in k.split]

        @block.sync
        def _(sp):
            for n, t in zip(k.split, raw):
                sp.dma_start(t[:, :, :], k.dram[n].rearrange("(c p) n -> p c n", p=P)).then_inc(k.split_loaded.sem, 16)
            for n in k.plain:
                sp.dma_start(k.w[n][:, :, :], k.dram[n].rearrange("(c p) n -> p c n", p=P)).then_inc(k.plain_loaded.sem, 16)
            sp.wait_ge(k.plain_loaded.sem, k.plain_loaded.at(len(k.plain)))

        @block.tensor
        def _(pe):
            for g in range(G):
                if k.first:
                    pe.wait_ge(k.x_loaded[g].sem, 16)
                for c in range(C):
                    last = pe.matmul(ps[:, g, :], k.ones_mean[:, :], k.x_t[:, c, group(g)], start=(c == 0), stop=(c == C - 1))
                last.then_inc(k.mean_ready.sem, 1)
            for g in range(G):
                pe.wait_ge(k.squared.sem, k.squared.at(g + 1))
                for c in range(C):
                    last = pe.matmul(ps[:, g, :], k.ones_mean[:, :], sq[:, c, group(g)], start=(c == 0), stop=(c == C - 1))
                last.then_inc(k.var_ready.sem, 1)
            for g in range(G):
                pe.wait_ge(k.diag_ready.sem, k.diag_ready.at(g + 1))
                pe.matmul(ps[:, G + g, :], k.ones_mean[:, :], diag[:, tiles_of(g), :].rearrange("p t n -> p (t n)"), start=True, stop=True).then_inc(k.inv_spread.sem, 1)

        @block.scalar
        def _(act):
            for g in range(G):
                act.wait_ge(k.centred.sem, k.centred.at(C * (g + 1)))
                act.activation(sq[:, :, group(g)], xc[:, :, group(g)], ACT.Square).then_inc(k.squared.sem, 1)
            for g in range(G):
                act.wait_ge(k.var_kept.sem, k.var_kept.at(g + 1))
                act.activation(sd[:, tiles_of(g)], sd[:, tiles_of(g)], ACT.Sqrt, bias=k.eps[:, 0:1]).then_inc(k.std_ready.sem, 1)
            for g in range(G):
                act.wait_ge(k.normed.sem, k.normed.at(g + 1))
                act.activation(k.n_h[:, :, group(g)], xc[:, :, group(g)], ACT.Copy).then_inc(k.high_ready.sem, 1)

        @block.vector
        def _(dve):
            for g in range(G):
                dve.wait_ge(k.mean_ready.sem, k.mean_ready.at(g + 1))
                for c in range(C):
                    dve.tensor_tensor(xc[:, c, group(g)], k.x_t[:, c, group(g)], ps[:, g, :], ALU.subtract).then_inc(k.centred.sem, 1)
            if k.first:
                dve.wait_ge(k.consts_loaded.sem, 16)

            def keep(g):
                dve.wait_ge(k.var_ready.sem, k.var_ready.at(g + 1))
                dve.tensor_tensor(diag[:, tiles_of(g), :], k.c["ident"].unsqueeze(1).broadcast_to([P, TG // P, P]),
                                  ps[:, g, :].rearrange("p (t n) -> p t n", n=P), ALU.mult).then_inc(k.var_kept_diag.sem, 1)
                dve.wait_ge(k.var_kept_diag.sem, k.var_kept_diag.at(g + 1))
                dve.tensor_reduce(sd[:, tiles_of(g)], diag[:, tiles_of(g), :], AX.X, ALU.add).then_inc(k.var_kept.sem, 1)

            def invert(g):
                dve.wait_ge(k.std_ready.sem, k.std_ready.at(g + 1))
                dve.reciprocal(sd[:, tiles_of(g)], sd[:, tiles_of(g)]).then_inc(k.inv_ready.sem, 1)
                dve.wait_ge(k.inv_ready.sem, k.inv_ready.at(g + 1))
                dve.tensor_tensor(diag[:, tiles_of(g), :], k.c["ident"].unsqueeze(1).broadcast_to([P, TG // P, P]),
                                  sd[:, tiles_of(g)].unsqueeze(2).broadcast_to([P, TG // P, P]), ALU.mult).then_inc(k.diag_ready.sem, 1)

            def scale(g):
                dve.wait_ge(k.inv_spread.sem, k.inv_spread.at(g + 1))
                dve.wait_ge(k.squared.sem, k.squared.at(g + 1))
                for c in range(C):
                    last = dve.scalar_tensor_tensor(xc[:, c, group(g)], xc[:, c, group(g)], NS * D, ps[:, G + g, :], ALU.mult, ALU.mult)
                last.then_inc(k.normed.sem, 1)
            keep(0)
            for g in range(G):
                if g + 1 < G:
                    keep(g + 1)
                invert(g)
                if g > 0:
                    scale(g - 1)
            scale(G - 1)
            for g in range(G // 2, G):
                dve.wait_ge(k.normed.sem, k.normed.at(g + 1))
                dve.wait_ge(k.high_ready.sem, k.high_ready.at(g + 1))
                dve.tensor_tensor(k.n_l[:, :, group(g)], xc[:, :, group(g)], k.n_h[:, :, group(g)], ALU.subtract)
            if k.first:
                dve.tensor_copy(k.ident_h[:, :], k.c["ident"])
                dve.tensor_copy(k.before_h[:, :], k.c["before"])
                dve.tensor_copy(k.ident_bf[:, :], k.c["ident"])
                dve.tensor_copy(k.repeat_bf[:, :], k.c["repeat"][0:S, :])
                dve.tensor_copy(k.causal_bf[:, :], k.c["causal"])

        @block.gpsimd
        def _(pool):
            pool.wait_ge(k.split_loaded.sem, k.split_loaded.at(len(k.split)))
            for n, t in zip(k.split, raw):
                h, l = k.w[n]
                pool.tensor_scalar(h[:, :, :], t[:, :, :], WS, 1.0, ALU.mult, ALU.mult)
                pool.tensor_scalar(t[:, :, :], t[:, :, :], WS, 1.0, ALU.mult, ALU.mult).then_inc(k.split_high.sem, 1)
                pool.wait_ge(k.split_high.sem, k.split_high.next())
                pool.tensor_tensor(l[:, :, :], t[:, :, :], h[:, :, :], ALU.subtract)
            for g in range(G // 2):
                pool.wait_ge(k.high_ready.sem, k.high_ready.at(g + 1))
                pool.tensor_tensor(k.n_l[:, :, group(g)], xc[:, :, group(g)], k.n_h[:, :, group(g)], ALU.subtract)
    for s, n in ((k.mean_ready, G), (k.squared, G), (k.var_ready, G), (k.std_ready, G), (k.inv_ready, G), (k.diag_ready, G), (k.inv_spread, G), (k.var_kept, G), (k.var_kept_diag, G), (k.centred, C * G),
                 (k.normed, G), (k.high_ready, G), (k.split_loaded, len(k.split)), (k.plain_loaded, len(k.plain))):
        s.base += n


def three(w, x):
    return ((w[0], x[0]), (w[0], x[1]), (w[1], x[0]))


def project(k, weight, src, finish_block, n_in=C, n_out=C, rows=P):
    nc, ps = k.nc, k.ps
    pairs = three(weight, src) if isinstance(weight, tuple) else ((weight, src),)
    with nc.Block() as block:
        @block.tensor
        def _(pe):
            for g in range(G):
                for m in range(n_out):
                    products = [(w, x, c) for w, x in pairs for c in range(n_in)]
                    for n, (w, x, c) in enumerate(products):
                        last = pe.matmul(ps[:, g * n_out + m, :], w[:, c, m * P:(m + 1) * P], x[:, c, group(g)],
                                         start=(n == 0), stop=(n == len(products) - 1))
                    last.then_inc(k.projected.sem, 1)
        finish_block(block)
    k.projected.base += G * n_out


def stage_heads_attention(k):
    nc, ps, c_ = k.nc, k.ps, k.c
    with ExitStack() as stage:
        stage_weights(k, stage, ["L0_xattn_wout_t"], ["L0_xattn_wq_t", "L0_xattn_wk_t", "L0_xattn_wv_t"])
        layernorm(k)
        heads_attention(k, stage)


def heads_attention(k, stage):
    nc, ps, c_ = k.nc, k.ps, k.c
    KR = SK - 1
    n = (k.n_h, k.n_l)
    q_t = k.sb("q_t", [P, C, T], ctx=stage)
    o_t = k.sb("o_t", [P, C, T], ctx=stage)
    last_t = k.sb("last_t", [P, C, B], ctx=stage)
    last_s = [k.sb(f"last_s{x}", [P, C, B], F16, ctx=stage) for x in range(2)]
    v_last = k.sb("v_last", [P, C, B], ctx=stage)

    def take_q(block):
        @block.sync
        def _(sp):
            sp.dma_start(last_t[:, :, :], k.dram["ctx_last_t"].rearrange("(c p) b -> p c b", p=P)).then_inc(k.a_last.sem, 16)

        @block.scalar
        def _(act):
            for g in range(G):
                for m in range(C):
                    act.wait_ge(k.projected.sem, k.projected.at(g * C + m + 1))
                    act.activation(q_t[:, m, group(g)], ps[:, g * C + m, :], ACT.Copy, scale=HD ** -0.5 / (WS * NS))

        @block.vector
        def _(dve):
            dve.wait_ge(k.a_last.sem, 16)
            dve.tensor_scalar(last_t[:, :, :], last_t[:, :, :], NS, None, ALU.mult).then_inc(k.a_split.sem, 1)
            dve.wait_ge(k.a_split.sem, 1)
            dve.tensor_copy(last_s[0][:, :, :], last_t[:, :, :]).then_inc(k.a_split.sem, 1)
            dve.wait_ge(k.a_split.sem, 2)
            dve.tensor_tensor(last_s[1][:, :, :], last_t[:, :, :], last_s[0][:, :, :], ALU.subtract)
    project(k, k.w["L0_xattn_wq_t"], n, take_q)

    with ExitStack() as ctx:
        ctx_t = [k.sb(f"ctx_t{p}", [P, C, SK], ctx=ctx) for p in range(2)]
        ctx_c = [k.sb(f"ctx_c{p}", [P, C, KR], ctx=ctx) for p in range(2)]
        ctx_s = [[k.sb(f"ctx_s{p}{x}", [P, C, KR], F16, ctx=ctx) for x in range(2)] for p in range(2)]
        mask_i = [k.sb(f"mask_i{p}", [S, SK], I32, ctx=ctx) for p in range(2)]
        mask_b = [k.sb(f"mask_b{p}", [S, SK], BF16, ctx=ctx) for p in range(2)]
        k_t = [k.sb(f"k_t{p}", [P, C, SK], ctx=ctx) for p in range(2)]
        v = [k.sb(f"v{p}", [P, 2, D], ctx=ctx) for p in range(2)]
        q_blk = [k.sb(f"q_blk{p}", [P, C, HC * S], ctx=ctx) for p in range(2)]
        neg_max = k.sb("neg_max", [P, 2, 4], ctx=ctx)
        sums = k.sb("sums", [P, 2, 4], ctx=ctx)
        inv = k.sb("inv", [P, 2, 4], ctx=ctx)
        probs = [k.sb(f"probs{p}", [P, 4, SK], ctx=ctx) for p in range(2)]
        pn = k.sb("pn", [P, 4, KR], ctx=ctx)
        p_t = k.sb("p_t", [P, 2, 512], ctx=ctx)
        o_own = k.sb("o_own", [P, C, HC, S], ctx=ctx)
        o_sum = k.sb("o_sum", [P, C, S], ctx=ctx)
        KB, VB, TB, OB, SB = 0, 1, 2, 3, 4
        wk, wv = k.w["L0_xattn_wk_t"], k.w["L0_xattn_wv_t"]

        with nc.Block() as block:
            @block.sync
            def _(sp):
                def fetch(i, p):
                    b = 2 * i + p
                    sp.wait_ge(k.a_centred.sem, k.a_centred.at(b - 1))
                    sp.dma_start(ctx_t[p][:, :, :], k.dram["ctx_t"][bass.ds(b, 1), :, :].rearrange("o (c p) n -> p (o c) n", p=P)).then_inc(k.a_ctx[p].sem, 16)
                    sp.wait_ge(k.a_maskb.sem, k.a_maskb.at(b - 1))
                    sp.dma_start(mask_i[p][:, :], k.dram["mask"][bass.ds(b, 1), :, :].rearrange("o s n -> (o s) n")).then_inc(k.a_mask[p].sem, 16)
                with sp.Fori(0, B // 2) as i:
                    fetch(i, 0)
                    fetch(i, 1)

            @block.tensor
            def _(pe):
                for m in range(C):
                    products = [(w, x, c) for w, x in three(wv, last_s) for c in range(C)]
                    for n_, (w, x, c) in enumerate(products):
                        last = pe.matmul(ps[:, SB, m * B:(m + 1) * B], w[:, c, m * P:(m + 1) * P], x[:, c, :], start=(n_ == 0), stop=(n_ == len(products) - 1))
                last.then_inc(k.a_vlast.sem, 1)

                def keys(i, p):
                    b = 2 * i + p
                    pe.wait_ge(k.a_low.sem, k.a_low.at(b + 1))
                    pe.wait_ge(k.a_kcopied.sem, k.a_kcopied.at(b))
                    for m in range(C):
                        products = [(w, x, c) for w, x in three(wk, ctx_s[p]) for c in range(C)]
                        for n_, (w, x, c) in enumerate(products):
                            last = pe.matmul(ps[:, KB, m * KR:(m + 1) * KR], w[:, c, m * P:(m + 1) * P], x[:, c, :], start=(n_ == 0), stop=(n_ == len(products) - 1))
                    last.then_inc(k.a_kproj.sem, 1)

                def values(i, p):
                    b = 2 * i + p
                    pe.wait_ge(k.a_vcopied.sem, k.a_vcopied.at(b))
                    for r in range(2):
                        products = [(w, x, c) for w, x in three(wv, ctx_s[p]) for c in range(C)]
                        for n_, (w, x, c) in enumerate(products):
                            last = pe.matmul(ps[:, VB, r * D:(r + 1) * D], x[:, c, r * P:(r + 1) * P], w[:, c, :], start=(n_ == 0), stop=(n_ == len(products) - 1))
                    last.then_inc(k.a_keys_done.sem, 1)

                def scores(i, p):
                    b = 2 * i + p
                    pe.wait_ge(k.a_kcopied.sem, k.a_kcopied.at(b + 1))
                    pe.wait_ge(k.a_qblk.sem, k.a_qblk.at(b + 1))
                    pe.wait_ge(k.a_maskb.sem, k.a_maskb.at(b + 1))
                    pe.wait_ge(k.a_exp.sem, k.a_exp.at(4 * b))
                    for j in range(4):
                        pe.matmul(ps[:, SB + j, 0:SK], k.repeat_bf[:, :], mask_b[p][:, :], start=True, stop=False)
                        last = pe.matmul(ps[:, SB + j, 0:SK], q_blk[p][:, j // 2, (j % 2) * P:(j % 2 + 1) * P], k_t[p][:, j // 2, :], start=False, stop=True)
                    last.then_inc(k.a_scored.sem, 1)

                def turn(i, p, r):
                    b = 2 * i + p
                    pe.wait_ge(k.a_normed.sem, k.a_normed.at(4 * (b + 1)))
                    pe.wait_ge(k.a_ptcopied.sem, k.a_ptcopied.at(2 * b + r))
                    for j in range(4):
                        last = pe.transpose(ps[:, TB, j * P:(j + 1) * P], pn[:, j, r * P:(r + 1) * P], c_["ident"])
                    last.then_inc(k.a_pt.sem, 1)

                def weigh(i, p):
                    b = 2 * i + p
                    pe.wait_ge(k.a_own.sem, k.a_own.at(b))
                    pe.wait_ge(k.a_vcopied.sem, k.a_vcopied.at(b + 1))
                    for m in range(C):
                        for r in range(2):
                            pe.wait_ge(k.a_ptcopied.sem, k.a_ptcopied.at(2 * b + r + 1))
                            last = pe.matmul(ps[:, OB, m * D:(m + 1) * D], v[p][:, r, m * P:(m + 1) * P], p_t[:, r, m * D:(m + 1) * D], start=(r == 0), stop=(r == 1))
                    last.then_inc(k.a_out.sem, 1)

                pe.wait_ge(k.a_vtaken.sem, 1)
                keys(0, 0)
                values(0, 0)
                scores(0, 0)
                keys(0, 1)
                values(0, 1)
                with pe.Fori(0, B // 2 - 1) as i:
                    for p in range(2):
                        scores(i + p, 1 - p)
                        turn(i, p, 0)
                        keys(i + 1, p)
                        turn(i, p, 1)
                        values(i + 1, p)
                        weigh(i, p)
                i = B // 2 - 1
                scores(i, 1)
                for p in range(2):
                    turn(i, p, 0)
                    turn(i, p, 1)
                    weigh(i, p)

            @block.scalar
            def _(act):
                act.preload_act_table(ACT.Exp)

                def high(i, p):
                    b = 2 * i + p
                    act.wait_ge(k.a_centred.sem, k.a_centred.at(b + 1))
                    act.wait_ge(k.a_keys_done.sem, k.a_keys_done.at(b - 1))
                    act.activation(ctx_s[p][0][:, :, :], ctx_c[p][:, :, :], ACT.Copy).then_inc(k.a_high.sem, 1)

                def take_keys(i, p):
                    b = 2 * i + p
                    act.wait_ge(k.a_kproj.sem, k.a_kproj.at(b + 1))
                    act.wait_ge(k.a_scored.sem, k.a_scored.at(b - 1))
                    act.activation(k_t[p][:, :, 0:KR], ps[:, KB, :].rearrange("p (c n) -> p c n", c=C), ACT.Copy, scale=1 / (WS * NS)).then_inc(k.a_kcopied.sem, 1)

                def take_values(i, p):
                    b = 2 * i + p
                    act.wait_ge(k.a_keys_done.sem, k.a_keys_done.at(b + 1))
                    act.wait_ge(k.a_out.sem, k.a_out.at(b - 1))
                    act.activation(v[p][:, :, :].rearrange("p r n -> p (r n)"), ps[:, VB, :], ACT.Copy, scale=1 / (WS * NS)).then_inc(k.a_vcopied.sem, 1)

                def softmax(i, p):
                    b = 2 * i + p
                    act.wait_ge(k.a_max.sem, k.a_max.at(b + 1))
                    act.wait_ge(k.a_normed.sem, k.a_normed.at(4 * (b - 1)))
                    for j in range(4):
                        act.activation(probs[p][:, j, :], ps[:, SB + j, 0:SK], ACT.Exp, bias=neg_max[:, p, j:j + 1], accum_out=sums[:, p, j:j + 1]).then_inc(k.a_exp.sem, 1)

                high(0, 0)
                high(0, 1)
                take_keys(0, 0)
                take_values(0, 0)
                high(1, 0)
                softmax(0, 0)
                take_keys(0, 1)
                take_values(0, 1)
                with act.Fori(0, B // 2 - 2) as i:
                    for p in range(2):
                        softmax(i + p, 1 - p)
                        take_keys(i + 1, p)
                        high(i + 1 + p, 1 - p)
                        take_values(i + 1, p)
                i = B // 2 - 2
                softmax(i, 1)
                take_keys(i + 1, 0)
                high(i + 1, 1)
                take_values(i + 1, 0)
                softmax(i + 1, 0)
                take_keys(i + 1, 1)
                take_values(i + 1, 1)
                softmax(i + 1, 1)

            @block.gpsimd
            def _(pool):
                def queries(i, p):
                    b = 2 * i + p
                    pool.wait_ge(k.a_scored.sem, k.a_scored.at(b - 1))
                    for c in range(C):
                        q = q_t[:, c, bass.ds(b * S, S)].unsqueeze(1).broadcast_to([P, HC, S])
                        last = pool.tensor_tensor(q_blk[p][:, c, :].rearrange("p (h q) -> p h q", h=HC), q, c_["head_block"].rearrange("p (h q) -> p h q", h=HC), ALU.mult)
                    last.then_inc(k.a_qblk.sem, 1)

                def low(i, p):
                    b = 2 * i + p
                    pool.wait_ge(k.a_high.sem, k.a_high.at(b + 1))
                    pool.tensor_tensor(ctx_s[p][1][:, :, :], ctx_c[p][:, :, :], ctx_s[p][0][:, :, :], ALU.subtract).then_inc(k.a_low.sem, 1)

                low(0, 0)
                queries(0, 0)
                with pool.Fori(0, B // 2 - 1) as i:
                    low(i, 1)
                    queries(i, 1)
                    low(i + 1, 0)
                    queries(i + 1, 0)
                low(B // 2 - 1, 1)
                queries(B // 2 - 1, 1)

            @block.vector
            def _(dve):
                for p in range(2):
                    dve.memset(k_t[p][:, :, KR:SK], 0.0)
                dve.wait_ge(k.a_vlast.sem, 1)
                dve.tensor_scalar(v_last[:, :, :].rearrange("p c b -> p (c b)"), ps[:, SB, 0:C * B], 1 / (WS * NS), None, ALU.mult).then_inc(k.a_vtaken.sem, 1)

                def prepare(i, p):
                    b = 2 * i + p
                    dve.wait_ge(k.a_ctx[p].sem, k.a_ctx[p].at(i + 1))
                    dve.wait_ge(k.a_low.sem, k.a_low.at(b - 1))
                    for c in range(C):
                        last = dve.tensor_scalar(ctx_c[p][:, c, :], ctx_t[p][:, c, 0:KR], ctx_t[p][:, c, KR:SK], NS, ALU.subtract, ALU.mult)
                    last.then_inc(k.a_centred.sem, 1)
                    dve.wait_ge(k.a_scored.sem, k.a_scored.at(b - 1))
                    dve.wait_ge(k.a_mask[p].sem, k.a_mask[p].at(i + 1))
                    dve.tensor_scalar(mask_b[p][:, :], mask_i[p][:, :], 1.0, MASKED, ALU.is_equal, ALU.mult).then_inc(k.a_maskb.sem, 1)

                def softmax(i, p):
                    b = 2 * i + p
                    dve.wait_ge(k.a_scored.sem, k.a_scored.at(b + 1))
                    dve.tensor_reduce(neg_max[:, p, :], ps[:, SB:SB + 4, 0:SK], AX.X, ALU.max, negate=True).then_inc(k.a_max.sem, 1)

                def normalise(i, p):
                    b = 2 * i + p
                    dve.wait_ge(k.a_exp.sem, k.a_exp.at(4 * (b + 1)))
                    dve.reciprocal(inv[:, p, :], sums[:, p, :]).then_inc(k.a_inv.sem, 1)
                    dve.wait_ge(k.a_inv.sem, k.a_inv.at(b + 1))
                    dve.wait_ge(k.a_pt.sem, k.a_pt.at(2 * b))
                    for j in range(4):
                        dve.tensor_scalar(pn[:, j, :], probs[p][:, j, 0:KR], inv[:, p, j:j + 1], None, ALU.mult).then_inc(k.a_normed.sem, 1)

                def turned(i, p, r):
                    b = 2 * i + p
                    dve.wait_ge(k.a_out.sem, k.a_out.at(b))
                    dve.wait_ge(k.a_pt.sem, k.a_pt.at(2 * b + r + 1))
                    dve.tensor_copy(p_t[:, r, :], ps[:, TB, :]).then_inc(k.a_ptcopied.sem, 1)

                def own(i, p):
                    b = 2 * i + p
                    dve.wait_ge(k.a_out.sem, k.a_out.at(b + 1))
                    for c in range(C):
                        last = dve.tensor_tensor(o_own[:, c, :, :], ps[:, OB, c * D:(c + 1) * D].rearrange("p (h q) -> p h q", h=HC),
                                                 c_["head_block"].rearrange("p (h q) -> p h q", h=HC), ALU.mult)
                    last.then_inc(k.a_own.sem, 1)
                    dve.wait_ge(k.a_own.sem, k.a_own.at(b + 1))
                    dve.tensor_reduce(o_sum[:, :, :], o_own[:, :, :, :].rearrange("p c h q -> p c q h"), AX.X, ALU.add).then_inc(k.a_osum.sem, 1)
                    dve.wait_ge(k.a_osum.sem, k.a_osum.at(b + 1))
                    dve.tensor_tensor(o_t[:, :, bass.ds(b * S, S)], o_sum[:, :, :], v_last[:, :, bass.ds(b, 1)].broadcast_to([P, C, S]), ALU.add)

                prepare(0, 0)
                prepare(0, 1)
                prepare(1, 0)
                softmax(0, 0)
                normalise(0, 0)
                with dve.Fori(0, B // 2 - 2) as i:
                    for p in range(2):
                        softmax(i + p, 1 - p)
                        turned(i, p, 0)
                        prepare(i + 1 + p, 1 - p)
                        turned(i, p, 1)
                        normalise(i + p, 1 - p)
                        own(i, p)
                i = B // 2 - 2
                for b in range(2 * i, B):
                    if b + 1 < B:
                        softmax((b + 1) // 2, (b + 1) % 2)
                    turned(b // 2, b % 2, 0)
                    if b + 3 < B:
                        prepare((b + 3) // 2, (b + 3) % 2)
                    turned(b // 2, b % 2, 1)
                    if b + 1 < B:
                        normalise((b + 1) // 2, (b + 1) % 2)
                    own(b // 2, b % 2)

    def add_out(block):
        @block.vector
        def _(dve):
            for g in range(G):
                for m in range(C):
                    dve.wait_ge(k.projected.sem, k.projected.at(g * C + m + 1))
                    dve.tensor_tensor(k.x_t[:, m, group(g)], k.x_t[:, m, group(g)], ps[:, g * C + m, :], ALU.add)
    project(k, k.w["L0_xattn_wout_t"], o_t, add_out)


def stage_recurrence(k):
    nc, ps = k.nc, k.ps
    with ExitStack() as ctx:
        stage_weights(k, ctx, ["L0_attn_W2", "L0_attn_b1", "L0_attn_b2", "L0_attn_init_h"], ["L0_attn_W1"])
        layernorm(k)
        w1, w2 = k.w["L0_attn_W1"], k.w["L0_attn_W2"]
        bias1, bias2, init = k.w["L0_attn_b1"], k.w["L0_attn_b2"], k.w["L0_attn_init_h"]
        bias_half = k.sb("bias_half", [P, J], ctx=ctx)
        g_init = k.sb("g_init", [P, 2, J], ctx=ctx)
        sig = [k.sb(f"sig{p}", [P, 3, TG], ctx=ctx) for p in range(2)]
        gate = [k.sb(f"gate{p}", [P, 2, TG], ctx=ctx) for p in range(2)]
        inv = [k.sb(f"ginv{p}", [P, TG], ctx=ctx) for p in range(2)]
        val = [k.sb(f"val{p}", [P, TG], ctx=ctx) for p in range(2)]
        hid = k.sb("hid", [P, J, TG], ctx=ctx)
        with nc.Block() as block:
            @block.tensor
            def _(pe):
                with pe.Fori(0, G) as g:
                    for j in range(J):
                        u = J * g + j
                        pe.wait_ge(k.r_sig.sem, k.r_sig.at(u - 1))
                        for part in range(3):
                            products = [(w, x, c) for w, x in three(w1, (k.n_h, k.n_l)) for c in range(C)]
                            for n, (w, x, c) in enumerate(products):
                                last = pe.matmul(ps[:, 3 * (j % 2) + part, :], w[:, c, part * DIN + j * P:part * DIN + (j + 1) * P],
                                                 x[:, c, group(g)], start=(n == 0), stop=(n == len(products) - 1))
                        last.then_inc(k.r_proj.sem, 1)
                    pe.wait_ge(k.r_added.sem, k.r_added.at(g))
                    for m in range(C):
                        for j in range(J):
                            pe.wait_ge(k.r_scan.sem, k.r_scan.at(J * g + j + 1))
                            last = pe.matmul(ps[:, 6 + m, :], w2[:, j, m * P:(m + 1) * P], hid[:, j, :], start=(j == 0), stop=(j == J - 1))
                    last.then_inc(k.r_out.sem, 1)

            @block.scalar
            def _(act):
                act.activation(g_init[:, 0, :], init[:, 0, :], ACT.Sigmoid).then_inc(k.r_init.sem, 1)
                act.wait_ge(k.r_init.sem, 2)
                with act.Fori(0, G) as g:
                    for j in range(J):
                        u = J * g + j
                        act.wait_ge(k.r_proj.sem, k.r_proj.at(u + 1))
                        act.wait_ge(k.r_scan.sem, k.r_scan.at(u - 1))
                        for part in range(3):
                            act.activation(sig[j % 2][:, part, :], ps[:, 3 * (j % 2) + part, :], ACT.Sigmoid, scale=1 / (WS * NS), bias=bias1[:, 0, part * J + j:part * J + j + 1])
                        act.activation(val[j % 2][:, :], ps[:, 3 * (j % 2), :], ACT.Identity, scale=1 / (WS * NS), bias=bias_half[:, j:j + 1]).then_inc(k.r_sig.sem, 1)

            @block.vector
            def _(dve):
                dve.tensor_scalar(bias_half[:, :], bias1[:, 0, 0:J], 0.5, None, ALU.add).then_inc(k.r_init.sem, 1)
                dve.wait_ge(k.r_init.sem, k.r_init.at(2))
                dve.scalar_tensor_tensor(g_init[:, 1, :], init[:, 0, :], 0.5, g_init[:, 0, :], ALU.add, ALU.max).then_inc(k.r_init.sem, 1)
                with dve.Fori(0, G) as g:
                    for j in range(J):
                        u = J * g + j
                        p = j % 2
                        sg, sf, si = (sig[p][:, n, :] for n in range(3))
                        dve.wait_ge(k.r_sig.sem, k.r_sig.at(u + 1))
                        dve.tensor_scalar(gate[p][:, 0, :], sf, TINY, None, ALU.max).then_inc(k.r_floor.sem, 1)
                        dve.tensor_tensor(val[p][:, :], val[p][:, :], sg, ALU.max)
                        dve.wait_ge(k.r_floor.sem, k.r_floor.at(u + 1))
                        dve.scalar_tensor_tensor(gate[p][:, 1, :], si, TINY, gate[p][:, 0, :], ALU.max, ALU.add).then_inc(k.r_sum.sem, 1)
                        dve.wait_ge(k.r_sum.sem, k.r_sum.at(u + 1))
                        dve.reciprocal(inv[p][:, :], gate[p][:, 1, :]).then_inc(k.r_inv.sem, 1)
                        dve.wait_ge(k.r_inv.sem, k.r_inv.at(u + 1))
                        dve.scalar_tensor_tensor(gate[p][:, 1, :], si, TINY, inv[p][:, :], ALU.max, ALU.mult)
                        dve.tensor_tensor(gate[p][:, 0, :], gate[p][:, 0, :], inv[p][:, :], ALU.mult).then_inc(k.r_gates.sem, 1)
                        dve.wait_ge(k.r_gates.sem, k.r_gates.at(u + 1))
                        dve.tensor_tensor(val[p][:, :], val[p][:, :], gate[p][:, 1, :], ALU.mult).then_inc(k.r_valued.sem, 1)
                        dve.wait_ge(k.r_valued.sem, k.r_valued.at(u + 1))
                        first_val, first_coef = val[p][:, 0:TG:S], gate[p][:, 0, 0:TG:S]
                        dve.scalar_tensor_tensor(first_val, first_coef, g_init[:, 1, j:j + 1], first_val, ALU.mult, ALU.add).then_inc(k.r_first.sem, 1)
                        dve.wait_ge(k.r_first.sem, k.r_first.at(2 * u + 1))
                        dve.tensor_scalar(first_coef, first_coef, 0.0, None, ALU.mult).then_inc(k.r_first.sem, 1)
                        dve.wait_ge(k.r_first.sem, k.r_first.at(2 * u + 2))
                        dve.wait_ge(k.r_out.sem, k.r_out.at(g))
                        dve.tensor_tensor_scan(hid[:, j, :], gate[p][:, 0, :], val[p][:, :], 0.0, ALU.mult, ALU.add).then_inc(k.r_scan.sem, 1)
                    dve.wait_ge(k.r_out.sem, k.r_out.at(g + 1))
                    for m in range(C):
                        x = k.x_t[:, m, group(g)]
                        last = dve.scalar_tensor_tensor(x, ps[:, 6 + m, :], bias2[:, 0, m:m + 1], x, ALU.add, ALU.add)
                    last.then_inc(k.r_added.sem, 1)


def top8(k, dve, values, v8, i8, i8f):
    for t in range(NT):
        last = dve.max(v8[:, t, :], values[:, t, :])
    last.then_inc(k.m_chain.sem, 1)
    dve.wait_ge(k.m_chain.sem, k.m_chain.next())
    for t in range(NT):
        last = dve.max_index(i8[:, t, :], v8[:, t, :], values[:, t, :])
    last.then_inc(k.m_chain.sem, 1)
    dve.wait_ge(k.m_chain.sem, k.m_chain.next())
    dve.tensor_copy(i8f[:, :, :], i8[:, :, :]).then_inc(k.m_chain.sem, 1)
    dve.wait_ge(k.m_chain.sem, k.m_chain.next())


class Mixture:

    def __init__(self, n, experts, chosen, blocks, width, rows, hidden, depth, gated, shared_weight):
        self.n, self.E, self.K, self.blocks, self.width = n, experts, chosen, blocks, width
        self.rows, self.hidden, self.depth, self.gated, self.shared_weight = rows, hidden, depth, gated, shared_weight
        self.pieces = 1 if gated else 2
        self.tiles = T * chosen // P + experts - 1
        self.feeds = blocks * experts // NT


MIX0 = Mixture(0, E0, K0, 4, F0, P, F0, 1, False, 0.1)
MIX1 = Mixture(1, E1, K1, 1, 2 * C * I1 + 2 * D, IH, 2 * P, 2, True, 1.0)
MAX_TILES = max(MIX0.tiles, MIX1.tiles)
AT_ONCE = 5
FC = F0 // P


class Routing:

    def __init__(self, k, mix, ctx):
        self.w = k.sb("r_w", [P, mix.K, NT], ctx=ctx)
        self.choice = k.sb("r_choice", [P, NT, 8], ctx=ctx)
        self.slot = k.sb("r_slot", [P, NT, mix.K], I32, ctx=ctx)
        self.table = k.sb("r_table", [P, mix.tiles], ctx=ctx)
        self.expert = k.sb("r_expert", [P, mix.tiles], I32, ctx=ctx)


def route(k, mix, wg, wh, wl, scores, choose, r):
    nc, ps, c_ = k.nc, k.ps, k.c
    E, K, NTL = mix.E, mix.K, mix.tiles
    LB, PB, SB = 7, 6, 5
    with ExitStack() as ctx, nc.Block() as block:
        hot = k.sb("hot", [P, K, E, NT], ctx=ctx)
        any_h = k.sb("any_h", [P, E, NT], F16, ctx=ctx)
        total = k.sb("total", [P, E, NT], ctx=ctx)
        later = k.sb("later", [P, E, NT], ctx=ctx)
        upto = k.sb("upto", [P, E, NT], ctx=ctx)
        place = k.sb("place", [P, E, NT], ctx=ctx)
        tmp = k.sb("tmp", [P, E, NT], ctx=ctx)
        need_i = k.sb("need_i", [P, E], I32, ctx=ctx)
        need = k.sb("need", [P, E], ctx=ctx)
        ones_e = k.sb("ones_e", [P, E], ctx=ctx)
        ends = k.sb("ends", [P, E], ctx=ctx)
        begins = k.sb("begins", [P, E], ctx=ctx)
        slot_f = k.sb("slot_f", [P, K, NT], ctx=ctx)
        lo_i = k.sb("lo_i", [P, K, NT], I32, ctx=ctx)
        hi_i = k.sb("hi_i", [P, K, NT], I32, ctx=ctx)
        lo_f = k.sb("lo_f", [P, K, NT], ctx=ctx)
        hi_f = k.sb("hi_f", [P, K, NT], ctx=ctx)
        ends_le = k.sb("ends_le", [P, NTL, E], ctx=ctx)
        exp_f = k.sb("exp_f", [P, NTL + AT_ONCE - 1], ctx=ctx)
        packed = k.sb("packed", [P, NTL], ctx=ctx)
        hot_lo = [k.sb(f"hot_lo{p}", [P, P], F16, ctx=ctx) for p in range(2)]
        hot_hi = [k.sb(f"hot_hi{p}", [P, NTL], F16, ctx=ctx) for p in range(2)]
        iota_h = k.sb("iota_h", [P, P], F16, ctx=ctx)
        raw = [k.sb(f"shared_raw{p}", [P, mix.width], ctx=ctx) for p in range(2)]
        row_sb = [k.sb(f"row_sb{p}", [P, 2 * D], F16, ctx=ctx) for p in range(2)]

        @block.tensor
        def _(pe):
            for t in range(NT):
                products = [(w, x, c) for w, x in three(wg, (k.n_h, k.n_l)) for c in range(C)]
                for n, (w, x, c) in enumerate(products):
                    last = pe.matmul(ps[:, LB, t * E:(t + 1) * E], x[:, c, t * P:(t + 1) * P], w[:, c, :], start=(n == 0), stop=(n == len(products) - 1))
            last.then_inc(k.m_logits.sem, 1)
            for t in range(NT):
                pe.wait_ge(k.m_rowcopied.sem, k.m_rowcopied.at(max(t - 1, 0)))
                row = ps[:, t % 2, 0:D].bitcast(F16)
                for x, n in enumerate((k.n_h, k.n_l)):
                    for c in range(C):
                        last = pe.transpose(row[:, (x * C + c) * P:(x * C + c + 1) * P], n[:, c, t * P:(t + 1) * P], k.ident_h[:, :])
                last.then_inc(k.m_rowt.sem, 1)
            pe.wait_ge(k.m_counted.sem, k.m_counted.at(1))
            pe.matmul(ps[:, PB, 0:E * NT], k.before_h[:, :], any_h[:, :, :].rearrange("p e t -> p (e t)"), start=True, stop=True)
            pe.matmul(ps[:, PB, E * NT:2 * E * NT], k.ones_h[:, :], any_h[:, :, :].rearrange("p e t -> p (e t)"), start=True, stop=True).then_inc(k.m_prefixed.sem, 1)

            def add_to_table(u, p, first, final):
                pe.wait_ge(k.m_onehot.sem, k.m_onehot.at(u + 1))
                pe.matmul(ps[:, SB, 0:NTL], hot_lo[p][:, :], hot_hi[p][:, :], start=first, stop=final).then_inc(k.m_placed.sem, 1)
            for kk in range(K):
                add_to_table(kk, kk % 2, kk == 0, False)
            with pe.Fori(1, NT - 1) as t:
                for kk in range(K):
                    add_to_table(t * K + kk, kk % 2, False, False)
            for kk in range(K):
                add_to_table((NT - 1) * K + kk, kk % 2, False, kk == K - 1)

        @block.scalar
        def _(act):
            scores(act)
            for t in range(NT):
                act.wait_ge(k.m_rowt.sem, k.m_rowt.at(t + 1))
                if t >= 2:
                    act.wait_ge(k.m_rows[t % 2].sem, k.m_rows[t % 2].at(t // 2))
                act.activation(row_sb[t % 2][:, :], ps[:, t % 2, 0:D].bitcast(F16), ACT.Copy).then_inc(k.m_rowcopied.sem, 1)

        @block.sync
        def _(sp):
            first = mix.E * mix.blocks
            for q in range(mix.blocks):
                sp.wait_ge(k.t_wlow.sem, k.t_wlow.at(max(q - 1, 0)))
                sp.dma_start(raw[q % 2][:, :], k.dram[f"m{mix.n}_w"][first + q, :, :]).then_inc(k.t_raw[q % 2].sem, 16)
            for t in range(NT):
                sp.wait_ge(k.m_rowcopied.sem, k.m_rowcopied.at(t + 1))
                sp.dma_start(k.n_rows[t * P:(t + 1) * P, :], row_sb[t % 2][:, :]).then_inc(k.m_rows[t % 2].sem, 16)
            for p in range(2):
                sp.wait_ge(k.m_rows[p].sem, k.m_rows[p].at(NT // 2))

        @block.gpsimd
        def _(pool):
            first = mix.E * mix.blocks
            for q in range(mix.blocks):
                pool.wait_ge(k.t_raw[q % 2].sem, k.t_raw[q % 2].at(q // 2 + 1))
                pool.tensor_scalar(wh[:, first + q, :], raw[q % 2][:, :], WS, 1.0, ALU.mult, ALU.mult)
                pool.tensor_scalar(raw[q % 2][:, :], raw[q % 2][:, :], WS, 1.0, ALU.mult, ALU.mult).then_inc(k.t_cast.sem, 1)
                pool.wait_ge(k.t_cast.sem, k.t_cast.at(q + 1))
                pool.tensor_tensor(wl[:, first + q, :], raw[q % 2][:, :], wh[:, first + q, :], ALU.subtract).then_inc(k.t_wlow.sem, 1)

        @block.vector
        def _(dve):
            dve.memset(ones_e[:, :], 1.0)
            dve.memset(exp_f[:, :], 0.0)
            dve.memset(later[:, :, 1:NT], 1.0)
            dve.memset(later[:, :, 0:1], 0.0)
            dve.tensor_copy(iota_h[:, :], c_["iota"])
            choose(dve)
            iota = c_["iota"][:, 0:E].unsqueeze(2).broadcast_to([P, E, NT])
            for kk in range(K):
                last = dve.tensor_tensor(hot[:, kk, :, :], iota, r.choice[:, :, kk].unsqueeze(1).broadcast_to([P, E, NT]), ALU.is_equal)
            last.then_inc(k.m_chain.sem, 1)
            dve.wait_ge(k.m_chain.sem, k.m_chain.next())
            dve.tensor_tensor(tmp[:, :, :], hot[:, 0, :, :], hot[:, 1, :, :], ALU.add).then_inc(k.m_chain.sem, 1)
            dve.wait_ge(k.m_chain.sem, k.m_chain.next())
            for kk in range(2, K):
                dve.tensor_tensor(tmp[:, :, :], tmp[:, :, :], hot[:, kk, :, :], ALU.add).then_inc(k.m_chain.sem, 1)
                dve.wait_ge(k.m_chain.sem, k.m_chain.next())
            dve.tensor_copy(any_h[:, :, :], tmp[:, :, :]).then_inc(k.m_counted.sem, 1)
            dve.wait_ge(k.m_prefixed.sem, k.m_prefixed.at(1))
            dve.tensor_copy(total[:, :, :].rearrange("p e t -> p (e t)"), ps[:, PB, E * NT:2 * E * NT]).then_inc(k.m_chain.sem, 1)
            dve.wait_ge(k.m_chain.sem, k.m_chain.next())
            dve.tensor_tensor_scan(upto[:, :, :].rearrange("p e t -> p (e t)"), later[:, :, :].rearrange("p e t -> p (e t)"),
                                   total[:, :, :].rearrange("p e t -> p (e t)"), 0.0, ALU.mult, ALU.add).then_inc(k.m_chain.sem, 1)
            dve.wait_ge(k.m_chain.sem, k.m_chain.next())
            dve.tensor_scalar(need_i[:, :], upto[:, :, NT - 1], float(P - 1), None, ALU.add).then_inc(k.m_chain.sem, 1)
            dve.tensor_tensor(tmp[:, :, :], upto[:, :, :], total[:, :, :], ALU.subtract)
            dve.wait_ge(k.m_chain.sem, k.m_chain.next())
            dve.tensor_scalar(need_i[:, :], need_i[:, :], 7, None, ALU.arith_shift_right).then_inc(k.m_chain.sem, 1)
            dve.wait_ge(k.m_chain.sem, k.m_chain.next())
            dve.tensor_copy(need[:, :], need_i[:, :]).then_inc(k.m_chain.sem, 1)
            dve.wait_ge(k.m_chain.sem, k.m_chain.next())
            dve.tensor_tensor_scan(ends[:, :], ones_e[:, :], need[:, :], 0.0, ALU.mult, ALU.add).then_inc(k.m_chain.sem, 1)
            dve.wait_ge(k.m_chain.sem, k.m_chain.next())
            dve.tensor_tensor(begins[:, :], ends[:, :], need[:, :], ALU.subtract)
            tile = c_["iota"][:, 0:NTL].unsqueeze(2).broadcast_to([P, NTL, E])
            dve.tensor_tensor(ends_le[:, :, :], ends[:, :].unsqueeze(1).broadcast_to([P, NTL, E]), tile, ALU.is_le)
            dve.tensor_tensor(place[:, :, :].rearrange("p e t -> p (e t)"), tmp[:, :, :].rearrange("p e t -> p (e t)"), ps[:, PB, 0:E * NT], ALU.add).then_inc(k.m_chain.sem, 1)
            dve.wait_ge(k.m_chain.sem, k.m_chain.next())
            dve.tensor_reduce(exp_f[:, 0:NTL], ends_le[:, :, :], AX.X, ALU.add)
            dve.scalar_tensor_tensor(place[:, :, :], begins[:, :].unsqueeze(2).broadcast_to([P, E, NT]), float(P), place[:, :, :], ALU.mult, ALU.add).then_inc(k.m_chain.sem, 1)
            dve.wait_ge(k.m_chain.sem, k.m_chain.next())
            dve.tensor_scalar(exp_f[:, 0:NTL], exp_f[:, 0:NTL], float(E - 1), None, ALU.min).then_inc(k.m_chain.sem, 1)
            dve.wait_ge(k.m_chain.sem, k.m_chain.next())
            for j in range(AT_ONCE - 2, -1, -1):
                digits = exp_f[:, AT_ONCE - 1:AT_ONCE - 1 + NTL] if j == AT_ONCE - 2 else packed[:, :]
                dve.scalar_tensor_tensor(packed[:, :], digits, float(E1), exp_f[:, j:j + NTL], ALU.mult, ALU.add).then_inc(k.m_chain.sem, 1)
                dve.wait_ge(k.m_chain.sem, k.m_chain.next())
            dve.tensor_copy(r.expert[:, :], packed[:, :])
            for kk in range(K):
                dve.tensor_tensor(hot[:, kk, :, :], hot[:, kk, :, :], place[:, :, :], ALU.mult).then_inc(k.m_chain.sem, 1)
                dve.wait_ge(k.m_chain.sem, k.m_chain.next())
                last = dve.tensor_reduce(slot_f[:, kk, :], hot[:, kk, :, :].rearrange("p e t -> p t e"), AX.X, ALU.add)
            last.then_inc(k.m_chain.sem, 1)
            dve.wait_ge(k.m_chain.sem, k.m_chain.next())
            dve.tensor_copy(r.slot[:, :, :].rearrange("p t k -> p k t"), slot_f[:, :, :]).then_inc(k.m_chain.sem, 1)
            dve.wait_ge(k.m_chain.sem, k.m_chain.next())
            dve.tensor_scalar(lo_i[:, :, :], r.slot[:, :, :].rearrange("p t k -> p k t"), P - 1, None, ALU.bitwise_and)
            dve.tensor_scalar(hi_i[:, :, :], r.slot[:, :, :].rearrange("p t k -> p k t"), 7, None, ALU.arith_shift_right).then_inc(k.m_chain.sem, 1)
            dve.wait_ge(k.m_chain.sem, k.m_chain.next())
            dve.tensor_copy(lo_f[:, :, :], lo_i[:, :, :])
            dve.tensor_copy(hi_f[:, :, :], hi_i[:, :, :]).then_inc(k.m_chain.sem, 1)
            dve.wait_ge(k.m_chain.sem, k.m_chain.next())
            with dve.Fori(0, NT) as t:
                for kk in range(K):
                    u, p = t * K + kk, kk % 2
                    dve.wait_ge(k.m_placed.sem, k.m_placed.at(u - 1))
                    dve.tensor_scalar(hot_lo[p][:, :], iota_h[:, :], lo_f[:, kk, bass.ds(t, 1)], c_["token"][:, bass.ds(t, 1)], ALU.is_equal, ALU.mult)
                    dve.tensor_scalar(hot_hi[p][:, :], iota_h[:, 0:NTL], hi_f[:, kk, bass.ds(t, 1)], None, ALU.is_equal).then_inc(k.m_onehot.sem, 1)
            dve.wait_ge(k.m_placed.sem, k.m_placed.at(NT * K))
            dve.tensor_copy(r.table[:, :], ps[:, SB, 0:NTL])
    for s, n in ((k.m_logits, 1), (k.m_rowt, NT), (k.m_rowcopied, NT), (k.m_rows[0], NT // 2), (k.m_rows[1], NT // 2), (k.m_counted, 1),
                 (k.m_prefixed, 1), (k.m_onehot, NT * K), (k.m_placed, NT * K), (k.m_shift, 1), (k.m_expd, 1), (k.t_cast, mix.blocks),
                 (k.t_wlow, mix.blocks), (k.t_raw[0], (mix.blocks + 1) // 2), (k.t_raw[1], mix.blocks // 2)):
        s.base += n


def tiles(k, mix, wh, wl, up, activate, down, r=None):
    nc, ps = k.nc, k.ps
    shared = r is None
    N = NT if shared else mix.tiles
    first_row = mix.tiles * P if shared else 0
    R, F = mix.rows, mix.feeds
    HP = mix.pieces
    W = mix.hidden // HP
    UB, YB, XB = 0, 4, 6
    with ExitStack() as ctx, nc.Block() as block:
        name = "shared" if shared else "routed"
        h32 = [k.sb(f"{name}_h{p}", [P, mix.hidden], ctx=ctx) for p in range(2)]
        hs = [tuple(k.sb(f"{name}_hs{p}{x}", [P, mix.hidden], F16, ctx=ctx) for x in range(2)) for p in range(mix.depth)]
        y = [k.sb(f"{name}_y{p}", [P, D], ctx=ctx) for p in range(2)]
        if shared:
            raw = [k.sb(f"raw{p}", [P, mix.width], ctx=ctx) for p in range(2)]
        else:
            rows = [k.sb(f"rows{b}", [P, 2 * D], F16, ctx=ctx) for b in range(4)]
            x_s = [k.sb(f"x_s{p}", [P, 2, C, P], F16, ctx=ctx) for p in range(2)]
            idx = [k.sb(f"row_i{b}", [P, 1], I32, ctx=ctx) for b in range(4)]

        def source(s, p):
            if shared:
                return tuple(n[:, :, bass.ds(s * P, P)] for n in (k.n_h, k.n_l))
            return tuple(x_s[p][:, x, :, :] for x in range(2))

        def experts(eng, s, n):
            if shared:
                return [mix.E] * n
            packed = eng.value_load(r.expert[0:1, bass.ds(s, 1)], min_val=0, max_val=E1 ** AT_ONCE - 1)
            return [nc.snap((packed // E1 ** j) % E1, engines=[eng.engine], min_val=0, max_val=mix.E - 1) for j in range(n)]

        def all_tiles(eng, body, with_experts=False):
            turns = (N - 2) // 4
            with eng.Fori(0, turns) as i:
                e = experts(eng, 4 * i, 5) if with_experts else [None] * 5
                for b in range(4):
                    body(i, 4 * i + b, b, 2, e[b:b + 2])
            e = experts(eng, 4 * turns, N - 4 * turns) if with_experts else [None] * (N - 4 * turns)
            for s in range(4 * turns, N):
                body(s // 4, s, s % 4, min(N - 1 - s, 2), e[s - 4 * turns:s - 4 * turns + 2])

        def fed(i, s, b):
            return [(s * F + f, f if F > 1 else b % 2, s if F > 1 else 2 * i + b // 2) for f in range(F)]

        @block.tensor
        def _(pe):
            def turn(i, s, b):
                p = b % 2
                pe.wait_ge(k.t_rows[b].sem, k.t_rows[b].at(i + 1))
                pe.wait_ge(k.t_xcopied.sem, k.t_xcopied.at(s - 1))
                out = ps[:, XB + p, 0:D].bitcast(F16)
                for x in range(2 * C):
                    last = pe.transpose(out[:, x * P:(x + 1) * P], rows[b][:, x * P:(x + 1) * P], k.ident_h[:, :])
                last.then_inc(k.t_trans.sem, 1)

            def ascend(s, p, e):
                if not shared:
                    pe.wait_ge(k.t_xcopied.sem, k.t_xcopied.at(s + 1))
                pe.wait_ge(k.t_low.sem, k.t_low.at(s - 1))
                for h in range(HP):
                    up(pe, e, source(s, p), UB + 2 * p, h).then_inc(k.t_up.sem, 1)

            def descend(s, p, e):
                pe.wait_ge(k.t_low.sem, k.t_low.at(s + 1))
                pe.wait_ge(k.t_ycopied.sem, k.t_ycopied.at(s - 1))
                down(pe, e, hs[p % mix.depth], ps[:, YB + p, 0:D]).then_inc(k.t_down.sem, 1)

            if not shared:
                turn(0, 0, 0)
                turn(0, 1, 1)
            ascend(0, 0, experts(pe, 0, 1)[0])

            def body(i, s, b, ahead, e):
                p = b % 2
                if not shared and ahead > 1:
                    turn(i + (b + 2) // 4, s + 2, (b + 2) % 4)
                if ahead > 0:
                    ascend(s + 1, 1 - p, e[1])
                descend(s, p, e[0])
            all_tiles(pe, body, with_experts=True)

        @block.scalar
        def _(act):
            biased = not mix.gated

            def silu(s, p, e):
                act.wait_ge(k.t_low.sem, k.t_low.at(s - 1))
                for h in range(HP):
                    act.wait_ge(k.t_up.sem, k.t_up.at(HP * s + h + 1))
                    activate(act, e, h32[p], UB + 2 * p, h).then_inc(k.t_act.sem, 1)

            silu(0, 0, experts(act, 0, 1)[0] if biased else None)

            def body(i, s, b, ahead, e):
                p = b % 2
                if ahead > 0:
                    silu(s + 1, 1 - p, e[1])
                if shared:
                    for q, w, n in fed(i, s, b):
                        act.wait_ge(k.t_raw[w].sem, k.t_raw[w].at(n + 1))
                        high = wh[:, bass.ds(q, 1), :].rearrange("p o n -> p (o n)")
                        act.activation(high, raw[w][:, :], ACT.Copy, scale=WS).then_inc(k.t_cast.sem, 1)
                act.wait_ge(k.t_down.sem, k.t_down.at(s + 1))
                act.wait_ge(k.t_stored[p].sem, k.t_stored[p].at(2 * i + b // 2))
                act.activation(y[p][:, :], ps[:, YB + p, 0:D], ACT.Copy, scale=1 / (WS * HS)).then_inc(k.t_ycopied.sem, 1)
                if shared:
                    act.wait_ge(k.t_ycopied.sem, k.t_ycopied.at(s + 1))
                    act.dma_start(k.y_rows[bass.ds(first_row + s * P, P), :], y[p][:, :]).then_inc(k.t_stored[p].sem, 16)
            all_tiles(act, body, with_experts=biased)
            if shared:
                for p in range(2):
                    act.wait_ge(k.t_stored[p].sem, k.t_stored[p].at(N // 2))

        @block.vector
        def _(dve):
            def take(s, p):
                dve.wait_ge(k.t_trans.sem, k.t_trans.at(s + 1))
                dve.wait_ge(k.t_up.sem, k.t_up.at(HP * (s - 1)))
                dve.tensor_copy(x_s[p][:, :, :, :].rearrange("p x c n -> p (x c n)"), ps[:, XB + p, 0:D].bitcast(F16)).then_inc(k.t_xcopied.sem, 1)

            def split(s, p):
                parts = hs[p % mix.depth]
                dve.wait_ge(k.t_down.sem, k.t_down.at(s + 1 - mix.depth))
                for n in range(HP):
                    piece = slice(n * W, (n + 1) * W)
                    h, high, low = h32[p][0:R, piece], parts[0][0:R, piece], parts[1][0:R, piece]
                    dve.wait_ge(k.t_act.sem, k.t_act.at(HP * s + n + 1))
                    if mix.gated:
                        dve.scalar_tensor_tensor(h, ps[0:R, UB + 2 * p, mix.hidden:2 * mix.hidden], HS / (WS * NS), h, ALU.mult, ALU.mult).then_inc(k.t_gated.sem, 1)
                        dve.wait_ge(k.t_gated.sem, k.t_gated.at(s + 1))
                        dve.tensor_copy(high, h).then_inc(k.t_high.sem, 1)
                        dve.wait_ge(k.t_high.sem, k.t_high.at(s + 1))
                        last = dve.tensor_tensor(low, h, high, ALU.subtract)
                    else:
                        dve.tensor_scalar(high, h, HS, None, ALU.mult).then_inc(k.t_high.sem, 1)
                        dve.wait_ge(k.t_high.sem, k.t_high.at(HP * s + n + 1))
                        last = dve.scalar_tensor_tensor(low, h, HS, high, ALU.mult, ALU.subtract)
                last.then_inc(k.t_low.sem, 1)

            if not shared:
                take(0, 0)
                take(1, 1)
            split(0, 0)

            def body(i, s, b, ahead, e):
                p = b % 2
                if not shared and ahead > 1:
                    take(s + 2, p)
                if ahead > 0:
                    split(s + 1, 1 - p)
                if shared:
                    for q, w, n in fed(i, s, b):
                        dve.wait_ge(k.t_cast.sem, k.t_cast.at(q + 1))
                        low = wl[:, bass.ds(q, 1), :].rearrange("p o n -> p (o n)")
                        high = wh[:, bass.ds(q, 1), :].rearrange("p o n -> p (o n)")
                        dve.scalar_tensor_tensor(low, raw[w][:, :], WS, high, ALU.mult, ALU.subtract).then_inc(k.t_wlow.sem, 1)
            all_tiles(dve, body)

        @block.sync
        def _(sp):
            def body(i, s, b, ahead, e):
                if shared:
                    for q, w, n in fed(i, s, b):
                        sp.wait_ge(k.t_wlow.sem, k.t_wlow.at(q - 1))
                        sp.dma_start(raw[w][:, :], k.dram[f"m{mix.n}_w"][bass.ds(q, 1), :, :].rearrange("o p n -> p (o n)")).then_inc(k.t_raw[w].sem, 16)
                else:
                    store(s, b % 2)

            def store(s, p):
                sp.wait_ge(k.t_ycopied.sem, k.t_ycopied.at(s + 1))
                sp.dma_start(k.y_rows[bass.ds(first_row + s * P, P), :], y[p][:, :]).then_inc(k.t_stored[p].sem, 16)
            all_tiles(sp, body)
            if not shared:
                for p in range(2):
                    sp.wait_ge(k.t_stored[p].sem, k.t_stored[p].at((N + 1 - p) // 2))

        @block.gpsimd
        def _(pool):
            def body(i, s, b, ahead, e):
                pool.wait_ge(k.t_trans.sem, k.t_trans.at(s - 3))
                pool.tensor_copy(idx[b][:, :], r.table[:, bass.ds(s, 1)]).then_inc(k.t_idx.sem, 1)
                pool.wait_ge(k.t_idx.sem, k.t_idx.at(2 * s + 1))
                pool.sem_inc(k.t_idx.sem, 1)
                pool.indirect_dma_start(rows[b][:, :], None, k.n_rows, bass.IndirectOffsetOnAxis(ap=idx[b][:, 0:1], axis=0)).then_inc(k.t_rows[b].sem, 16)
            if not shared:
                all_tiles(pool, body)
    for s in (k.t_low, k.t_down, k.t_ycopied):
        s.base += N
    for s in (k.t_up, k.t_act, k.t_high):
        s.base += HP * N
    if mix.gated:
        k.t_gated.base += N
    for p in range(2):
        k.t_stored[p].base += (N + 1 - p) // 2
    if shared:
        for s in (k.t_cast, k.t_wlow):
            s.base += N * F
        for p in range(2):
            k.t_raw[p].base += N * F // 2
    else:
        for s in (k.t_trans, k.t_xcopied):
            s.base += N
        k.t_idx.base += 2 * N
        for b in range(4):
            k.t_rows[b].base += (N + 3 - b) // 4


def combine(k, mix, r, biases=None):
    nc, ps, c_ = k.nc, k.ps, k.c
    E, K = mix.E, mix.K
    with ExitStack() as ctx:
        own_share = k.sb("own_share", [P, P], ctx=ctx)
        y = [k.sb(f"c_y{p}", [P, K + 1, D], ctx=ctx) for p in range(4)]
        diag = [k.sb(f"c_diag{p}", [P, K, P], ctx=ctx) for p in range(4)]
        idx = [k.sb(f"c_i{p}", [P, K], I32, ctx=ctx) for p in range(4)]
        if biases is not None:
            b2, cw_t = biases, k.sb("cw_t", [E + 1, T], ctx=ctx)
            combine_weights(k, mix, r, cw_t)
        OB = 4
        with nc.Block() as block:
            def all_tiles(eng, body):
                with eng.Fori(0, NT // 4) as i:
                    for p in range(4):
                        body(i, 4 * i + p, p)

            @block.sync
            def _(sp):
                def body(i, t, p):
                    sp.wait_ge(k.g_summed.sem, k.g_summed.at(t - 3))
                    sp.dma_start(y[p][:, K, :], k.y_rows[bass.ds((mix.tiles + t) * P, P), :]).then_inc(k.g_shared[p].sem, 16)
                all_tiles(sp, body)

            @block.gpsimd
            def _(pool):
                def body(i, t, p):
                    pool.wait_ge(k.g_idx.sem, k.g_idx.at(t + 1))
                    pool.sem_inc(k.g_fetching.sem, 1)
                    for n in range(K):
                        pool.indirect_dma_start(y[p][:, n, :], None, k.y_rows[0:mix.tiles * P, :], bass.IndirectOffsetOnAxis(ap=idx[p][:, n:n + 1], axis=0)).then_inc(k.g_load[p].sem, 16)
                all_tiles(pool, body)

            @block.tensor
            def _(pe):
                def body(i, t, p):
                    pe.wait_ge(k.g_load[p].sem, k.g_load[p].at(K * (i + 1)))
                    pe.wait_ge(k.g_shared[p].sem, k.g_shared[p].at(i + 1))
                    pe.wait_ge(k.g_diag.sem, k.g_diag.at(t + 1))
                    pe.wait_ge(k.g_added.sem, k.g_added.at(t - 3))
                    for m in range(C):
                        out = ps[:, OB + p, m * P:(m + 1) * P]
                        if biases is not None:
                            pe.matmul(out, b2[:, m * P:(m + 1) * P], cw_t[:, bass.ds(t * P, P)], start=True, stop=False)
                        for n in range(K + 1):
                            share = diag[p][:, n, :] if n < K else own_share[:, :]
                            last = pe.matmul(out, y[p][:, n, m * P:(m + 1) * P], share, start=(n == 0 and biases is None), stop=(n == K))
                    last.then_inc(k.g_summed.sem, 1)
                all_tiles(pe, body)

            @block.vector
            def _(dve):
                dve.tensor_scalar(own_share[:, :], c_["ident"], mix.shared_weight, None, ALU.mult)

                def body(i, t, p):
                    dve.wait_ge(k.g_summed.sem, k.g_summed.at(t - 3))
                    dve.tensor_copy(idx[p][:, :], r.slot[:, bass.ds(t, 1), :].rearrange("p o k -> p (o k)")).then_inc(k.g_idx.sem, 1)
                    for n in range(K):
                        last = dve.tensor_scalar(diag[p][:, n, :], c_["ident"], r.w[:, n, bass.ds(t, 1)], None, ALU.mult)
                    last.then_inc(k.g_diag.sem, 1)

                def add(t, p):
                    dve.wait_ge(k.g_summed.sem, k.g_summed.at(t + 1))
                    x = k.x_t[:, :, bass.ds(t * P, P)]
                    dve.tensor_tensor(x, x, ps[:, OB + p, 0:D].rearrange("p (c n) -> p c n", c=C), ALU.add).then_inc(k.g_added.sem, 1)
                for p in range(4):
                    body(0, p, p)
                with dve.Fori(0, NT // 4 - 1) as i:
                    for p in range(4):
                        add(4 * i + p, p)
                        body(i + 1, 4 * i + 4 + p, p)
                for p in range(4):
                    add(NT - 4 + p, p)
    for s in (k.g_summed, k.g_diag, k.g_added, k.g_idx):
        s.base += NT
    for p in range(4):
        k.g_load[p].base += K * NT // 4
        k.g_shared[p].base += NT // 4


def combine_weights(k, mix, r, cw_t):
    nc, ps, c_ = k.nc, k.ps, k.c
    E, K = mix.E, mix.K
    with ExitStack() as ctx, nc.Block() as block:
        hot = k.sb("cw_hot", [P, K, NT, E], ctx=ctx)
        cw = k.sb("cw", [P, NT, E + 1], ctx=ctx)

        @block.vector
        def _(dve):
            dve.memset(cw[:, :, E:E + 1], mix.shared_weight)
            for n in range(K):
                last = dve.tensor_tensor(hot[:, n, :, :], c_["iota"][:, 0:E].unsqueeze(1).broadcast_to([P, NT, E]), r.choice[:, :, n:n + 1].broadcast_to([P, NT, E]), ALU.is_equal)
            last.then_inc(k.m_chain.sem, 1)
            dve.wait_ge(k.m_chain.sem, k.m_chain.next())
            for n in range(K):
                last = dve.tensor_tensor(hot[:, n, :, :], hot[:, n, :, :], r.w[:, n, :].unsqueeze(2).broadcast_to([P, NT, E]), ALU.mult)
            last.then_inc(k.m_chain.sem, 1)
            dve.wait_ge(k.m_chain.sem, k.m_chain.next())
            assert K == 2
            dve.tensor_tensor(cw[:, :, 0:E], hot[:, 0, :, :], hot[:, 1, :, :], ALU.add).then_inc(k.m_cw.sem, 1)
            dve.wait_ge(k.m_cwt.sem, k.m_cwt.at(1))
            dve.tensor_copy(cw_t[:, :].rearrange("e (g n) -> e g n", g=G), ps[0:E + 1, 0:G, :])

        @block.tensor
        def _(pe):
            pe.wait_ge(k.m_cw.sem, k.m_cw.at(1))
            for t in range(NT):
                last = pe.transpose(ps[0:E + 1, t // 4, (t % 4) * P:(t % 4 + 1) * P], cw[:, t, :], c_["ident"])
            last.then_inc(k.m_cwt.sem, 1)
    k.m_cw.base += 1
    k.m_cwt.base += 1


def at_block(w, q, lo, n):
    size = 2 * w.shape[2]
    octets = w[:, :, :].rearrange("p q n -> p (q n)").bitcast(mybir.dt.uint8)
    return octets[:, bass.ds(q * size + 2 * lo, 2 * n)].bitcast(F16)


def stage_first_mixture(k):
    nc, ps = k.nc, k.ps
    mix = MIX0
    with ExitStack() as stage:
        r = Routing(k, mix, stage)
        b1 = k.sb("b1", [P, (E0 + 1) * FC], ctx=stage)
        b2 = k.sb("b2", [E0 + 1, D], ctx=stage)
        stage_weights(k, stage, [], ["L0_ffn_Wg"])
        layernorm(k)
        with ExitStack() as ctx:
            wh, wl = (k.sb(f"m_w{x}", [P, (E0 + 1) * mix.blocks, mix.width], F16, ctx=ctx) for x in "hl")
            route_first(k, mix, wh, wl, r, b1, b2)

            def up(pe, e, x, bank, piece):
                for f in range(piece * FC // 2, (piece + 1) * FC // 2):
                    products = [(w, a, c) for w, a in three((wh, wl), x) for c in range(C)]
                    for n, (w, a, c) in enumerate(products):
                        last = pe.matmul(ps[:, bank + f // 4, (f % 4) * P:(f % 4 + 1) * P], at_block(w, e * mix.blocks + c, f * P, P), a[:, c, :],
                                         start=(n == 0), stop=(n == len(products) - 1))
                return last

            def activate(act, e, h, bank, piece):
                for f in range(piece * FC // 2, (piece + 1) * FC // 2):
                    last = act.activation(h[:, f * P:(f + 1) * P], ps[:, bank + f // 4, (f % 4) * P:(f % 4 + 1) * P], ACT.Silu, scale=1 / (WS * NS),
                                          bias=b1[:, bass.ds(e * FC + f, 1)])
                return last

            def down(pe, e, hs, out):
                products = [(w, a, f) for w, a in three((wh, wl), hs) for f in range(FC)]
                for n, (w, a, f) in enumerate(products):
                    last = pe.matmul(out, a[:, f * P:(f + 1) * P], at_block(w, e * mix.blocks + 2 + f // 4, (f % 4) * D, D),
                                     start=(n == 0), stop=(n == len(products) - 1))
                return last

            tiles(k, mix, wh, wl, up, activate, down)
            tiles(k, mix, wh, wl, up, activate, down, r)
        combine(k, mix, r, b2)


def route_first(k, mix, wh, wl, r, b1, b2):
    nc, ps = k.nc, k.ps
    with ExitStack() as ctx:
        lg = k.sb("lg", [P, NT, E0], ctx=ctx)
        v8 = k.sb("v8", [P, NT, 8], ctx=ctx)
        i8 = k.sb("i8", [P, NT, 8], U32, ctx=ctx)
        ex = k.sb("ex", [P, NT, 8], ctx=ctx)
        z = k.sb("z", [P, 4, NT], ctx=ctx)

        def scores(act):
            act.wait_ge(k.m_shift.sem, k.m_shift.at(1))
            act.activation(ex[:, :, :], ex[:, :, :], ACT.Exp).then_inc(k.m_expd.sem, 1)

        def choose(dve):
            dve.wait_ge(k.m_logits.sem, k.m_logits.at(1))
            dve.tensor_scalar(lg[:, :, :].rearrange("p t e -> p (t e)"), ps[:, 7, 0:NT * E0], 1 / (WS * NS), None, ALU.mult).then_inc(k.m_chain.sem, 1)
            dve.wait_ge(k.m_chain.sem, k.m_chain.next())
            top8(k, dve, lg, v8, i8, r.choice)
            dve.tensor_tensor(ex[:, :, :], v8[:, :, :], v8[:, :, 0:1].broadcast_to([P, NT, 8]), ALU.subtract).then_inc(k.m_shift.sem, 1)
            dve.wait_ge(k.m_expd.sem, k.m_expd.at(1))
            dve.tensor_reduce(z[:, 0, :], ex[:, :, :], AX.X, ALU.add)
            dve.tensor_tensor(z[:, 2, :], ex[:, :, 0], ex[:, :, 1], ALU.add).then_inc(k.m_chain.sem, 1)
            dve.wait_ge(k.m_chain.sem, k.m_chain.next())
            dve.scalar_tensor_tensor(z[:, 1, :], z[:, 0, :], 1e-9, z[:, 2, :], ALU.mult, ALU.add).then_inc(k.m_chain.sem, 1)
            dve.wait_ge(k.m_chain.sem, k.m_chain.next())
            dve.reciprocal(z[:, 3, :], z[:, 1, :]).then_inc(k.m_chain.sem, 1)
            dve.wait_ge(k.m_chain.sem, k.m_chain.next())
            for n in range(K0):
                dve.tensor_tensor(r.w[:, n, :], ex[:, :, n], z[:, 3, :], ALU.mult)

        with nc.Block() as block:
            @block.sync
            def _(sp):
                sp.dma_start(b1[:, :], k.dram["m0_b1"]).then_inc(k.m_bias.sem, 16)
                sp.dma_start(b2[:, :], k.dram["m0_b2"]).then_inc(k.m_bias.sem, 16)
                sp.wait_ge(k.m_bias.sem, 32)
        route(k, mix, k.w["L0_ffn_Wg"], wh, wl, scores, choose, r)


def stage_single_attention(k):
    with ExitStack() as stage:
        stage_weights(k, stage, ["L1_xattn_wk_t", "L1_xattn_wv", "L1_xattn_bq", "L1_xattn_bk", "L1_xattn_bv"], ["L1_xattn_wq"])
        layernorm(k)
        single_attention(k, stage)


def single_attention(k, stage):
    nc, ps, c_ = k.nc, k.ps, k.c
    scale = D ** -0.5
    q_t = k.sb("q_t", [P, C, T], ctx=stage)
    o_t = q_t
    qp_t = k.sb("qp_t", [P, C, T], ctx=stage)

    def take_q(block):
        @block.scalar
        def _(act):
            for g in range(G):
                for m in range(C):
                    act.wait_ge(k.projected.sem, k.projected.at(g * C + m + 1))
                    act.activation(q_t[:, m, group(g)], ps[:, g * C + m, :], ACT.Identity, scale=1 / (WS * NS), bias=k.w["L1_xattn_bq"][:, 0, m:m + 1])
    project(k, k.w["L1_xattn_wq"], (k.n_h, k.n_l), take_q)

    with ExitStack() as ctx:
        QB = 4
        NQ = B // QB
        q_bk = k.sb("q_bk", [1, T], ctx=ctx)

        def take_qp(block):
            @block.scalar
            def _(act):
                for g in range(G):
                    for m in range(C):
                        act.wait_ge(k.projected.sem, k.projected.at(g * C + m + 1))
                        act.activation(qp_t[:, m, group(g)], ps[:, g * C + m, :], ACT.Copy, scale=scale)
        project(k, k.w["L1_xattn_wk_t"], q_t, take_qp)
        with nc.Block() as block:
            @block.tensor
            def _(pe):
                for g in range(G):
                    for c in range(C):
                        last = pe.matmul(ps[0:1, g, :], k.w["L1_xattn_bk"][:, 0, c:c + 1], q_t[:, c, group(g)], start=(c == 0), stop=(c == C - 1))
                    last.then_inc(k.projected.sem, 1)

            @block.scalar
            def _(act):
                for g in range(G):
                    act.wait_ge(k.projected.sem, k.projected.at(g + 1))
                    act.activation(q_bk[0:1, group(g)], ps[0:1, g, :], ACT.Copy, scale=scale)
        k.projected.base += G

        ctx_t = [k.sb(f"b_ctx_t{a}", [P, QB, C, SK], ctx=ctx) for a in range(4)]
        ctx_n = [k.sb(f"b_ctx{a}", [P, QB, 2, D], ctx=ctx) for a in range(4)]
        ctx_l = [k.sb(f"b_ctx_last{a}", [QB, D], ctx=ctx) for a in range(4)]
        q_s = [k.sb(f"b_q{p}", [P, C, P], ctx=ctx) for p in range(2)]
        qb_s = [k.sb(f"b_qbk{p}", [1, P], ctx=ctx) for p in range(2)]
        neg_max = k.sb("b_neg_max", [P, 2], ctx=ctx)
        sums = k.sb("b_sums", [P, 2], ctx=ctx)
        inv = k.sb("b_inv", [P, 2], ctx=ctx)
        probs = [k.sb(f"b_probs{p}", [P, SK], ctx=ctx) for p in range(2)]
        pn = [k.sb(f"b_pn{p}", [P, SK], ctx=ctx) for p in range(2)]
        p_t = [k.sb(f"b_p_t{p}", [P, 2, P], ctx=ctx) for p in range(2)]
        pn_l = [k.sb(f"b_pn_last{p}", [P, QB], ctx=ctx) for p in range(2)]
        p_l = [k.sb(f"b_p_last{p}", [QB, P], ctx=ctx) for p in range(2)]
        o_s = [k.sb(f"b_o{p}", [P, D], ctx=ctx) for p in range(2)]
        SB, TB, OB, FB = 0, 2, 4, 6

        with nc.Block() as block:
            @block.sync
            def _(sp):
                def fetch(i, a):
                    n = 4 * i + a
                    sp.wait_ge(k.b_scored.sem, k.b_scored.at(n - 3))
                    sp.dma_start(ctx_t[a][:, :, :, :].rearrange("p j c n -> p (j c) n"), k.dram["ctx_t"][bass.ds(n * QB, QB), :, :].rearrange("j (c p) n -> p (j c) n", p=P)).then_inc(k.b_ctx_t[a].sem, 16)
                with sp.Fori(0, NQ // 4) as i:
                    for a in range(4):
                        fetch(i, a)

            @block.gpsimd
            def _(pool):
                def fetch(i, a):
                    n = 4 * i + a
                    pool.wait_ge(k.b_out.sem, k.b_out.at(n - 3))
                    rows = k.dram["ctx"][bass.ds(n * QB, QB), :, :]
                    for r in range(2):
                        pool.dma_start(ctx_n[a][:, :, r, :], rows[:, r * P:(r + 1) * P, :].rearrange("j p d -> p j d")).then_inc(k.b_ctx[a].sem, 16)
                    pool.dma_start(ctx_l[a][:, :], rows[:, 2 * P:SK, :].rearrange("j o d -> j (o d)")).then_inc(k.b_ctx[a].sem, 16)
                with pool.Fori(0, NQ // 4) as i:
                    for a in range(4):
                        fetch(i, a)

            @block.tensor
            def _(pe):
                def scores(i, a):
                    n, p = 4 * i + a, a % 2
                    pe.wait_ge(k.b_ctx_t[a].sem, k.b_ctx_t[a].at(i + 1))
                    pe.wait_ge(k.b_qs.sem, k.b_qs.at(n + 1))
                    pe.wait_ge(k.b_exp.sem, k.b_exp.at(n - 1))
                    pe.matmul(ps[:, SB + p, 0:SK], qb_s[p][0:1, :], k.ones_row[0:1, :], start=True, stop=False, skip_group_check=True)
                    for j in range(QB):
                        for c in range(C):
                            last = pe.matmul(ps[j * S:(j + 1) * S, SB + p, 0:SK], q_s[p][:, c, j * S:(j + 1) * S], ctx_t[a][:, j, c, :],
                                             start=False, stop=(c == C - 1), skip_group_check=True)
                    last.then_inc(k.b_scored.sem, 1)

                def turn(i, a):
                    n, p = 4 * i + a, a % 2
                    pe.wait_ge(k.b_normed.sem, k.b_normed.at(n + 1))
                    pe.wait_ge(k.b_tcopied.sem, k.b_tcopied.at(n - 1))
                    for r in range(2):
                        pe.transpose(ps[:, TB + p, r * P:(r + 1) * P], pn[p][:, r * P:(r + 1) * P], c_["ident"])
                    pe.transpose(ps[0:QB, TB + p, 2 * P:3 * P], pn_l[p][:, :], c_["ident"]).then_inc(k.b_trans.sem, 1)

                def turn_outputs(n, p):
                    pe.wait_ge(k.b_ocopied.sem, k.b_ocopied.at(n + 1))
                    pe.wait_ge(k.b_taken.sem, k.b_taken.at(n - 1))
                    for c in range(C):
                        last = pe.transpose(ps[:, FB + p, c * P:(c + 1) * P], o_s[p][:, c * P:(c + 1) * P], c_["ident"])
                    last.then_inc(k.b_oturned.sem, 1)

                def weigh(i, a):
                    n, p = 4 * i + a, a % 2
                    pe.wait_ge(k.b_ctx[a].sem, k.b_ctx[a].at(3 * (i + 1)))
                    pe.wait_ge(k.b_ocopied.sem, k.b_ocopied.at(n - 1))
                    pe.wait_ge(k.b_tcopied.sem, k.b_tcopied.at(n + 1))
                    pe.matmul(ps[:, OB + p, 0:D], p_l[p][:, :], ctx_l[a][:, :], start=True, stop=False, skip_group_check=True)
                    for j in range(QB):
                        for r in range(2):
                            last = pe.matmul(ps[j * S:(j + 1) * S, OB + p, 0:D], p_t[p][:, r, j * S:(j + 1) * S], ctx_n[a][:, j, r, :],
                                             start=False, stop=(r == 1), skip_group_check=True)
                    last.then_inc(k.b_out.sem, 1)

                scores(0, 0)
                turn(0, 0)
                scores(0, 1)
                weigh(0, 0)
                with pe.Fori(0, NQ // 4 - 1) as i:
                    for a in range(1, 5):
                        turn(i + a // 4, a % 4)
                        scores(i + (a + 1) // 4, (a + 1) % 4)
                        turn_outputs(4 * i + a - 1, (a - 1) % 2)
                        weigh(i + a // 4, a % 4)
                i = NQ // 4 - 1
                for a in range(1, 4):
                    turn(i, a)
                    if a < 3:
                        scores(i, a + 1)
                    turn_outputs(4 * i + a - 1, (a - 1) % 2)
                    weigh(i, a)
                turn_outputs(NQ - 1, 1)

            @block.scalar
            def _(act):
                def softmax(i, p):
                    n = 2 * i + p
                    act.wait_ge(k.b_max.sem, k.b_max.at(n + 1))
                    act.wait_ge(k.b_normed.sem, k.b_normed.at(n - 1))
                    act.activation(probs[p][:, :], ps[:, SB + p, 0:SK], ACT.Exp, bias=neg_max[:, p:p + 1], accum_out=sums[:, p:p + 1]).then_inc(k.b_exp.sem, 1)

                def outputs(n, p):
                    act.wait_ge(k.b_out.sem, k.b_out.at(n + 1))
                    act.wait_ge(k.b_oturned.sem, k.b_oturned.at(n - 1))
                    act.activation(o_s[p][:, :], ps[:, OB + p, 0:D], ACT.Copy).then_inc(k.b_ocopied.sem, 1)
                softmax(0, 0)
                with act.Fori(0, NQ // 2 - 1) as i:
                    for p in range(2):
                        softmax(i + p, 1 - p)
                        outputs(2 * i + p, p)
                softmax(NQ // 2 - 1, 1)
                outputs(NQ - 2, 0)
                outputs(NQ - 1, 1)

            @block.vector
            def _(dve):
                def queries(i, p):
                    n = 2 * i + p
                    dve.wait_ge(k.b_scored.sem, k.b_scored.at(n - 1))
                    dve.tensor_copy(q_s[p][:, :, :], qp_t[:, :, bass.ds(n * P, P)])
                    dve.tensor_copy(qb_s[p][0:1, :], q_bk[0:1, bass.ds(n * P, P)]).then_inc(k.b_qs.sem, 1)

                def softmax(i, p):
                    n = 2 * i + p
                    dve.wait_ge(k.b_scored.sem, k.b_scored.at(n + 1))
                    dve.tensor_reduce(neg_max[:, p:p + 1], ps[:, SB + p, 0:SK], AX.X, ALU.max, negate=True).then_inc(k.b_max.sem, 1)
                    dve.wait_ge(k.b_exp.sem, k.b_exp.at(n + 1))
                    dve.reciprocal(inv[:, p:p + 1], sums[:, p:p + 1]).then_inc(k.b_inv.sem, 1)
                    dve.wait_ge(k.b_inv.sem, k.b_inv.at(n + 1))
                    dve.wait_ge(k.b_trans.sem, k.b_trans.at(n - 1))
                    dve.tensor_scalar(pn[p][:, :], probs[p][:, :], inv[:, p:p + 1], None, ALU.mult)
                    dve.tensor_scalar(pn_l[p][:, :], c_["sequence"], inv[:, p:p + 1], probs[p][:, 2 * P:SK], ALU.mult, ALU.mult).then_inc(k.b_normed.sem, 1)

                def turned(i, p):
                    n = 2 * i + p
                    dve.wait_ge(k.b_out.sem, k.b_out.at(n - 1))
                    dve.wait_ge(k.b_trans.sem, k.b_trans.at(n + 1))
                    dve.tensor_copy(p_l[p][:, :], ps[0:QB, TB + p, 2 * P:3 * P])
                    dve.tensor_copy(p_t[p][:, :, :].rearrange("p r q -> p (r q)"), ps[:, TB + p, 0:2 * P]).then_inc(k.b_tcopied.sem, 1)

                def outputs(i, p):
                    n = 2 * i + p
                    dve.wait_ge(k.b_oturned.sem, k.b_oturned.at(n + 1))
                    dve.tensor_copy(o_t[:, :, bass.ds(n * P, P)], ps[:, FB + p, 0:2 * P].rearrange("p (c q) -> p c q", c=C)).then_inc(k.b_taken.sem, 1)

                queries(0, 0)
                queries(0, 1)
                softmax(0, 0)
                turned(0, 0)
                queries(1, 0)
                softmax(0, 1)
                with dve.Fori(0, NQ // 2 - 2) as i:
                    for p in range(2):
                        turned(i + p, 1 - p)
                        queries(i + 1 + p, 1 - p)
                        softmax(i + 1, p)
                        outputs(i, p)
                for n in range(NQ - 3, NQ):
                    turned(n // 2, n % 2)
                    if n + 2 < NQ:
                        queries((n + 2) // 2, n % 2)
                    if n + 1 < NQ:
                        softmax((n + 1) // 2, (n + 1) % 2)
                    outputs((n - 1) // 2, (n - 1) % 2)
                outputs(NQ // 2 - 1, 1)

    def add_out(block):
        @block.vector
        def _(dve):
            for g in range(G):
                for m in range(C):
                    dve.wait_ge(k.projected.sem, k.projected.at(g * C + m + 1))
                    x = k.x_t[:, m, group(g)]
                    dve.scalar_tensor_tensor(x, ps[:, g * C + m, :], k.w["L1_xattn_bv"][:, 0, m:m + 1], x, ALU.add, ALU.add)
    project(k, k.w["L1_xattn_wv"], o_t, add_out)


def stage_causal_attention(k):
    with ExitStack() as stage:
        stage_weights(k, stage, ["L1_attn_bq", "L1_attn_bk", "L1_attn_bv"], ["L1_attn_Wq_t", "L1_attn_Wk_t", "L1_attn_Wv_t"])
        layernorm(k)
        causal_attention(k, stage)


def causal_attention(k, stage):
    nc, ps, c_ = k.nc, k.ps, k.c
    scale = D ** -0.5
    q_t = k.sb("q_t", [P, C, T], ctx=stage)            
    k_t = k.sb("k_t", [P, C, T], ctx=stage)
    n = (k.n_h, k.n_l)

    def take_q(block):
        @block.scalar
        def _(act):
            for g in range(G):
                for m in range(C):
                    act.wait_ge(k.projected.sem, k.projected.at(g * C + m + 1))
                    act.activation(q_t[:, m, group(g)], ps[:, g * C + m, :], ACT.Identity, scale=1 / (WS * NS), bias=k.w["L1_attn_bq"][:, 0, m:m + 1])
    project(k, k.w["L1_attn_Wq_t"], n, take_q)

    def take_k(block):
        @block.scalar
        def _(act):
            for g in range(G):
                for m in range(C):
                    act.wait_ge(k.projected.sem, k.projected.at(g * C + m + 1))
                    act.activation(k_t[:, m, group(g)], ps[:, g * C + m, :], ACT.Identity, scale=1 / (WS * NS), bias=k.w["L1_attn_bk"][:, 0, m:m + 1])
    project(k, k.w["L1_attn_Wk_t"], n, take_k)

    with ExitStack() as ctx:
        n_s = [[k.sb(f"c_n{p}{x}", [P, C, P], F16, ctx=ctx) for x in range(2)] for p in range(2)]
        q_s = [k.sb(f"c_q{p}", [P, C, P], ctx=ctx) for p in range(2)]
        v = [k.sb(f"c_v{p}", [P, D], ctx=ctx) for p in range(2)]
        neg_max = k.sb("c_neg_max", [P, 2], ctx=ctx)
        sums = k.sb("c_sums", [P, 2], ctx=ctx)
        inv = k.sb("c_inv", [P, 2], ctx=ctx)
        probs = [k.sb(f"c_probs{p}", [P, P], ctx=ctx) for p in range(2)]
        pn = [k.sb(f"c_pn{p}", [P, P], ctx=ctx) for p in range(2)]
        p_t = [k.sb(f"c_p_t{p}", [P, P], ctx=ctx) for p in range(2)]
        VB, SB, TB, OB = 0, 2, 4, 6
        wv = k.w["L1_attn_Wv_t"]

        with nc.Block() as block:
            @block.gpsimd
            def _(pool):
                with pool.Fori(0, NT // 2) as i:
                    for p in range(2):
                        t = 2 * i + p
                        pool.wait_ge(k.c_scored.sem, k.c_scored.at(t - 1))
                        for x in range(2):
                            pool.tensor_copy(n_s[p][x][:, :, :], n[x][:, :, bass.ds(t * P, P)])
                        pool.tensor_copy(q_s[p][:, :, :], q_t[:, :, bass.ds(t * P, P)]).then_inc(k.c_static.sem, 1)

            @block.tensor
            def _(pe):
                def scores(i, p):
                    t = 2 * i + p
                    pe.wait_ge(k.c_static.sem, k.c_static.at(t + 1))
                    pe.wait_ge(k.c_vcopied.sem, k.c_vcopied.at(t - 1))
                    products = [(w, x, c) for w, x in three(wv, n_s[p]) for c in range(C)]
                    for m, (w, x, c) in enumerate(products):
                        pe.matmul(ps[:, VB + p, 0:D], x[:, c, :], w[:, c, :], start=(m == 0), stop=(m == len(products) - 1))
                    pe.wait_ge(k.c_exp.sem, k.c_exp.at(t - 1))
                    pe.matmul(ps[:, SB + p, 0:P], k.ident_bf[:, :], k.causal_bf[:, :], start=True, stop=False)
                    for c in range(C):
                        last = pe.matmul(ps[:, SB + p, 0:P], q_s[p][:, c, :], k_t[:, c, bass.ds(t * P, P)], start=False, stop=(c == C - 1))
                    last.then_inc(k.c_scored.sem, 1)

                def weigh(i, p):
                    t = 2 * i + p
                    pe.wait_ge(k.c_normed.sem, k.c_normed.at(t + 1))
                    pe.wait_ge(k.c_tcopied.sem, k.c_tcopied.at(t - 1))
                    pe.transpose(ps[:, TB + p, 0:P], pn[p][:, :], c_["ident"]).then_inc(k.c_trans.sem, 1)
                    pe.wait_ge(k.c_tcopied.sem, k.c_tcopied.at(t + 1))
                    pe.wait_ge(k.c_vcopied.sem, k.c_vcopied.at(t + 1))
                    pe.wait_ge(k.c_taken.sem, k.c_taken.at(t - 1))
                    for c in range(C):
                        last = pe.matmul(ps[:, OB + p, c * P:(c + 1) * P], v[p][:, c * P:(c + 1) * P], p_t[p][:, :], start=True, stop=True)
                    last.then_inc(k.c_out.sem, 1)

                scores(0, 0)
                with pe.Fori(0, NT // 2 - 1) as i:
                    scores(i, 1)
                    weigh(i, 0)
                    scores(i + 1, 0)
                    weigh(i, 1)
                i = NT // 2 - 1
                scores(i, 1)
                weigh(i, 0)
                weigh(i, 1)

            @block.scalar
            def _(act):
                with act.Fori(0, NT // 2) as i:
                    for p in range(2):
                        t = 2 * i + p
                        act.wait_ge(k.c_scored.sem, k.c_scored.at(t + 1))
                        act.wait_ge(k.c_out.sem, k.c_out.at(t - 1))
                        act.activation(v[p][:, :], ps[:, VB + p, 0:D], ACT.Copy, scale=1 / (WS * NS)).then_inc(k.c_vcopied.sem, 1)
                        act.wait_ge(k.c_max.sem, k.c_max.at(2 * (t + 1)))
                        act.wait_ge(k.c_normed.sem, k.c_normed.at(t - 1))
                        act.activation(probs[p][:, :], ps[:, SB + p, 0:P], ACT.Exp, scale=scale, bias=neg_max[:, p:p + 1], accum_out=sums[:, p:p + 1]).then_inc(k.c_exp.sem, 1)

            @block.vector
            def _(dve):
                with dve.Fori(0, NT // 2) as i:
                    for p in range(2):
                        t = 2 * i + p
                        dve.wait_ge(k.c_scored.sem, k.c_scored.at(t + 1))
                        dve.tensor_reduce(neg_max[:, p:p + 1], ps[:, SB + p, 0:P], AX.X, ALU.max, negate=True).then_inc(k.c_max.sem, 1)
                        dve.wait_ge(k.c_max.sem, k.c_max.at(2 * t + 1))
                        dve.tensor_scalar(neg_max[:, p:p + 1], neg_max[:, p:p + 1], scale, None, ALU.mult).then_inc(k.c_max.sem, 1)
                        dve.wait_ge(k.c_exp.sem, k.c_exp.at(t + 1))
                        dve.reciprocal(inv[:, p:p + 1], sums[:, p:p + 1]).then_inc(k.c_inv.sem, 1)
                        dve.wait_ge(k.c_inv.sem, k.c_inv.at(t + 1))
                        dve.wait_ge(k.c_trans.sem, k.c_trans.at(t - 1))
                        dve.tensor_scalar(pn[p][:, :], probs[p][:, :], inv[:, p:p + 1], None, ALU.mult).then_inc(k.c_normed.sem, 1)
                        dve.wait_ge(k.c_out.sem, k.c_out.at(t - 1))
                        dve.wait_ge(k.c_trans.sem, k.c_trans.at(t + 1))
                        dve.tensor_copy(p_t[p][:, :], ps[:, TB + p, 0:P]).then_inc(k.c_tcopied.sem, 1)
                        dve.wait_ge(k.c_out.sem, k.c_out.at(t + 1))
                        for c in range(C):
                            x = k.x_t[:, c, bass.ds(t * P, P)]
                            last = dve.scalar_tensor_tensor(x, ps[:, OB + p, c * P:(c + 1) * P], k.w["L1_attn_bv"][:, 0, c:c + 1], x, ALU.add, ALU.add)
                        last.then_inc(k.c_taken.sem, 1)


def stage_second_mixture(k):
    nc, ps = k.nc, k.ps
    mix = MIX1
    gate_at, up_at, down_at = 0, C * I1, 2 * C * I1
    with ExitStack() as stage:
        r = Routing(k, mix, stage)
        stage_weights(k, stage, ["L1_ffn_gate_bias"], ["L1_ffn_gate_w_t"])
        layernorm(k)
        with ExitStack() as ctx:
            wh, wl = (k.sb(f"m_w{x}", [P, E1 + 1, mix.width], F16, ctx=ctx) for x in "hl")
            route_second(k, mix, wh, wl, r)

            def up(pe, e, x, bank, piece):
                for part, at in enumerate((gate_at, up_at)):
                    for h in range(2):
                        products = [(w, a, c) for w, a in three((wh, wl), x) for c in range(C)]
                        for n, (w, a, c) in enumerate(products):
                            last = pe.matmul(ps[0:IH, bank, (2 * part + h) * P:(2 * part + h + 1) * P], at_block(w, e, at + c * I1 + h * IH, IH), a[:, c, :],
                                             start=(n == 0), stop=(n == len(products) - 1))
                return last

            def activate(act, e, h, bank, piece):
                return act.activation(h[0:IH, :], ps[0:IH, bank, 0:2 * P], ACT.Silu, scale=1 / (WS * NS))

            def down(pe, e, hs, out):
                products = [(w, a, h) for w, a in three((wh, wl), hs) for h in range(2)]
                for n, (w, a, h) in enumerate(products):
                    last = pe.matmul(out, a[0:IH, h * P:(h + 1) * P], at_block(w[0:IH, :, :], e, down_at + h * D, D),
                                     start=(n == 0), stop=(n == len(products) - 1))
                return last

            tiles(k, mix, wh, wl, up, activate, down)
            tiles(k, mix, wh, wl, up, activate, down, r)
        combine(k, mix, r)


def route_second(k, mix, wh, wl, r):
    nc, ps, c_ = k.nc, k.ps, k.c
    NG, EG = 4, E1 // 4
    gate_bias = k.w["L1_ffn_gate_bias"]
    with ExitStack() as ctx:
        sc = k.sb("sc", [P, NT, E1], ctx=ctx)
        sb = k.sb("sbias", [P, NT, NG, EG], ctx=ctx)
        pair = k.sb("pair", [P, 6, NT, NG], ctx=ctx)
        rank = k.sb("rank", [P, 3, NT, NG * NG], ctx=ctx)
        allowed = k.sb("allowed", [P, NT, NG], ctx=ctx)
        masked = k.sb("masked", [P, NT, E1], ctx=ctx)
        v8 = k.sb("v8", [P, NT, 8], ctx=ctx)
        i8 = k.sb("i8", [P, NT, 8], U32, ctx=ctx)
        one = k.sb("one", [P, K1, NT, E1], ctx=ctx)
        z = k.sb("z", [P, 2, NT], ctx=ctx)

        def scores(act):
            act.wait_ge(k.m_logits.sem, k.m_logits.at(1))
            act.activation(sc[:, :, :].rearrange("p t e -> p (t e)"), ps[:, 7, 0:NT * E1], ACT.Sigmoid, scale=1 / (WS * NS)).then_inc(k.m_expd.sem, 1)

        def choose(dve):
            dve.wait_ge(k.m_expd.sem, k.m_expd.at(1))
            flat = sb[:, :, :, :].rearrange("p t g e -> p t (g e)")
            dve.tensor_tensor(flat, sc[:, :, :], gate_bias[:, 0:1, :].broadcast_to([P, NT, E1]), ALU.add).then_inc(k.m_chain.sem, 1)
            dve.wait_ge(k.m_chain.sem, k.m_chain.next())
            pairs = [(a, b) for a in range(EG) for b in range(a + 1, EG)]
            for n, (a, b) in enumerate(pairs):
                last = dve.tensor_tensor(pair[:, n, :, :], sb[:, :, :, a], sb[:, :, :, b], ALU.add)
            last.then_inc(k.m_chain.sem, 1)
            dve.wait_ge(k.m_chain.sem, k.m_chain.next())
            for n in range(1, len(pairs)):
                dve.tensor_tensor(pair[:, 0, :, :], pair[:, 0, :, :], pair[:, n, :, :], ALU.max).then_inc(k.m_chain.sem, 1)
                dve.wait_ge(k.m_chain.sem, k.m_chain.next())
            score = pair[:, 0, :, :]
            own = score.unsqueeze(3).broadcast_to([P, NT, NG, NG])
            other = score.unsqueeze(2).broadcast_to([P, NT, NG, NG])
            ranks = [rank[:, n, :, :].rearrange("p t (a b) -> p t a b", a=NG) for n in range(3)]
            dve.tensor_tensor(ranks[0], other, own, ALU.is_gt)
            dve.tensor_tensor(ranks[1], other, own, ALU.is_equal).then_inc(k.m_chain.sem, 1)
            dve.wait_ge(k.m_chain.sem, k.m_chain.next())
            earlier = c_["earlier"].unsqueeze(1).broadcast_to([P, NT, NG * NG])
            dve.tensor_tensor(rank[:, 1, :, :], rank[:, 1, :, :], earlier, ALU.mult).then_inc(k.m_chain.sem, 1)
            dve.wait_ge(k.m_chain.sem, k.m_chain.next())
            dve.tensor_tensor(rank[:, 2, :, :], rank[:, 0, :, :], rank[:, 1, :, :], ALU.add).then_inc(k.m_chain.sem, 1)
            dve.wait_ge(k.m_chain.sem, k.m_chain.next())
            dve.tensor_reduce(allowed[:, :, :], ranks[2], AX.X, ALU.add).then_inc(k.m_chain.sem, 1)
            dve.wait_ge(k.m_chain.sem, k.m_chain.next())
            dve.tensor_scalar(allowed[:, :, :], allowed[:, :, :], 2.0, MASKED, ALU.is_ge, ALU.mult).then_inc(k.m_chain.sem, 1)
            dve.wait_ge(k.m_chain.sem, k.m_chain.next())
            dve.tensor_tensor(masked[:, :, :].rearrange("p t (g e) -> p t g e", g=NG), sb[:, :, :, :], allowed[:, :, :].unsqueeze(3).broadcast_to([P, NT, NG, EG]), ALU.add).then_inc(k.m_chain.sem, 1)
            dve.wait_ge(k.m_chain.sem, k.m_chain.next())
            top8(k, dve, masked, v8, i8, r.choice)
            for n in range(K1):
                last = dve.tensor_tensor(one[:, n, :, :], c_["iota"][:, 0:E1].unsqueeze(1).broadcast_to([P, NT, E1]), r.choice[:, :, n:n + 1].broadcast_to([P, NT, E1]), ALU.is_equal)
            last.then_inc(k.m_chain.sem, 1)
            dve.wait_ge(k.m_chain.sem, k.m_chain.next())
            for n in range(K1):
                last = dve.tensor_tensor(one[:, n, :, :], one[:, n, :, :], sc[:, :, :], ALU.mult)
            last.then_inc(k.m_chain.sem, 1)
            dve.wait_ge(k.m_chain.sem, k.m_chain.next())
            for n in range(K1):
                last = dve.tensor_reduce(r.w[:, n, :], one[:, n, :, :], AX.X, ALU.add)
            last.then_inc(k.m_chain.sem, 1)
            dve.wait_ge(k.m_chain.sem, k.m_chain.next())
            dve.tensor_reduce(z[:, 0, :], r.w[:, :, :].rearrange("p k t -> p t k"), AX.X, ALU.add).then_inc(k.m_chain.sem, 1)
            dve.wait_ge(k.m_chain.sem, k.m_chain.next())
            dve.tensor_scalar(z[:, 0, :], z[:, 0, :], 1e-20, None, ALU.add).then_inc(k.m_chain.sem, 1)
            dve.wait_ge(k.m_chain.sem, k.m_chain.next())
            dve.reciprocal(z[:, 1, :], z[:, 0, :]).then_inc(k.m_chain.sem, 1)
            dve.wait_ge(k.m_chain.sem, k.m_chain.next())
            dve.scalar_tensor_tensor(r.w[:, :, :], r.w[:, :, :], 2.5, z[:, 1, :].unsqueeze(1).broadcast_to([P, K1, NT]), ALU.mult, ALU.mult)

        route(k, mix, k.w["L1_ffn_gate_w_t"], wh, wl, scores, choose, r)


def build(nc, dram):
    with ExitStack() as ctx:
        k = Core(nc, ctx, dram)
        k.ps = ctx.enter_context(nc.psum_tensor("ps", [P, 8, 512], F32))
        k.x_t = k.sb("x_t_sb", [P, C, T])
        k.n_h = k.sb("n_h", [P, C, T], F16)
        k.n_l = k.sb("n_l", [P, C, T], F16)
        k.consts = k.sb("consts_sb", [P, sum(CONST.values())])
        k.c, at = {}, 0
        for name, n in CONST.items():
            k.c[name] = k.consts[:, at:at + n]
            at += n
        k.ones_mean = k.sb("ones_mean", [P, P])
        k.ones_row = k.sb("ones_row", [1, SK])
        k.ones_h = k.sb("ones_h", [P, P], F16)
        k.eps = k.sb("eps", [P, 1])
        k.ident_h = k.sb("ident_h", [P, P], F16)
        k.before_h = k.sb("before_h", [P, P], F16)
        k.ident_bf = k.sb("ident_bf", [P, P], BF16)
        k.repeat_bf = k.sb("repeat_bf", [S, P], BF16)
        k.causal_bf = k.sb("causal_bf", [P, P], BF16)
        k.w = {}
        k.n_rows = nc.dram_tensor("n_rows", [T, 2 * D], F16, kind="Internal").ap()
        k.y_rows = nc.dram_tensor("y_rows", [MAX_TILES * P + T, D], F32, kind="Internal").ap()

        k.mean_ready = k.count("mean_ready")
        k.squared = k.count("squared")
        k.var_ready = k.count("var_ready")
        k.std_ready = k.count("std_ready")
        k.inv_ready = k.count("inv_ready")
        k.diag_ready = k.count("diag_ready")
        k.inv_spread = k.count("inv_spread")
        k.var_kept = k.count("var_kept")
        k.var_kept_diag = k.count("var_kept_diag")
        k.centred = k.count("centred")
        k.normed = k.count("normed")
        k.high_ready = k.count("high_ready")
        k.split_high = k.count("split_high")
        k.projected = k.count("projected")
        k.a_keys_done = k.count("a_keys_done", 2)
        k.a_kproj = k.count("a_kproj")
        k.a_kcopied = k.count("a_kcopied", 1)
        k.a_vcopied = k.count("a_vcopied", 1)
        k.a_qblk = k.count("a_qblk")
        k.a_maskb = k.count("a_maskb", 2)
        k.a_ptcopied = k.count("a_ptcopied", 2)
        k.a_scored = k.count("a_scored", 2)
        k.a_normed = k.count("a_normed", 8)
        k.a_pt = k.count("a_pt", 2)
        k.a_own = k.count("a_own", 1)
        k.a_out = k.count("a_out", 2)
        k.a_max = k.count("a_max")
        k.a_exp = k.count("a_exp", 4)
        k.a_inv = k.count("a_inv")
        k.a_centred = k.count("a_centred", 2)
        k.a_high = k.count("a_high")
        k.a_low = k.count("a_low", 2)
        k.a_osum = k.count("a_osum")
        k.a_vlast = k.count("a_vlast")
        k.a_vtaken = k.count("a_vtaken")
        k.a_split = k.count("a_split")
        k.r_proj = k.count("r_proj")
        k.r_added = k.count("r_added", 1)
        k.r_scan = k.count("r_scan", 2)
        k.r_out = k.count("r_out", 1)
        k.r_init = k.count("r_init")
        k.r_valued = k.count("r_valued")
        k.r_sig = k.count("r_sig", 2)
        k.r_floor = k.count("r_floor")
        k.r_sum = k.count("r_sum")
        k.r_inv = k.count("r_inv")
        k.r_gates = k.count("r_gates")
        k.r_first = k.count("r_first")
        k.m_chain = k.count("m_chain")
        k.m_logits = k.count("m_logits")
        k.m_counted = k.count("m_counted")
        k.m_prefixed = k.count("m_prefixed")
        k.m_onehot = k.count("m_onehot", 2)
        k.m_placed = k.count("m_placed", 2)
        k.m_rowt = k.count("m_rowt")
        k.m_rowcopied = k.count("m_rowcopied", 1)
        k.m_shift = k.count("m_shift")
        k.m_expd = k.count("m_expd")
        k.m_cw = k.count("m_cw")
        k.m_cwt = k.count("m_cwt")
        k.t_trans = k.count("t_trans", 4)
        k.t_xcopied = k.count("t_xcopied", 2)
        k.t_up = k.count("t_up", 4)
        k.t_act = k.count("t_act", 2)
        k.t_high = k.count("t_high", 2)
        k.t_low = k.count("t_low", 2)
        k.t_down = k.count("t_down", 2)
        k.t_ycopied = k.count("t_ycopied", 2)
        k.t_idx = k.count("t_idx")
        k.t_cast = k.count("t_cast", 2)
        k.t_wlow = k.count("t_wlow", 2)
        k.t_gated = k.count("t_gated")
        k.g_idx = k.count("g_idx")
        k.g_fetching = k.count("g_fetching")
        k.g_diag = k.count("g_diag")
        k.g_added = k.count("g_added", 4)
        k.g_summed = k.count("g_summed", 4)
        k.b_scored = k.count("b_scored", 4)
        k.b_out = k.count("b_out", 4)
        k.b_qs = k.count("b_qs")
        k.b_exp = k.count("b_exp", 2)
        k.b_normed = k.count("b_normed", 2)
        k.b_tcopied = k.count("b_tcopied", 2)
        k.b_trans = k.count("b_trans", 2)
        k.b_taken = k.count("b_taken", 2)
        k.b_ocopied = k.count("b_ocopied", 2)
        k.b_oturned = k.count("b_oturned", 2)
        k.b_max = k.count("b_max")
        k.b_inv = k.count("b_inv")
        k.c_static = k.count("c_static")
        k.c_scored = k.count("c_scored", 2)
        k.c_vcopied = k.count("c_vcopied", 2)
        k.c_exp = k.count("c_exp", 2)
        k.c_normed = k.count("c_normed", 2)
        k.c_tcopied = k.count("c_tcopied", 2)
        k.c_trans = k.count("c_trans", 2)
        k.c_taken = k.count("c_taken", 2)
        k.c_out = k.count("c_out", 2)
        k.c_max = k.count("c_max")
        k.c_inv = k.count("c_inv")
        k.consts_loaded = k.count("consts_loaded", unit=16)
        k.plain_loaded = k.count("plain_loaded", unit=16)
        k.split_loaded = k.count("split_loaded", unit=16)
        k.out_stored = k.count("out_stored", unit=16)
        k.a_last = k.count("a_last", unit=16)
        k.m_bias = k.count("m_bias", unit=16)
        k.a_ctx = [k.count(f"a_ctx{p}", unit=16) for p in range(2)]
        k.a_mask = [k.count(f"a_mask{p}", unit=16) for p in range(2)]
        k.t_raw = [k.count(f"t_raw{p}", unit=16) for p in range(2)]
        k.m_rows = [k.count(f"m_rows{p}", unit=16) for p in range(2)]
        k.g_shared = [k.count(f"g_shared{p}", unit=16) for p in range(4)]
        k.g_load = [k.count(f"g_load{p}", unit=16) for p in range(4)]
        k.b_ctx_t = [k.count(f"b_ctx_t{p}", unit=16) for p in range(4)]
        k.b_ctx = [k.count(f"b_ctx{p}", unit=16) for p in range(4)]
        k.t_rows = [k.count(f"t_rows{p}", unit=16) for p in range(4)]
        k.t_stored = [k.count(f"t_stored{p}", 1, unit=16) for p in range(2)]
        k.x_loaded = [k.count(f"x_loaded{g}", unit=16) for g in range(G)]

        start(k)
        stages = [stage_heads_attention, stage_recurrence, stage_first_mixture, stage_single_attention,
                  stage_causal_attention, stage_second_mixture]
        for s in STAGES:
            k.stage = stages[s].__name__
            k.first = s == STAGES[0]
            stages[s](k)

        with nc.Block() as block:
            @block.sync
            def _(sp):
                sp.dma_start(dram["out"].rearrange("(c p) t -> p c t", p=P), k.x_t[:, :, :]).then_inc(k.out_stored.sem, 16)
                sp.wait_ge(k.out_stored.sem, k.out_stored.at(1))


def columns(a):
    return np.ascontiguousarray(a.reshape(-1, P).T)


def lay_out(i):
    T_ = np.transpose
    a = {
        "x_t": i["x"].reshape(T, D).T, "consts": const_table(),
        "ctx_t": T_(i["ctx_1024"], (0, 2, 1)), "ctx_last_t": i["ctx_1024"][:, SK - 1, :].T, "ctx": i["ctx_1024"], "mask": i["mask_BxSxS2_ik1"],
        "L0_xattn_wq_t": i["L0_xattn_wq"].T, "L0_xattn_wk_t": i["L0_xattn_wk"].T, "L0_xattn_wv_t": i["L0_xattn_wv"].T,
        "L0_xattn_wout_t": i["L0_xattn_w_out"].T,
        "L0_attn_W1": i["L0_attn_W1"], "L0_attn_W2": i["L0_attn_W2"], "L0_ffn_Wg": i["L0_ffn_Wg"],
        "L1_xattn_wq": i["L1_xattn_wq"], "L1_xattn_wk_t": i["L1_xattn_wk"].T, "L1_xattn_wv": i["L1_xattn_wv"],
        "L1_attn_Wq_t": i["L1_attn_Wq"].T, "L1_attn_Wk_t": i["L1_attn_Wk"].T, "L1_attn_Wv_t": i["L1_attn_Wv"].T,
        "L1_ffn_gate_w_t": i["L1_ffn_gate_w"].T,
        "L1_ffn_gate_bias": np.broadcast_to(i["L1_ffn_gate_bias"][None, :], (P, E1)),
    }
    for n in ["L0_attn_b1", "L0_attn_b2", "L0_attn_init_h", "L1_xattn_bq", "L1_xattn_bk", "L1_xattn_bv", "L1_attn_bq", "L1_attn_bk", "L1_attn_bv"]:
        a[n] = columns(i[n])
    w1 = np.concatenate([i["L0_ffn_W1"], i["L0_ffn_Ws1"][None]]).reshape(E0 + 1, C, P, F0)
    w2 = np.concatenate([i["L0_ffn_W2"], i["L0_ffn_Ws2"][None]]).reshape(E0 + 1, 2, F0 // P // 2, P, D)
    w2 = T_(w2, (0, 1, 3, 2, 4)).reshape(E0 + 1, 2, P, F0)
    a["m0_w"] = np.concatenate([w1, w2], axis=1).reshape(-1, P, F0)
    a["m0_b1"] = columns(np.concatenate([i["L0_ffn_b1"], i["L0_ffn_bs1"][None]]))
    a["m0_b2"] = np.concatenate([i["L0_ffn_b2"], i["L0_ffn_bs2"][None]])
    up = [np.concatenate([i[f"L1_ffn_{n}"], i[f"L1_ffn_{m}"][None]]) for n, m in (("w1", "ws1"), ("w3", "ws3"))]
    up = [T_(w, (0, 2, 1)).reshape(E1 + 1, C, P, I1) for w in up]
    down = np.concatenate([i["L1_ffn_w2"], i["L1_ffn_ws2"][None]])
    down = T_(down, (0, 2, 1)).reshape(E1 + 1, 2, IH, D)
    down = np.concatenate([down, np.zeros((E1 + 1, 2, P - IH, D), down.dtype)], axis=2)
    a["m1_w"] = np.concatenate([T_(w, (0, 2, 1, 3)).reshape(E1 + 1, P, -1) for w in (*up, down)], axis=2)
    return {n: np.ascontiguousarray(v) for n, v in a.items()}


def kernel(**inputs):
    import concourse.bacc as bacc
    from concourse.bass_utils import run_bass_kernel_spmd

    arrays = lay_out({n: np.asarray(v) for n, v in inputs.items()})
    nc = bacc.Bacc("TRN2", target_bir_lowering=False, num_devices=1)
    dram = {n: nc.dram_tensor(f"in_{n}", a.shape, mybir.dt.from_np(a.dtype), kind="ExternalInput").ap() for n, a in arrays.items()}
    dram["out"] = nc.dram_tensor("out_0_dram", [D, T], F32, kind="ExternalOutput").ap()
    build(nc, dram)
    r = run_bass_kernel_spmd(nc, [{f"in_{n}": a for n, a in arrays.items()}], core_ids=[0])
    return np.ascontiguousarray(r.results[0]["out_0_dram"].T).reshape(B, S, D)
```
